# Optimizing a Trainium2 kernel written in Bass

```python
import numpy as np
import jax
import jax.numpy as jnp

def _softmax(x, axis=-1):
    return jax.nn.softmax(x, axis=axis)

def _gelu(x):
    return jax.nn.gelu(x, approximate=True)

def _silu(x):
    return jax.nn.silu(x)

def _sigmoid(x):
    return jax.nn.sigmoid(x)

def _layernorm(x, axis=-1, eps=1e-05):
    m = jnp.mean(x, axis=axis, keepdims=True)
    v = jnp.var(x, axis=axis, keepdims=True)
    return (x - m) / jnp.sqrt(v + eps)

def _scatter_add(tgt, idx, src, axis=0):
    return tgt.at[idx].add(src)

def _segment_sum(src, seg, n):
    return jax.ops.segment_sum(src, seg, n)
kernel_name = 'mk_gps_d1_gnn_r8_88787d'

def setup_inputs(seed: int=0):
    np.random.seed(seed)
    _w = jnp.asarray

    def _rec_inputs():
        import jax
        import jax.numpy as jnp
        _gk = jax.random.key(seed)
        x = -8.776e-05 + 1 * jax.random.normal(jax.random.fold_in(_gk, 1), (6250, 256), jnp.float32)
        _s = jax.random.randint(jax.random.fold_in(_gk, 2), (100000,), 0, 6250, jnp.int32)
        _d = jax.random.randint(jax.random.fold_in(_gk, 3), (100000,), 0, 6250, jnp.int32)
        _loop = jnp.arange(6250, dtype=jnp.int32)
        src = jnp.concatenate([_s, _d, _loop])
        dst = jnp.concatenate([_d, _s, _loop])
        _o = jnp.argsort(dst, stable=True)
        src = src[_o]
        dst = dst[_o]
        edge_type_8 = jax.random.randint(jax.random.fold_in(_gk, 12), (206250,), 0, 8, jnp.int32)
        return (x, src, dst, edge_type_8)
    x, src, dst, edge_type_8 = _rec_inputs()

    def _L0_gnn_setup():
        import jax, jax.numpy as jnp
        import numpy as np
        N_NODES = 2500
        N_EDGES = 80000
        D = 256
        N_RELS = 8
        N_BASES = 4
        LN_EPS = 1e-05
        key = jax.random.key(seed)
        ks = jax.random.split(key, 8)
        node_feats = jax.random.normal(ks[0], (N_NODES, D), dtype=jnp.float32)
        src = jax.random.randint(ks[1], (N_EDGES,), 0, N_NODES, dtype=jnp.int32)
        dst = jax.random.randint(ks[2], (N_EDGES,), 0, N_NODES, dtype=jnp.int32)
        edge_types = jax.random.randint(ks[3], (N_EDGES,), 0, N_RELS, dtype=jnp.int32)
        basis = jax.random.normal(ks[4], (N_BASES, D, D), dtype=jnp.float32) * (1.0 / np.sqrt(D))
        comp = jax.random.normal(ks[5], (N_RELS, N_BASES), dtype=jnp.float32) * (1.0 / np.sqrt(N_BASES))
        loop_w = jax.random.normal(ks[6], (D, D), dtype=jnp.float32) * (1.0 / np.sqrt(D))
        h_bias = jnp.zeros((D,), dtype=jnp.float32)
        ln_gamma = jnp.ones((D,), dtype=jnp.float32)
        ln_beta = jnp.zeros((D,), dtype=jnp.float32)
        return {'node_feats': node_feats, 'src': src, 'dst': dst, 'edge_types': edge_types, 'basis': basis, 'comp': comp, 'loop_w': loop_w, 'h_bias': h_bias, 'ln_gamma': ln_gamma, 'ln_beta': ln_beta}
    _L0_gnn_all = _L0_gnn_setup()
    _L0_gnn_in = {k: v for k, v in _L0_gnn_all.items() if k in ('basis', 'comp', 'loop_w', 'h_bias', 'ln_gamma', 'ln_beta')}
    del _L0_gnn_all

    def _L0_mix_setup():
        import jax, jax.numpy as jnp
        import numpy as np
        NHEAD = 8
        ATT_EPS = 1e-06
        LN_EPS = 1e-05

        def _layernorm(x, g, b):
            mu = jnp.mean(x, axis=-1, keepdims=True)
            var = jnp.mean(jnp.square(x - mu), axis=-1, keepdims=True)
            return (x - mu) * jax.lax.rsqrt(var + LN_EPS) * g + b
        key = jax.random.key(seed)
        ks = jax.random.split(key, 7)
        N, L, C = (4, 2048, 256)
        s = 1.0 / np.sqrt(C)
        return {'x': jax.random.normal(ks[0], (N, L, C), jnp.float32), 'Wq': jax.random.normal(ks[1], (C, C), jnp.float32) * s, 'Wk': jax.random.normal(ks[2], (C, C), jnp.float32) * s, 'Wv': jax.random.normal(ks[3], (C, C), jnp.float32) * s, 'Wm': jax.random.normal(ks[4], (C, C), jnp.float32) * s, 'W1': jax.random.normal(ks[5], (2 * C, 2 * C), jnp.float32) * (1.0 / np.sqrt(2 * C)), 'W2': jax.random.normal(ks[6], (2 * C, C), jnp.float32) * (1.0 / np.sqrt(2 * C)), 'g1': jnp.ones((C,), jnp.float32), 'b1': jnp.zeros((C,), jnp.float32), 'g2': jnp.ones((C,), jnp.float32), 'b2': jnp.zeros((C,), jnp.float32)}
    _L0_mix_all = _L0_mix_setup()
    _L0_mix_in = {k: v for k, v in _L0_mix_all.items() if k in ('Wq', 'Wk', 'Wv', 'Wm', 'W1', 'W2', 'g1', 'b1', 'g2', 'b2')}
    del _L0_mix_all

    def _L0_ffn_setup():
        import jax, jax.numpy as jnp
        import numpy as np
        TOP_K = 2
        LN_EPS = 1e-05
        key = jax.random.key(seed)
        ks = jax.random.split(key, 8)
        B, S, D, E, H = (16, 1024, 256, 8, 1024)
        x = jax.random.normal(ks[0], (B, S, D), dtype=jnp.float32)
        Wr = jax.random.normal(ks[1], (D, E), dtype=jnp.float32) * 0.1
        br = jnp.zeros((E,), dtype=jnp.float32)
        ln_g = jnp.ones((E, D), dtype=jnp.float32)
        ln_b = jnp.zeros((E, D), dtype=jnp.float32)
        W1 = jax.random.normal(ks[2], (E, D, H), dtype=jnp.float32) * (1.0 / np.sqrt(D))
        b1 = jnp.zeros((E, H), dtype=jnp.float32)
        W2 = jax.random.normal(ks[3], (E, H, D), dtype=jnp.float32) * (1.0 / np.sqrt(H))
        b2 = jnp.zeros((E, D), dtype=jnp.float32)
        return {'x': x, 'Wr': Wr, 'br': br, 'ln_g': ln_g, 'ln_b': ln_b, 'W1': W1, 'b1': b1, 'W2': W2, 'b2': b2}
    _L0_ffn_all = _L0_ffn_setup()
    _L0_ffn_in = {k: v for k, v in _L0_ffn_all.items() if k in ('Wr', 'br', 'ln_g', 'ln_b', 'W1', 'b1', 'W2', 'b2')}
    del _L0_ffn_all
    return {'x': x, 'src': src, 'dst': dst, 'edge_type_8': edge_type_8, 'L0_gnn_basis': _L0_gnn_in['basis'], 'L0_gnn_comp': _L0_gnn_in['comp'], 'L0_gnn_loop_w': _L0_gnn_in['loop_w'], 'L0_gnn_h_bias': _L0_gnn_in['h_bias'], 'L0_gnn_ln_gamma': _L0_gnn_in['ln_gamma'], 'L0_gnn_ln_beta': _L0_gnn_in['ln_beta'], 'L0_mix_Wq': _L0_mix_in['Wq'], 'L0_mix_Wk': _L0_mix_in['Wk'], 'L0_mix_Wv': _L0_mix_in['Wv'], 'L0_mix_Wm': _L0_mix_in['Wm'], 'L0_mix_W1': _L0_mix_in['W1'], 'L0_mix_W2': _L0_mix_in['W2'], 'L0_mix_g1': _L0_mix_in['g1'], 'L0_mix_b1': _L0_mix_in['b1'], 'L0_mix_g2': _L0_mix_in['g2'], 'L0_mix_b2': _L0_mix_in['b2'], 'L0_ffn_Wr': _L0_ffn_in['Wr'], 'L0_ffn_br': _L0_ffn_in['br'], 'L0_ffn_ln_g': _L0_ffn_in['ln_g'], 'L0_ffn_ln_b': _L0_ffn_in['ln_b'], 'L0_ffn_W1': _L0_ffn_in['W1'], 'L0_ffn_b1': _L0_ffn_in['b1'], 'L0_ffn_W2': _L0_ffn_in['W2'], 'L0_ffn_b2': _L0_ffn_in['b2']}

def reference(x, src, dst, edge_type_8, L0_gnn_basis, L0_gnn_comp, L0_gnn_loop_w, L0_gnn_h_bias, L0_gnn_ln_gamma, L0_gnn_ln_beta, L0_mix_Wq, L0_mix_Wk, L0_mix_Wv, L0_mix_Wm, L0_mix_W1, L0_mix_W2, L0_mix_g1, L0_mix_b1, L0_mix_g2, L0_mix_b2, L0_ffn_Wr, L0_ffn_br, L0_ffn_ln_g, L0_ffn_ln_b, L0_ffn_W1, L0_ffn_b1, L0_ffn_W2, L0_ffn_b2):
    import jax
    import jax.numpy as jnp

    def _L0_gnn_ref(node_feats, src, dst, edge_types, basis, comp, loop_w, h_bias, ln_gamma, ln_beta):
        import jax, jax.numpy as jnp
        import numpy as np
        N_NODES = 2500
        N_EDGES = 80000
        D = 256
        N_RELS = 8
        N_BASES = 4
        LN_EPS = 1e-05
        W = jnp.einsum('rb,bio->rio', comp, basis)
        h_all = jnp.einsum('ni,rio->nro', node_feats, W)
        msgs = h_all[src, edge_types]
        agg = jax.ops.segment_sum(msgs, dst, num_segments=node_feats.shape[0])
        rgcn_out = agg + node_feats @ loop_w + h_bias
        h = jax.nn.gelu(rgcn_out + node_feats, approximate=False)
        mu = jnp.mean(h, axis=-1, keepdims=True)
        var = jnp.mean(jnp.square(h - mu), axis=-1, keepdims=True)
        return (h - mu) * jax.lax.rsqrt(var + LN_EPS) * ln_gamma + ln_beta

    def _L0_mix_ref(x, Wq, Wk, Wv, Wm, W1, W2, g1, b1, g2, b2):
        import jax, jax.numpy as jnp
        import numpy as np
        NHEAD = 8
        ATT_EPS = 1e-06
        LN_EPS = 1e-05

        def _layernorm(x, g, b):
            mu = jnp.mean(x, axis=-1, keepdims=True)
            var = jnp.mean(jnp.square(x - mu), axis=-1, keepdims=True)
            return (x - mu) * jax.lax.rsqrt(var + LN_EPS) * g + b
        N, L, C = x.shape
        H = NHEAD
        D = C // H
        q = (x @ Wq).reshape(N, L, H, D)
        k = (x @ Wk).reshape(N, L, H, D)
        v = (x @ Wv).reshape(N, L, H, D)
        Q = jax.nn.elu(q) + 1.0
        K = jax.nn.elu(k) + 1.0
        v = v / L
        KV = jnp.einsum('nshd,nshv->nhdv', K, v)
        Z = 1.0 / (jnp.einsum('nlhd,nhd->nlh', Q, K.sum(axis=1)) + ATT_EPS)
        msg = jnp.einsum('nlhd,nhdv,nlh->nlhv', Q, KV, Z) * L
        msg = msg.reshape(N, L, C) @ Wm
        msg = _layernorm(msg, g1, b1)
        h = jnp.concatenate([x, msg], axis=-1) @ W1
        h = jax.nn.relu(h) @ W2
        msg = _layernorm(h, g2, b2)
        return x + msg

    def _L0_ffn_ref(x, Wr, br, ln_g, ln_b, W1, b1, W2, b2):
        import jax, jax.numpy as jnp
        import numpy as np
        TOP_K = 2
        LN_EPS = 1e-05
        B, S, D = x.shape
        N = B * S
        xt = x.reshape(N, D)
        logits = xt @ Wr + br
        probs = jax.nn.softmax(logits, axis=-1)
        top_p, top_idx = jax.lax.top_k(probs, TOP_K)
        weights = top_p / top_p.sum(axis=-1, keepdims=True)
        mu = xt.mean(axis=-1, keepdims=True)
        var = ((xt - mu) ** 2).mean(axis=-1, keepdims=True)
        xn = (xt - mu) * jax.lax.rsqrt(var + LN_EPS)
        xe = xn[None, :, :] * ln_g[:, None, :] + ln_b[:, None, :]
        h = jax.nn.gelu(jnp.einsum('end,edh->enh', xe, W1) + b1[:, None, :], approximate=False)
        y = jnp.einsum('enh,ehd->end', h, W2) + b2[:, None, :]
        y_tok = jnp.transpose(y, (1, 0, 2))
        sel = jnp.take_along_axis(y_tok, top_idx[:, :, None], axis=1)
        out = (weights[:, :, None] * sel).sum(axis=1)
        return out.reshape(B, S, D)
    xn = _layernorm(x, axis=-1)
    x = x + _L0_gnn_ref(xn, src, dst, edge_type_8, L0_gnn_basis, L0_gnn_comp, L0_gnn_loop_w, L0_gnn_h_bias, L0_gnn_ln_gamma, L0_gnn_ln_beta) + _L0_mix_ref(xn[None], L0_mix_Wq, L0_mix_Wk, L0_mix_Wv, L0_mix_Wm, L0_mix_W1, L0_mix_W2, L0_mix_g1, L0_mix_b1, L0_mix_g2, L0_mix_b2)[0]
    x = x + _L0_ffn_ref(_layernorm(x, axis=-1)[None], L0_ffn_Wr, L0_ffn_br, L0_ffn_ln_g, L0_ffn_ln_b, L0_ffn_W1, L0_ffn_b1, L0_ffn_W2, L0_ffn_b2)[0]
    return x

_drawn_inputs = setup_inputs


def setup_inputs(seed=0):
    import zlib

    import numpy as np

    out = dict(_drawn_inputs(seed))
    spreads = {'L0_gnn_h_bias': (0.0, 0.463),
     'L0_gnn_ln_gamma': (1.0, 0.2),
     'L0_gnn_ln_beta': (0.0, 0.1),
     'L0_mix_g1': (1.0, 0.2),
     'L0_mix_b1': (0.0, 0.1),
     'L0_mix_g2': (1.0, 0.2),
     'L0_mix_b2': (0.0, 0.1),
     'L0_ffn_br': (0.0, 0.1),
     'L0_ffn_ln_g': (1.0, 0.2),
     'L0_ffn_ln_b': (0.0, 0.396),
     'L0_ffn_b1': (0.0, 0.385),
     'L0_ffn_b2': (0.0, 0.268)}
    factors = {}
    for name, (base, spread) in spreads.items():
        noise = np.random.default_rng([zlib.crc32(name.encode()), seed]).standard_normal(out[name].shape)
        drawn = base * np.exp(spread * noise) if base else spread * noise
        out[name] = jnp.asarray(drawn.astype(out[name].dtype))
    for name, factor in factors.items():
        out[name] = (out[name] * factor).astype(out[name].dtype)
    return out
```

```python
from contextlib import ExitStack

import concourse.bass as bass
from concourse import mybir

F32 = mybir.dt.float32
I32 = mybir.dt.int32
ALU = mybir.AluOpType
ACT = mybir.ActivationFunctionType
AX = mybir.AxisListType

P = 128
ds = bass.ds


class Chain:

    def __init__(self, eng, sem):
        self.eng, self.sem, self.n = eng, sem, 0

    def at(self, value):
        self.n = value

    def link(self, ins):
        ins.then_inc(self.sem, 1)
        self.n = self.n + 1
        self.eng.wait_ge(self.sem, self.n)


def rsqrt_steps(dve, chain, var, eps, x, y, t):
    chain.link(dve.tensor_scalar(x, var, eps, None, ALU.add))
    chain.link(dve.tensor_scalar(t.bitcast(I32), x.bitcast(I32), 1, None, ALU.logical_shift_right))
    chain.link(dve.tensor_scalar(y.bitcast(I32), t.bitcast(I32), -1.0, float(0x5F3759DF), ALU.mult, ALU.add))
    for _ in range(4):
        chain.link(dve.tensor_tensor(t, y, y, ALU.mult))
        chain.link(dve.tensor_tensor(t, t, x, ALU.mult))
        chain.link(dve.tensor_scalar(t, t, -0.5, 1.5, ALU.mult, ALU.add))
        chain.link(dve.tensor_tensor(y, y, t, ALU.mult))



def after(eng, s, n):
    if not (isinstance(n, int) and n <= 0):
        eng.wait_ge(s, n)


def row_of(t, b):
    return t[:, ds(b, 1), :].rearrange("p o d -> p (o d)")


def bass_gps_layer(nc, x, src, dst, etype, basis, comp, loop_w, h_bias, gamma, beta,
                   Wq, Wk, Wv, Wm, W1m, W2m, g1, b1m, g2, b2m,
                   Wr, br, ln_g, ln_b, W1, b1, W2, b2, out):
    N, D = x.shape
    E = src.shape[0]
    NB = -(-N // P)
    NP = NB * P
    LAST = N - (NB - 1) * P
    KD = D // P
    NREL, NBASE = comp.shape
    HEADS = 8
    HD = D // HEADS
    NEX, HID = b1.shape
    KH = HID // P
    LN_EPS, ATT_EPS = 1e-5, 1e-6
    GT = 4
    GE = GT * P
    NG = -(-E // GE)
    GC = -(-NG // P)
    NGP = GC * P
    FULLC = (E // GE) // P
    LASTC_FULL = E // GE - FULLC * P
    LASTC_REST = E - (E // GE) * GE
    GPB = NG // NB
    SLOTS = 4
    assert GPB % SLOTS == 0
    REST = NG - NB * GPB
    MT = 256
    NT = (2 * N + NEX * MT) // MT + 1
    NT_LEAST = -(-2 * N // MT)
    MH = MT // P
    BZ = 6

    h_table = nc.dram_tensor("h_table", (NP * NREL, D), F32).ap()
    xn_rows = nc.dram_tensor("xn_rows", (NB, P, D), F32).ap()
    xn_cols = nc.dram_tensor("xn_cols", (NB, P, D), F32).ap()
    bucket = nc.dram_tensor("bucket", (NT * MT, D), F32).ap()
    answers = nc.dram_tensor("answers", (NT * MT, D), F32).ap()

    with ExitStack() as ctx:
        def sb(name, shape, dt=F32):
            return ctx.enter_context(nc.sbuf_tensor(name, shape, dt))

        def sem(name):
            return ctx.enter_context(nc.semaphore(name))

        agg = sb("agg", [P, NB, D])
        xt_all = sb("xt_all", [P, NB, D])
        big = sb("big", [P, 10 * 1024])
        ring = sb("ring", [P, SLOTS, GT, D])
        w_rel = big[:, 0:4096].rearrange("p (k n) -> p k n", k=KD)
        wkv = big[:, 4096:5120].rearrange("p (k n) -> p k n", k=KD)
        wq = big[:, 5120:5632].rearrange("p (k n) -> p k n", k=KD)
        wm = big[:, 5632:6144].rearrange("p (k n) -> p k n", k=KD)
        w1m = big[:, 6144:8192].rearrange("p (k n) -> p k n", k=2 * KD)
        w2m = big[:, 8192:9216].rearrange("p (k n) -> p k n", k=2 * KD)
        wloop = big[:, 9216:9728].rearrange("p (k n) -> p k n", k=KD)
        compb = big[:, 9728:9728 + NREL * NBASE].rearrange("p (r b) -> p r b", r=NREL)
        we1 = [big[:, 4096 * i:4096 * i + 2048].rearrange("p (k n) -> p k n", k=KD) for i in range(2)]
        we2 = [big[:, 4096 * i + 2048:4096 * i + 4096].rearrange("p (k n) -> p k n", k=KH) for i in range(2)]
        EP = KH + 2 * KD
        eparm = [big[:, 8192 + 1024 * i:8192 + 1024 * i + EP] for i in range(2)]
        eb2 = [big[:, 8192 + 1024 * i + 256:8192 + 1024 * i + 256 + D] for i in range(2)]
        stage = ring[:, :, :, :].rearrange("p s t d -> p (s t d)").rearrange("p (u n) -> p u n", u=2)
        basis_sb = stage[:, 0, 0:KD * NBASE * D].rearrange("p (k b d) -> p k b d", k=KD, b=NBASE)
        flat = xt_all[:, :, :].rearrange("p b d -> p (b d)")
        CW = GC * GE
        src_i = flat[:, 0:CW].bitcast(I32).rearrange("p (c e) -> p c e", c=GC)
        et_i = flat[:, CW:2 * CW].bitcast(I32).rearrange("p (c e) -> p c e", c=GC)
        dst_i = flat[:, 2 * CW:3 * CW].bitcast(I32).rearrange("p (c e) -> p c e", c=GC)
        row_f = flat[:, 3 * CW:4 * CW].rearrange("p (c e) -> p c e", c=GC)
        dst_f = flat[:, 4 * CW:5 * CW].rearrange("p (c e) -> p c e", c=GC)
        low_f = flat[:, 5 * CW:5 * CW + GE]
        dcol = sb("dcol", [P, NG, GT])
        icol = sb("icol", [P, NG, GT], I32)
        group_tab = sb("group_tab", [1, 3, NGP], I32)
        tab_f = flat[0:1, 5 * CW + GE:5 * CW + GE + 3 * NGP].rearrange("o (t g) -> o t g", t=3)
        span = sb("span", [P, 8, GC])
        span_i = sb("span_i", [P, 2, GC], I32)

        ident = sb("ident", [P, P])
        upper = sb("upper", [P, P])
        ones = sb("ones", [P, P])
        zeros = sb("zeros", [P, D])
        heads = sb("heads", [P, P])
        iota_f = sb("iota_f", [P, P])
        valid = sb("valid", [P, NB])
        rows = sb("rows", [P, 6, D])
        hbias_b, gamma_b, beta_b, g2_b, b2m_b = (rows[:, i, :] for i in range(5))
        wr_sb = rows[:, 5, 0:KD * NEX].rearrange("p (k e) -> p k e", k=KD)
        br_b = rows[:, 5, 64:64 + NEX]
        g1c = rows[:, 5, 80:80 + KD]
        b1c = rows[:, 5, 84:84 + KD]
        eps_c = rows[:, 5, 88:89]
        stats = sb("stats", [P, NB, 6])
        mv = sb("mv", [P, NB, 2])
        rstd = sb("rstd", [P, 3, NB])
        rs1 = sb("rs1", [P, 8])
        idx_now = sb("idx_now", [P, 2, SLOTS, GT], I32)
        onehot = sb("onehot", [P, 2, GT, P])
        onehot_x = sb("onehot_x", [P, GT, P])
        drel_x = sb("drel_x", [P, GT])
        xnb = sb("xnb", [P, 2, D])
        xTb = sb("xTb", [P, 2, KD, P])
        kmin = sb("kmin", [P, D])
        kexp = sb("kexp", [P, D])
        kphi = sb("kphi", [P, KD, P])
        vb = sb("vb", [P, KD, P + 2])
        kvd = sb("kvd", [P, KD, P])
        ksd = sb("ksd", [P, KD, P])
        msgT = sb("msgT", [P, KD, P])
        m1 = xnb[:, 1, :]
        m1T = xTb[:, 1, :, :]
        h1T = sb("h1T", [P, 2 * KD, P])
        h2n = sb("h2n", [P, D])
        x_rows = sb("x_rows", [P, D])
        den = sb("den", [P, D])
        mst = sb("mst", [P, 8])
        block_off = sb("block_off", [P, NB])

        bank = [ctx.enter_context(nc.psum_tensor(f"bank{i}", [P, 512], F32)) for i in range(8)]

        block = ctx.enter_context(nc.Block())

        x_in = [sem(f"x_in{i}") for i in range(7)]
        edges_in = sem("edges_in")
        weights_in = sem("weights_in")
        small_in = sem("small_in")
        pads_set = sem("pads_set")
        consts_set = sem("consts_set")
        rel_ready = sem("rel_ready")
        dve_own = sem("dve_own")
        edge_rows_ready = sem("edge_rows_ready")
        edge_cols_up = sem("edge_cols_up")
        edge_cols_down = sem("edge_cols_down")
        tables_ready = sem("tables_ready")
        xn_ready = sem("xn_ready")
        xn_free = sem("xn_free")
        xT_up = sem("xT_up")
        xT_ready = sem("xT_ready")
        xT_stored = [sem(f"xT_stored{i}") for i in range(2)]
        xn_stored = [sem(f"xn_stored{i}") for i in range(2)]
        loop_up = sem("loop_up")
        table_up = sem("table_up")
        table_down_a = sem("table_down_a")
        table_down_d = sem("table_down_d")
        stage_stored = [sem(f"stage_stored{i}") for i in range(2)]
        kv_up = sem("kv_up")
        kmin_ready = sem("kmin_ready")
        kexp_ready = sem("kexp_ready")
        kphi_ready = sem("kphi_ready")
        v_ready = sem("v_ready")
        vones_ready = sem("vones_ready")
        agg_bias = sem("agg_bias")
        agg_init = sem("agg_init")
        kv_used = sem("kv_used")
        kvd_ready = sem("kvd_ready")
        zero_stored = sem("zero_stored")

        idx_ready = sem("idx_ready")
        slot_seen = sem("slot_seen")
        waits_passed = sem("waits_passed")
        rows_in = [sem(f"rows_in{i}") for i in range(SLOTS)]
        onehot_ready = sem("onehot_ready")
        sum_up = sem("sum_up")
        sum_down = sem("sum_down")
        extra_onehot = sem("extra_onehot")
        extra_up = sem("extra_up")
        extra_down = sem("extra_down")
        extra_rel = sem("extra_rel")
        mix_cols_in = sem("mix_cols_in")
        mix_rows_in = sem("mix_rows_in")
        mix_own = sem("mix_own")
        q_up = sem("q_up")
        qmin_ready = sem("qmin_ready")
        qexp_ready = sem("qexp_ready")
        qphi_ready = sem("qphi_ready")
        nd_up = sem("nd_up")
        den_ready = sem("den_ready")
        msg_ready = sem("msg_ready")
        m_up = sem("m_up")
        m_stats = sem("m_stats")
        m1_ready = sem("m1_ready")
        m1T_up = sem("m1T_up")
        m1T_ready = sem("m1T_ready")
        f_up = sem("f_up")
        h1_ready = sem("h1_ready")
        h2_up = sem("h2_up")
        h2_stats = sem("h2_stats")
        h2n_ready = sem("h2n_ready")
        mix_ready = sem("mix_ready")

        def row_dram(t, b):
            return t[ds(b, 1), :, :].rearrange("o p d -> (o p) d")

        def sp_program(sp):
            for i in range(6):
                sp.dma_start(agg[:, 8 * i:8 * i + 8, :],
                             x[1024 * i:1024 * i + 1024, :].rearrange("(b p) d -> p b d", p=P)).then_inc(x_in[i], 16)
            sp.wait_ge(pads_set, 4)
            sp.dma_start(agg[0:LAST, NB - 1, :], x[(NB - 1) * P:N, :]).then_inc(x_in[6], 16)
            for k in range(KD):
                sp.dma_start(basis_sb[:, k, :, :], basis[:, k * P:(k + 1) * P, :].rearrange("b p o -> p b o")).then_inc(weights_in, 16)
            sp.dma_start(compb, comp.rearrange("r b -> (r b)").partition_broadcast(P)
                         .rearrange("p (r b) -> p r b", r=NREL)).then_inc(weights_in, 16)
            sp.dma_start(wloop, loop_w.rearrange("(k p) o -> p k o", p=P)).then_inc(weights_in, 16)
            sp.dma_start(wkv[:, :, 0:D], Wk.rearrange("(k p) o -> p k o", p=P)).then_inc(weights_in, 16)
            sp.dma_start(wkv[:, :, D:2 * D], Wv.rearrange("(k p) o -> p k o", p=P)).then_inc(weights_in, 16)
            sp.dma_start(wq, Wq.rearrange("(k p) o -> p k o", p=P)).then_inc(weights_in, 16)
            sp.dma_start(wm, Wm.rearrange("(k p) o -> p k o", p=P)).then_inc(weights_in, 16)
            sp.dma_start(w1m, W1m.rearrange("(k p) o -> p k o", p=P)).then_inc(weights_in, 16)
            sp.dma_start(w2m, W2m.rearrange("(k p) o -> p k o", p=P)).then_inc(weights_in, 16)
            for row, vec in ((hbias_b, h_bias), (gamma_b, gamma), (beta_b, beta), (g2_b, g2), (b2m_b, b2m), (br_b, br)):
                sp.dma_start(row, vec.partition_broadcast(P)).then_inc(small_in, 16)
            sp.dma_start(wr_sb, Wr.rearrange("(k p) e -> p k e", p=P)).then_inc(small_in, 16)
            sp.dma_start(g1c, g1.rearrange("(k p) -> p k", p=P), allow_slow_non_contiguous=True).then_inc(small_in, 16)
            sp.dma_start(b1c, b1m.rearrange("(k p) -> p k", p=P), allow_slow_non_contiguous=True).then_inc(small_in, 16)
            def store_block(b, u, i):
                sp.wait_ge(xn_ready, b + 1)
                sp.dma_start(row_dram(xn_rows, b), xnb[:, u, :]).then_inc(xn_stored[u], 16)
                sp.wait_ge(xT_ready, b + 1)
                sp.dma_start(row_dram(xn_cols, b), xTb[:, u, :, :].rearrange("p k n -> p (k n)")).then_inc(xT_stored[u], 16)
                sp.wait_ge(table_down_a, 2 * b + 2)
                sp.wait_ge(table_down_d, 2 * b + 2)
                sp.dma_start(h_table[ds(b * (P * NREL), P * NREL), :].rearrange("(p r) d -> p (r d)", r=NREL),
                             stage[:, u, :]).then_inc(stage_stored[u], 16)
            store_block(0, 0, 0)
            store_block(1, 1, 0)
            with sp.Fori(1, NB // 2) as i:
                store_block(2 * i, 0, i)
                store_block(2 * i + 1, 1, i)
            store_block(NB - 1, 0, NB // 2)
            sp_mix(sp)
            sp_tail(sp)

        def pool_program(pool):
            pool.memset(agg[:, NB - 1, :], 0.0).then_inc(pads_set, 1)
            for t in (src_i, et_i):
                pool.memset(t[:, GC - 1, :], 0).then_inc(pads_set, 1)
            pool.memset(dst_i[:, GC - 1, :], -1).then_inc(pads_set, 1)
            pool.memset(ident[:, :], 0.0).then_inc(consts_set, 1)
            pool.memset(ones[:, :], 1.0).then_inc(consts_set, 1)
            pool.memset(zeros[:, :], 0.0).then_inc(consts_set, 1)
            pool.memset(eps_c, ATT_EPS).then_inc(consts_set, 1)
            pool.iota(iota_f[:, :], [[1, P]], base=0, channel_multiplier=0,
                      allow_small_or_imprecise_dtypes=True).then_inc(consts_set, 1)
            pool.iota(block_off[:, :], [[P, NB]], base=0, channel_multiplier=0,
                      allow_small_or_imprecise_dtypes=True).then_inc(consts_set, 1)
            pool.wait_ge(consts_set, 6)
            pool.affine_select(out=ident[:, :], in_=ident[:, :], pattern=[[-1, P]], compare_op=ALU.not_equal,
                               fill=1.0, base=0, channel_multiplier=1).then_inc(consts_set, 1)
            pool.affine_select(out=upper[:, :], in_=ones[:, :], pattern=[[1, P]], compare_op=ALU.is_gt,
                               fill=0.0, base=0, channel_multiplier=-1).then_inc(consts_set, 1)
            pool.affine_select(out=heads[:, :], in_=ones[:, :], pattern=[[-HD, P // HD], [0, HD]], compare_op=ALU.is_ge,
                               fill=0.0, base=0, channel_multiplier=1).then_inc(consts_set, 1)
            pool.affine_select(out=valid[:, :], in_=ones[:, 0:NB], pattern=[[-P, NB]], compare_op=ALU.is_ge,
                               fill=0.0, base=N - 1, channel_multiplier=-1).then_inc(consts_set, 1)
            pool.wait_ge(consts_set, 10)
            pool.affine_select(out=heads[:, :], in_=heads[:, :], pattern=[[HD, P // HD], [0, HD]], compare_op=ALU.is_ge,
                               fill=0.0, base=HD - 1, channel_multiplier=-1).then_inc(consts_set, 1)
            for t, a in ((src_i, src), (et_i, etype), (dst_i, dst)):
                full = FULLC * P * GE
                pool.dma_start(t[:, 0:FULLC, :], a[0:full].rearrange("(c p e) -> p c e", p=P, e=GE)).then_inc(edges_in, 16)
                pool.wait_ge(pads_set, 4)
                more = full + LASTC_FULL * GE
                pool.dma_start(t[0:LASTC_FULL, GC - 1, :], a[full:more].rearrange("(p e) -> p e", e=GE)).then_inc(edges_in, 16)
                pool.dma_start(t[LASTC_FULL:LASTC_FULL + 1, GC - 1, 0:LASTC_REST],
                               a[more:E].rearrange("(p e) -> p e", p=1)).then_inc(edges_in, 16)
            pool.wait_ge(consts_set, 11)
            with pool.Fori(0, NT * MT // P // BZ) as i:
                pool.dma_start(bucket[ds(i * P * BZ, P * BZ), :].rearrange("(u p) d -> p u d", p=P),
                               zeros[:, :].unsqueeze(1).to_broadcast([P, BZ, D])).then_inc(zero_stored, 16)
            gather_rows(pool)
            pool_tail(pool)

        GTOT = NG

        def gather_rows(pool):
            pool.wait_ge(stage_stored[0], 16 * ((NB + 1) // 2))
            pool.wait_ge(stage_stored[1], 16 * (NB // 2))
            pool.wait_ge(tables_ready, 1)

            def turn(g0, w, half, k):
                pool.tensor_copy(idx_now[:, half, 0:k, :], icol[:, ds(g0, k), :]).then_inc(idx_ready, 1)
                pool.wait_ge(idx_ready, w + 1)
                pool.sem_inc(slot_seen, 1)
                for s in range(k):
                    if not (isinstance(g0, int) and g0 < SLOTS):
                        pool.wait_ge(sum_up, g0 + s - SLOTS + 1)
                        pool.sem_inc(slot_seen, 1)
                    for q in range(GT):
                        pool.indirect_dma_start(
                            out=ring[:, s, q, :], out_offset=None, in_=h_table,
                            in_offset=bass.IndirectOffsetOnAxis(ap=idx_now[:, half, s, q:q + 1], axis=0),
                        ).then_inc(rows_in[s], 16)

            turns = NG // SLOTS
            turn(0, 0, 0, SLOTS)
            turn(SLOTS, 1, 1, SLOTS)
            with pool.Fori(1, turns // 2) as i:
                turn(i * (2 * SLOTS), 2 * i, 0, SLOTS)
                turn(i * (2 * SLOTS) + SLOTS, 2 * i + 1, 1, SLOTS)
            assert turns % 2 == 0
            turn(turns * SLOTS, turns, 0, NG % SLOTS)

        def sp_mix(sp):
            sp.wait_ge(table_up, 4 * NB)
            for u in range(2):
                n = 16 * ((NB + 1 - u) // 2)
                sp.wait_ge(xT_stored[u], n)
                sp.wait_ge(xn_stored[u], n)
            sp.wait_ge(agg_init, NB)

            def body(b):
                after(sp, f_up, b)
                sp.dma_start(xTb[:, 0, :, :].rearrange("p k n -> p (k n)"), row_dram(xn_cols, b)).then_inc(mix_cols_in, 16)
                after(sp, mix_ready, b)
                sp.dma_start(xnb[:, 0, :], row_dram(xn_rows, b)).then_inc(mix_rows_in, 16)
                n = LAST if isinstance(b, int) and b == NB - 1 else P
                sp.dma_start(x_rows[0:n, :], x[ds(b * P, n), :]).then_inc(mix_rows_in, 16)
            body(0)
            with sp.Fori(1, NB - 1) as b:
                body(b)
            body(NB - 1)

        H_BANKS, T_BANK, KV_BANK, A_BANKS = (0, 1, 2, 3), 4, 5, (6, 7)
        TAB_BANKS = (5, 6)
        QM_BANK, ND_BANK, F_BANK, TG_BANK, S_BANKS, X_BANK = 0, 1, 2, 3, (4, 5), 6
        psT = bank[T_BANK][:, 0:D]
        psL = bank[T_BANK][:, D:2 * D]

        def pe_tables(pe):
            pe.wait_ge(consts_set, 11)
            pe.wait_ge(edge_rows_ready, 1)
            n = 0
            for c in range(GC):
                for a in (dst_f, row_f):
                    if n >= 4:
                        pe.wait_ge(edge_cols_down, n - 3)
                    for q in range(GT):
                        m = pe.transpose(bank[H_BANKS[n % 4]][:, q * P:(q + 1) * P], a[:, c, q * P:(q + 1) * P],
                                         ident[:, :])
                    m.then_inc(edge_cols_up, 1)
                    n += 1
            for j in range(2):
                for c in range(GC):
                    m = pe.matmul(bank[TAB_BANKS[j]][0:1, c * P:(c + 1) * P], span[:, 4 + j, c:c + 1], ident[:, :],
                                  start=True, stop=True)
            m.then_inc(edge_cols_up, 1)

        NTAB = 2 * GC + 1

        def pe_block(pe, b, u, i):
            pe.wait_ge(xn_ready, b + 1)
            after(pe, agg_init, b)
            for k in range(KD):
                m = pe.transpose(psT[:, k * P:(k + 1) * P], xnb[:, u, k * P:(k + 1) * P], ident[:, :])
            m.then_inc(xT_up, 1)
            pe.wait_ge(xT_ready, b + 1)
            after(pe, kphi_ready, b)
            after(pe, v_ready, b)
            for k in range(KD):
                m = pe.matmul(bank[KV_BANK][:, :], xTb[:, u, k, :], wkv[:, k, :], start=k == 0, stop=k == KD - 1)
            m.then_inc(kv_up, 1)
            for k in range(KD):
                m = pe.matmul(psL, xTb[:, u, k, :], wloop[:, k, :], start=k == 0, stop=k == KD - 1)
            m.then_inc(loop_up, 1)
            for j in range(4):
                if j % 2 == 0:
                    after(pe, table_down_a, 2 * (b - 1) + j // 2 + 1)
                else:
                    after(pe, table_down_d, 2 * (b - 1) + j // 2 + 1)
                for k in range(KD):
                    m = pe.matmul(bank[H_BANKS[j]][:, :], xTb[:, u, k, :], w_rel[:, k, 512 * j:512 * j + 512],
                                  start=k == 0, stop=k == KD - 1)
                m.then_inc(table_up, 1)
            pe.wait_ge(kphi_ready, b + 1)
            pe.wait_ge(v_ready, b + 1)
            pe.wait_ge(vones_ready, b + 1)
            for h in range(KD):
                m = pe.matmul(bank[A_BANKS[h]][:, 0:P + 2], kphi[:, h, :], vb[:, h, :], start=False, stop=False,
                              skip_group_check=True)
            m.then_inc(kv_used, 1)

        def pe_extra(pe, g, s):
            n = pe.value_load(group_tab[0:1, 1, ds(g, 1)], min_val=1, max_val=NB)
            with pe.If(n > 1):
                before = pe.value_load(group_tab[0:1, 2, ds(g, 1)], min_val=0, max_val=NGP * NB)
                with pe.Fori(1, n) as k:
                    pe.wait_ge(extra_onehot, before + k)
                    pe.wait_ge(extra_down, before + k)
                    for q in range(GT):
                        m = pe.matmul(bank[X_BANK][:, 0:D], onehot_x[:, q, :], ring[:, s, q, :],
                                      start=q == 0, stop=q == GT - 1)
                    m.then_inc(extra_up, 1)

        def pe_group(pe, g, j, use):
            s, u = j % SLOTS, j % 2
            pe.wait_ge(rows_in[s], 16 * GT * (use + 1))
            pe_extra(pe, g, s)
            pe.wait_ge(onehot_ready, g + 1)
            after(pe, sum_down, g - 1)
            for q in range(GT):
                m = pe.matmul(bank[S_BANKS[u]][:, 0:D], onehot[:, u, q, :], ring[:, s, q, :],
                              start=q == 0, stop=q == GT - 1)
            m.then_inc(sum_up, 1)

        def pe_mix(pe):
            psQ, psM = bank[QM_BANK][:, 0:D], bank[QM_BANK][:, D:2 * D]
            psT2, psG = bank[TG_BANK][:, 0:D], bank[TG_BANK][:, D:2 * D]
            xT = xTb[:, 0, :, :]
            pe.wait_ge(table_down_a, 2 * NB)
            pe.wait_ge(table_down_d, 2 * NB)
            pe.wait_ge(kvd_ready, 2 * KD)

            def body(b):
                def group(j):
                    pe_group(pe, b * GPB + j, j, b * (GPB // SLOTS) + j // SLOTS)
                pe.wait_ge(mix_cols_in, 16 * (b + 1))
                after(pe, m1_ready, b)
                for o in range(KD):
                    for k in range(KD):
                        m = pe.matmul(psQ[:, o * P:(o + 1) * P], wq[:, k, o * P:(o + 1) * P], xT[:, k, :],
                                      start=k == 0, stop=k == KD - 1)
                m.then_inc(q_up, 1)
                group(0)
                pe.wait_ge(qphi_ready, b + 1)
                after(pe, msg_ready, b)
                for o in range(KD):
                    pe.matmul(bank[ND_BANK][:, D + o * P:D + (o + 1) * P], ksd[:, o, :], kphi[:, o, :],
                              start=True, stop=True)
                for o in range(KD):
                    m = pe.matmul(bank[ND_BANK][:, o * P:(o + 1) * P], kvd[:, o, :], kphi[:, o, :],
                                  start=True, stop=True)
                m.then_inc(nd_up, 1)
                group(1)
                pe.wait_ge(msg_ready, b + 1)
                for k in range(KD):
                    m = pe.matmul(psM, msgT[:, k, :], wm[:, k, :], start=k == 0, stop=k == KD - 1)
                m.then_inc(m_up, 1)
                group(2)
                group(3)
                pe.wait_ge(m1_ready, b + 1)
                after(pe, h2n_ready, b)
                for k in range(KD):
                    m = pe.transpose(psT2[:, k * P:(k + 1) * P], m1[:, k * P:(k + 1) * P], ident[:, :])
                m.then_inc(m1T_up, 1)
                group(4)
                pe.wait_ge(m1T_ready, b + 1)
                after(pe, h1_ready, b)
                for o in range(2 * KD):
                    for k in range(2 * KD):
                        m = pe.matmul(bank[F_BANK][:, o * P:(o + 1) * P], w1m[:, k, o * P:(o + 1) * P],
                                      xT[:, k, :] if k < KD else m1T[:, k - KD, :], start=k == 0, stop=k == 2 * KD - 1)
                m.then_inc(f_up, 1)
                group(5)
                group(6)
                pe.wait_ge(h1_ready, b + 1)
                for k in range(2 * KD):
                    m = pe.matmul(psG, h1T[:, k, :], w2m[:, k, :], start=k == 0, stop=k == 2 * KD - 1)
                m.then_inc(h2_up, 1)
                group(7)

            body(0)
            with pe.Fori(1, NB) as b:
                body(b)
            for j in range(REST):
                g = NB * GPB + j
                pe_group(pe, g, j, g // SLOTS)

        def pe_program(pe):
            pe_tables(pe)
            pe.wait_ge(rel_ready, 1)
            pe.wait_ge(weights_in, 16 * 10)
            pe.wait_ge(edge_cols_down, NTAB)
            for h in range(KD):
                pe.matmul(bank[A_BANKS[h]][:, 0:P + 2], zeros[:, 0:P], zeros[:, 0:P + 2], start=True, stop=False,
                          skip_group_check=True)
            pe_block(pe, 0, 0, 0)
            pe_block(pe, 1, 1, 0)
            with pe.Fori(1, NB // 2) as i:
                pe_block(pe, 2 * i, 0, i)
                pe_block(pe, 2 * i + 1, 1, i)
            pe_block(pe, NB - 1, 0, NB // 2)
            for h in range(KD):
                m = pe.matmul(bank[A_BANKS[h]][:, 0:P + 2], zeros[:, 0:P], zeros[:, 0:P + 2], start=False, stop=True,
                              skip_group_check=True)
            m.then_inc(kv_used, 1)
            pe_mix(pe)
            pe_tail(pe)

        def act_block(act, b, u, i):
            act.wait_ge(xT_up, b + 1)
            after(act, xT_stored[u], 16 * i)
            act.copy(xTb[:, u, :, :].rearrange("p k n -> p (k n)"), psT).then_inc(xT_ready, 1)
            act.wait_ge(kmin_ready, b + 1)
            after(act, kphi_ready, b)
            act.activation(kexp[:, :], kmin[:, :], ACT.Exp).then_inc(kexp_ready, 1)
            act.wait_ge(kv_up, b + 1)
            after(act, kv_used, b)
            act.activation(vb[:, :, 0:P], bank[KV_BANK][:, D:2 * D].rearrange("p (k n) -> p k n", k=KD),
                           ACT.Copy, scale=valid[:, ds(b, 1)]).then_inc(v_ready, 1)
            after(act, stage_stored[u], 16 * i)
            for j in (0, 2):
                act.wait_ge(table_up, 4 * b + j + 1)
                act.copy(stage[:, u, 512 * j:512 * j + 512], bank[H_BANKS[j]][:, :]).then_inc(table_down_a, 1)

        def act_program(act):
            act.wait_ge(consts_set, 11)
            act.wait_ge(rel_ready, 1)
            act_block(act, 0, 0, 0)
            act_block(act, 1, 1, 0)
            with act.Fori(1, NB // 2) as i:
                act_block(act, 2 * i, 0, i)
                act_block(act, 2 * i + 1, 1, i)
            act_block(act, NB - 1, 0, NB // 2)
            act_mix(act)
            act_tail(act)

        def act_mix(act):
            def body(b):
                act.wait_ge(qmin_ready, b + 1)
                after(act, qphi_ready, b)
                act.activation(kexp[:, :], kmin[:, :], ACT.Exp).then_inc(qexp_ready, 1)
                act.wait_ge(nd_up, b + 1)
                after(act, msg_ready, b)
                act.activation(den[:, :], bank[ND_BANK][:, D:2 * D], ACT.Identity, bias=eps_c).then_inc(den_ready, 1)
                act.wait_ge(m_stats, b + 1)
                after(act, m1T_up, b)
                act.activation(m1, bank[QM_BANK][:, D:2 * D], ACT.Identity, scale=rs1[:, 1:2],
                               bias=rs1[:, 3:4]).then_inc(m1_ready, 1)
                act.wait_ge(f_up, b + 1)
                after(act, h2_up, b)
                act.activation(h1T[:, :, :].rearrange("p k n -> p (k n)"), bank[F_BANK][:, :], ACT.Relu).then_inc(h1_ready, 1)
                act.wait_ge(h2_stats, b + 1)
                after(act, mix_ready, b)
                act.activation(h2n[:, :], bank[TG_BANK][:, D:2 * D], ACT.Identity, scale=rs1[:, 5:6],
                               bias=rs1[:, 7:8]).then_inc(h2n_ready, 1)
            body(0)
            with act.Fori(1, NB) as b:
                body(b)

        def dve_group(dve, g, j):
            u = j % 2
            first = dve.value_load(group_tab[0:1, 0, ds(g, 1)], min_val=0, max_val=NB - 1)
            n = dve.value_load(group_tab[0:1, 1, ds(g, 1)], min_val=1, max_val=NB)
            with dve.If(n > 1):
                before = dve.value_load(group_tab[0:1, 2, ds(g, 1)], min_val=0, max_val=NGP * NB)
                with dve.Fori(1, n) as k:
                    dve.wait_ge(extra_down, before + k)
                    dve.tensor_scalar(drel_x[:, :], dcol[:, ds(g, 1), :].rearrange("p o t -> p (o t)"),
                                      block_off[:, ds(k, 1)], None, ALU.subtract).then_inc(extra_rel, 1)
                    dve.wait_ge(extra_rel, before + k)
                    dve.tensor_tensor(onehot_x[:, :, :], drel_x[:, :].unsqueeze(2).to_broadcast([P, GT, P]),
                                      iota_f[:, :].unsqueeze(1).to_broadcast([P, GT, P]), ALU.is_equal).then_inc(extra_onehot, 1)
                    dve.wait_ge(extra_up, before + k)
                    after(dve, sum_down, g - 1)
                    at = row_of(agg, nc.s_assert_within(first + k, 0, NB - 1))
                    dve.tensor_tensor(at, at, bank[X_BANK][:, 0:D], ALU.add).then_inc(extra_down, 1)
                dve.wait_ge(extra_down, before + n)
                dve.sem_inc(waits_passed, 1)
            after(dve, sum_up, g - 1)
            dve.tensor_tensor(onehot[:, u, :, :], dcol[:, ds(g, 1), :].rearrange("p o t -> p (o t)").unsqueeze(2)
                              .to_broadcast([P, GT, P]), iota_f[:, :].unsqueeze(1).to_broadcast([P, GT, P]),
                              ALU.is_equal).then_inc(onehot_ready, 1)
            if not (isinstance(g, int) and g == 0):
                dve_sum(dve, g - 1, 1 - u)

        def dve_sum(dve, g, u):
            first = dve.value_load(group_tab[0:1, 0, ds(g, 1)], min_val=0, max_val=NB - 1)
            dve.wait_ge(sum_up, g + 1)
            after(dve, sum_down, g)
            dve.tensor_tensor(row_of(agg, first), row_of(agg, first), bank[S_BANKS[u]][:, 0:D], ALU.add).then_inc(sum_down, 1)

        def norm_numbers(dve, ch, ps, x, r, t, shift, done):
            ch.link(dve.bn_stats(mst[:, 0:6], ps))
            dve.sem_inc(waits_passed, 1)
            ch.link(dve.bn_aggr(mst[:, 6:8], mst[:, 0:6]))
            rsqrt_steps(dve, ch, mst[:, 7:8], LN_EPS, x, r, t)
            dve.scalar_tensor_tensor(shift, mst[:, 6:7], -1.0, r, ALU.mult, ALU.mult).then_inc(done, 1)

        def dve_mix(dve):
            ch = Chain(dve, mix_own)
            dve.sem_inc(extra_down, 1)
            dve.wait_ge(kv_used, NB + 1)
            for h in range(KD):
                dve.tensor_tensor(kvd[:, h, :], heads[:, :], bank[A_BANKS[h]][:, 0:P], ALU.mult).then_inc(kvd_ready, 1)
                dve.tensor_scalar(ksd[:, h, :], heads[:, :], bank[A_BANKS[h]][:, P:P + 1], None, ALU.mult).then_inc(kvd_ready, 1)

            def body(b):
                def group(j):
                    dve_group(dve, b * GPB + j, j)
                q = bank[QM_BANK][:, 0:D]
                dve.wait_ge(q_up, b + 1)
                dve.tensor_scalar(kmin[:, :], q, 0.0, None, ALU.min).then_inc(qmin_ready, 1)
                dve.wait_ge(qexp_ready, b + 1)
                dve.scalar_tensor_tensor(kphi[:, :, :].rearrange("p k n -> p (k n)"), q, 0.0, kexp[:, :],
                                         ALU.max, ALU.add).then_inc(qphi_ready, 1)
                group(0)
                dve.wait_ge(den_ready, b + 1)
                ch.link(dve.reciprocal(den[:, :], den[:, :]))
                dve.tensor_tensor(msgT[:, :, :].rearrange("p k n -> p (k n)"), bank[ND_BANK][:, 0:D], den[:, :],
                                  ALU.mult).then_inc(msg_ready, 1)
                group(1)
                dve.wait_ge(m_up, b + 1)
                after(dve, m1_ready, b)
                norm_numbers(dve, ch, bank[QM_BANK][:, D:2 * D], rs1[:, 0:1], rs1[:, 1:2], rs1[:, 2:3], rs1[:, 3:4], m_stats)
                group(2)
                group(3)
                dve.wait_ge(m1T_up, b + 1)
                for k in range(KD):
                    m = dve.tensor_scalar(m1T[:, k, :], bank[TG_BANK][:, k * P:(k + 1) * P], g1c[:, k:k + 1],
                                          b1c[:, k:k + 1], ALU.mult, ALU.add)
                m.then_inc(m1T_ready, 1)
                group(4)
                group(5)
                group(6)
                dve.wait_ge(h2_up, b + 1)
                after(dve, h2n_ready, b)
                norm_numbers(dve, ch, bank[TG_BANK][:, D:2 * D], rs1[:, 4:5], rs1[:, 5:6], rs1[:, 6:7], rs1[:, 7:8], h2_stats)
                group(7)
                dve.wait_ge(h2n_ready, b + 1)
                ch.link(dve.tensor_tensor(h2n[:, :], h2n[:, :], g2_b, ALU.mult))
                ch.link(dve.tensor_tensor(h2n[:, :], h2n[:, :], b2m_b, ALU.add))
                dve.wait_ge(mix_rows_in, 32 * (b + 1))
                ch.link(dve.tensor_tensor(h2n[:, :], h2n[:, :], xnb[:, 0, :], ALU.add))
                dve.tensor_tensor(row_of(xt_all, b), h2n[:, :], x_rows[:, :], ALU.add).then_inc(mix_ready, 1)

            body(0)
            per_block = ch.n
            with dve.Fori(1, NB) as b:
                ch.at(b * per_block)
                body(b)
            for j in range(REST):
                dve_group(dve, NB * GPB + j, j)
            dve_sum(dve, NG - 1, (REST - 1) % 2)

        def mean_and_variance(dve, ch):
            mean, var, t = mv[:, :, 0], mv[:, :, 1], rstd[:, 2, :]
            ch.link(dve.tensor_tensor(t, stats[:, :, 1], stats[:, :, 4], ALU.subtract))
            ch.link(dve.tensor_scalar(t, t, 0.5, None, ALU.mult))
            ch.link(dve.tensor_tensor(t, t, t, ALU.mult))
            ch.link(dve.tensor_tensor(var, stats[:, :, 2], stats[:, :, 5], ALU.add))
            ch.link(dve.scalar_tensor_tensor(var, var, 1.0 / D, t, ALU.mult, ALU.add))
            ch.link(dve.tensor_tensor(mean, stats[:, :, 1], stats[:, :, 4], ALU.add))
            ch.link(dve.tensor_scalar(mean, mean, 0.5, None, ALU.mult))

        def dve_setup(dve, ch):
            dve.wait_ge(weights_in, 16 * 10)
            for r in range(NREL):
                o = w_rel[:, :, D * r:D * r + D]
                ch.link(dve.tensor_scalar(o, basis_sb[:, :, 0, :], compb[:, r, 0:1], None, ALU.mult))
                for i in range(1, NBASE):
                    ch.link(dve.scalar_tensor_tensor(o, basis_sb[:, :, i, :], compb[:, r, i:i + 1], o, ALU.mult, ALU.add))
            dve.wait_ge(edges_in, 16 * 9)
            dve.scalar_tensor_tensor(row_f, src_i, float(NREL), et_i, ALU.mult, ALU.add).then_inc(dve_own, 1)
            ch.n += 1
            ch.link(dve.tensor_copy(dst_f, dst_i))
            ch.link(dve.tensor_scalar(low_f, dst_f[:, GC - 1, :], 0.0, 1e6, ALU.is_lt, ALU.mult))
            ch.link(dve.tensor_tensor(low_f, low_f, dst_f[:, GC - 1, :], ALU.add))
            ch.link(dve.tensor_reduce(span[:, 0, 0:GC - 1], dst_f[:, 0:GC - 1, :], AX.X, ALU.min))
            ch.link(dve.tensor_reduce(span[:, 0, GC - 1:GC], low_f, AX.X, ALU.min))
            ch.link(dve.tensor_reduce(span[:, 1, :], dst_f, AX.X, ALU.max))
            ch.link(dve.tensor_copy(span_i[:, :, :], span[:, 0:2, :]))
            ch.link(dve.tensor_scalar(span_i[:, :, :], span_i[:, :, :], 7, None, ALU.arith_shift_right))
            ch.link(dve.tensor_copy(span[:, 2:4, :], span_i[:, :, :]))
            ch.link(dve.tensor_copy(span[:, 4, :], span[:, 2, :]))
            ch.link(dve.tensor_tensor(span[:, 5, :], span[:, 3, :], span[:, 2, :], ALU.subtract))
            ch.link(dve.tensor_scalar(span[:, 5, :], span[:, 5, :], 1.0, None, ALU.add))
            ch.link(dve.tensor_scalar(span[:, 6, :], span[:, 2, :], float(P), None, ALU.mult))
            for c in range(GC):
                m = dve.tensor_scalar(dst_f[:, c, :], dst_f[:, c, :], span[:, 6, c:c + 1], None, ALU.subtract)
                m.then_inc(dve_own, 1)
                ch.n += 1
            dve.wait_ge(dve_own, ch.n)
            dve.sem_inc(edge_rows_ready, 1)
            n = 0
            for c in range(GC):
                for o in (dcol, icol):
                    dve.wait_ge(edge_cols_up, n + 1)
                    k = min(P, NG - c * P)
                    dve.tensor_copy(o[:, c * P:c * P + k, :],
                                    bank[H_BANKS[n % 4]][:, :].rearrange("p (q g) -> p g q", q=GT)[:, 0:k, :]).then_inc(edge_cols_down, 1)
                    n += 1
            dve.wait_ge(edge_cols_up, n + 1)
            for j in range(2):
                ch.link(dve.tensor_copy(tab_f[:, j, :], bank[TAB_BANKS[j]][0:1, :]))
            ch.link(dve.tensor_copy(group_tab[:, 0:2, :], tab_f[:, 0:2, :]))
            ch.link(dve.tensor_scalar(tab_f[:, 1, :], tab_f[:, 1, :], -1.0, None, ALU.add))
            ch.link(dve.memset(tab_f[:, 2, 0:1], 0.0))
            ch.link(dve.tensor_tensor_scan(tab_f[:, 2, 1:NGP], tab_f[:, 1, 0:NGP - 1], tab_f[:, 1, 0:NGP - 1], 0.0,
                                           ALU.add, ALU.max))
            ch.link(dve.tensor_copy(group_tab[:, 2, :], tab_f[:, 2, :]))
            dve.sem_inc(edge_cols_down, 1)
            dve.sem_inc(tables_ready, 1)
            for i in range(7):
                dve.wait_ge(x_in[i], 16)
                for b in range(8 * i, min(8 * i + 8, NB)):
                    m = dve.bn_stats(stats[:, b, :], agg[:, b, :])
                    m.then_inc(dve_own, 1)
                    ch.n += 1
            dve.wait_ge(dve_own, ch.n)
            mean_and_variance(dve, ch)
            rsqrt_steps(dve, ch, mv[:, :, 1], LN_EPS, rstd[:, 1, :], rstd[:, 0, :], rstd[:, 2, :])

        def dve_normalise(dve, b, u, i):
            after(dve, xn_stored[u], 16 * i)
            after(dve, xT_up, b - 1)
            dve.tensor_scalar(xnb[:, u, :], row_of(agg, b), mv[:, ds(b, 1), 0], rstd[:, 0, ds(b, 1)],
                              ALU.subtract, ALU.mult).then_inc(xn_ready, 1)

        def dve_block(dve, b, u, i):
            dve.wait_ge(kv_up, b + 1)
            after(dve, kexp_ready, b)
            dve.tensor_scalar(kmin[:, :], bank[KV_BANK][:, 0:D], 0.0, None, ALU.min).then_inc(kmin_ready, 1)
            after(dve, kv_used, b)
            dve.tensor_copy(vb[:, :, P:P + 2], valid[:, ds(b, 1)].unsqueeze(2).to_broadcast([P, KD, 2])).then_inc(vones_ready, 1)
            dve.wait_ge(xn_ready, b + 1)
            dve.tensor_tensor(row_of(agg, b), xnb[:, u, :], hbias_b, ALU.add).then_inc(agg_bias, 1)
            dve.wait_ge(kexp_ready, b + 1)
            dve.wait_ge(v_ready, b + 1)
            dve.scalar_tensor_tensor(kphi[:, :, :].rearrange("p k n -> p (k n)"), bank[KV_BANK][:, 0:D], 0.0, kexp[:, :],
                                     ALU.max, ALU.add).then_inc(kphi_ready, 1)
            dve.wait_ge(loop_up, b + 1)
            dve.wait_ge(agg_bias, b + 1)
            dve.tensor_tensor(row_of(agg, b), row_of(agg, b), psL, ALU.add).then_inc(agg_init, 1)
            after(dve, stage_stored[u], 16 * i)
            for j in (1, 3):
                dve.wait_ge(table_up, 4 * b + j + 1)
                dve.tensor_copy(stage[:, u, 512 * j:512 * j + 512], bank[H_BANKS[j]][:, :]).then_inc(table_down_d, 1)

        def dve_program(dve):
            ch = Chain(dve, dve_own)
            dve_setup(dve, ch)
            dve.sem_inc(rel_ready, 1)
            dve.wait_ge(small_in, 16 * 9)
            dve.wait_ge(consts_set, 11)
            dve_normalise(dve, 0, 0, 0)
            dve_normalise(dve, 1, 1, 0)
            dve_block(dve, 0, 0, 0)
            dve_normalise(dve, 2, 0, 1)
            dve_block(dve, 1, 1, 0)
            with dve.Fori(1, NB // 2) as i:
                dve_normalise(dve, 2 * i + 1, 1, i)
                dve_block(dve, 2 * i, 0, i)
                dve_normalise(dve, 2 * i + 2, 0, i + 1)
                dve_block(dve, 2 * i + 1, 1, i)
            dve_block(dve, NB - 1, 0, NB // 2)
            dve_mix(dve)
            dve_tail(dve, ch)

        GB = 7
        NC = NB // GB
        assert NB % GB == 0
        temps = ring[:, :, :, :].rearrange("p s t d -> p (s t d)")
        W8 = NB * NEX
        logit, prob, pick1, pick2, cand, rank, index, tmp8 = (
            temps[:, W8 * i:W8 * (i + 1)].rearrange("p (b e) -> p b e", e=NEX) for i in range(8))
        tmp1 = temps[:, W8 * 8:W8 * 8 + 8 * NB].rearrange("p (i b) -> p i b", i=8)
        small = temps[:, W8 * 9:W8 * 9 + 8 * NEX].rearrange("p (i e) -> p i e", i=8)
        small_i = small[:, 7, :].bitcast(I32)
        keep = dcol[:, :, :].rearrange("p g t -> p (g t)")
        gates = keep[:, 0:2 * NB].rearrange("p (b k) -> p b k", k=2)
        slot_f = keep[:, 2 * NB:4 * NB].rearrange("p (b k) -> p b k", k=2)
        slots = keep[:, 4 * NB:6 * NB].bitcast(I32).rearrange("p (b k) -> p b k", k=2)
        starts = group_tab[0:1, 0, 0:NEX + 1]
        xtb = xnb
        xtT = xTb
        scat = onehot[:, :, :, :].rearrange("p u t n -> p (u t n)")[:, 0:2 * D].rearrange("p (u d) -> p u d", u=2)
        idx2 = idx_now[:, :, 0, 0:2]
        xg = xnb
        xgT = xTb[:, :, :, :].rearrange("p u k n -> p (u k n)").rearrange("p (k n) -> p k n", k=KD)
        hT = temps[:, 0:KH * MT].rearrange("p (k n) -> p k n", k=KH)
        yb = temps[:, KH * MT:KH * MT + MH * D].rearrange("p (m d) -> p m d", m=MH)
        got = onehot[:, :, :, :].rearrange("p u t n -> p (u t n)").rearrange("p (u k d) -> p u k d", u=2, k=2)
        res = xnb

        gelu_ready = sem("gelu_ready")
        tail_own = sem("tail_own")
        gnn_numbers = sem("gnn_numbers")
        gnn_normed = sem("gnn_normed")
        x2_numbers = sem("x2_numbers")
        xt_ready = sem("xt_ready")
        xt_kept = sem("xt_kept")
        xt_counted = sem("xt_counted")
        xtT_up = sem("xtT_up")
        xtT_ready = sem("xtT_ready")
        logit_up = sem("logit_up")
        logit_ready = sem("logit_ready")
        shifted_ready = sem("shifted_ready")
        exp_ready = sem("exp_ready")
        picks_ready = sem("picks_ready")
        ranks_up = sem("ranks_up")
        slots_ready = sem("slots_ready")
        scat_ready = sem("scat_ready")
        pair_idx = sem("pair_idx")
        scattered = [sem(f"scattered{i}") for i in range(2)]
        experts_in = [sem(f"experts_in{i}") for i in range(2)]
        expert_used = sem("expert_used")
        bucket_in = sem("bucket_in")
        bucketT_up = sem("bucketT_up")
        bucketT_ready = sem("bucketT_ready")
        hidden_up = sem("hidden_up")
        hidden_ready = sem("hidden_ready")
        answer_up = sem("answer_up")
        answer_ready = sem("answer_ready")
        answer_stored = sem("answer_stored")
        got_in = [sem(f"got_in{i}") for i in range(2)]
        res_part = sem("res_part")
        answers_there = sem("answers_there")
        res_ready = sem("res_ready")
        res_stored = [sem(f"res_stored{i}") for i in range(2)]

        def pairs(eng, body):
            body(0, 0, 0)
            body(1, 1, 0)
            with eng.Fori(1, NB // 2) as i:
                body(2 * i, 0, i)
                body(2 * i + 1, 1, i)
            body(NB - 1, 0, NB // 2)

        def rows_in_block(b):
            return LAST if isinstance(b, int) and b == NB - 1 else P

        def act_tail(act):
            act.wait_ge(sum_down, NG)
            with act.Fori(0, NC) as c:
                v = agg[:, ds(c * GB, GB), :]
                act.activation(v, v, ACT.Gelu).then_inc(gelu_ready, 1)
            act.wait_ge(gnn_numbers, 1)
            with act.Fori(0, NB) as b:
                act.activation(row_of(agg, b), row_of(agg, b), ACT.Identity, scale=rstd[:, 0, ds(b, 1)],
                               bias=rstd[:, 2, ds(b, 1)]).then_inc(gnn_normed, 1)
            act.wait_ge(x2_numbers, 1)

            def block_of(b, u, i):
                after(act, xt_counted, b - 1)
                after(act, xtT_up, b - 1)
                act.activation(xtb[:, u, :], row_of(agg, b), ACT.Identity, scale=rstd[:, 0, ds(b, 1)],
                               bias=rstd[:, 2, ds(b, 1)]).then_inc(xt_ready, 1)
                act.activation(row_of(xt_all, b), row_of(agg, b), ACT.Identity, scale=rstd[:, 0, ds(b, 1)],
                               bias=rstd[:, 2, ds(b, 1)]).then_inc(xt_kept, 1)
            pairs(act, block_of)
            act.wait_ge(shifted_ready, 1)
            act.activation(prob, logit, ACT.Exp).then_inc(exp_ready, 1)
            act.wait_ge(slots_ready, 1)
            act.wait_ge(res_part, 1)
            def expert(e, u, i):
                act.wait_ge(experts_in[u], 96 * (i + 1))
                act.sem_inc(waits_passed, 1)
                lo = act.value_load(starts[:, ds(e, 1)], min_val=0, max_val=NT - 1)
                hi = act.value_load(starts[:, ds(e + 1, 1)], min_val=1, max_val=NT)
                with act.Fori(lo, hi) as j:
                    act.wait_ge(bucketT_up, j + 1)
                    for k in range(KD):
                        m = act.activation(xgT[:, k, :], bank[T_BANK][:, k * MT:(k + 1) * MT], ACT.Identity,
                                           scale=eparm[u][:, KH + k:KH + k + 1],
                                           bias=eparm[u][:, KH + KD + k:KH + KD + k + 1])
                    m.then_inc(bucketT_ready, 1)
                    for c in range(KH):
                        act.wait_ge(hidden_up, KH * j + c + 1)
                        act.activation(hT[:, c, :], bank[H_BANKS[c % 4]][:, 0:MT], ACT.Gelu,
                                       bias=eparm[u][:, c:c + 1]).then_inc(hidden_ready, 1)
            with act.Fori(0, NEX // 2) as i:
                expert(2 * i, 0, i)
                expert(2 * i + 1, 1, i)

        def pe_tail(pe):
            psX = bank[T_BANK][:, 0:D]
            psR = bank[KV_BANK][:, 0:NEX]
            pe.wait_ge(x2_numbers, 1)

            def block_of(b, u, i):
                pe.wait_ge(xt_ready, b + 1)
                after(pe, xtT_ready, b)
                for k in range(KD):
                    m = pe.transpose(psX[:, k * P:(k + 1) * P], xtb[:, u, k * P:(k + 1) * P], ident[:, :])
                m.then_inc(xtT_up, 1)
                pe.wait_ge(xtT_ready, b + 1)
                after(pe, logit_ready, b)
                for k in range(KD):
                    m = pe.matmul(psR, xtT[:, u, k, :], wr_sb[:, k, :], start=k == 0, stop=k == KD - 1)
                m.then_inc(logit_up, 1)
            pairs(pe, block_of)
            pe.wait_ge(picks_ready, 1)
            cf = cand.rearrange("p b e -> p (b e)")
            pe.matmul(bank[A_BANKS[0]][:, 0:W8], upper[:, :], cf, start=True, stop=True)
            pe.matmul(bank[A_BANKS[1]][:, 0:W8], ones[:, :], cf, start=True, stop=True).then_inc(ranks_up, 1)
            pe.wait_ge(slots_ready, 1)

            def expert(e, u, i):
                pe.wait_ge(experts_in[u], 96 * (i + 1))
                pe.sem_inc(waits_passed, 1)
                lo = pe.value_load(starts[:, ds(e, 1)], min_val=0, max_val=NT - 1)
                hi = pe.value_load(starts[:, ds(e + 1, 1)], min_val=1, max_val=NT)
                with pe.Fori(lo, hi) as j:
                    pe.wait_ge(bucket_in, 16 * (j + 1))
                    for h in range(MH):
                        for k in range(KD):
                            m = pe.transpose(bank[T_BANK][:, k * MT + h * P:k * MT + (h + 1) * P],
                                             xg[:, h, k * P:(k + 1) * P], ident[:, :])
                    m.then_inc(bucketT_up, 1)
                    pe.wait_ge(bucketT_ready, j + 1)

                    def first_layer(c):
                        pe.wait_ge(hidden_ready, KH * j + c + 1)
                        for k in range(KD):
                            m = pe.matmul(bank[H_BANKS[c % 4]][:, 0:MT], we1[u][:, k, c * P:(c + 1) * P], xgT[:, k, :],
                                          start=k == 0, stop=k == KD - 1)
                        m.then_inc(hidden_up, 1)

                    def second_layer(c):
                        pe.wait_ge(hidden_ready, KH * j + c + 5)
                        if c == 0:
                            pe.wait_ge(answer_ready, j + 1)
                        for h in range(MH):
                            m = pe.matmul(bank[A_BANKS[h]][:, 0:D], hT[:, c, h * P:(h + 1) * P], we2[u][:, c, :],
                                          start=c == 0, stop=c == KH - 1)
                        return m
                    AHEAD = 3
                    for c in range(AHEAD):
                        first_layer(c)
                    for c in range(KH):
                        m = second_layer(c)
                        if c + AHEAD < KH:
                            first_layer(c + AHEAD)
                    m.then_inc(answer_up, 1)
            with pe.Fori(0, NEX // 2) as i:
                expert(2 * i, 0, i)
                expert(2 * i + 1, 1, i)

        def sp_tail(sp):
            sp.dma_start(answers[NT_LEAST * MT:NT * MT, :].rearrange("(u p) d -> p u d", p=P),
                         zeros[:, :].unsqueeze(1).to_broadcast([P, (NT - NT_LEAST) * MH, D])).then_inc(answer_stored, 16)
            sp.wait_ge(answer_stored, 16)
            for u in range(2):
                sp.wait_ge(scattered[u], 32 * ((NB + 1 - u) // 2))
            sp.wait_ge(logit_up, NB)
            total = sp.value_load(starts[:, NEX:NEX + 1], min_val=NEX, max_val=NT)

            def load(j):
                sp.dma_start(xg[:, :, :], bucket[ds(j * MT, MT), :].rearrange("(m p) d -> p m d", p=P)).then_inc(bucket_in, 16)

            def store(j):
                sp.dma_start(answers[ds(j * MT, MT), :].rearrange("(m p) d -> p m d", p=P), yb).then_inc(answer_stored, 16)
            load(0)
            with sp.Fori(1, total) as j:
                sp.wait_ge(bucketT_up, j)
                load(j)
                sp.wait_ge(answer_ready, j + 1)
                store(j - 1)
            sp.wait_ge(answer_ready, total + 1)
            store(total - 1)
            sp.wait_ge(answer_stored, total * 16 + 16)
            sp.sem_inc(answers_there, 1)

            def block_of(b, u, i):
                n = rows_in_block(b)
                sp.wait_ge(res_ready, b + 1)
                sp.dma_start(out[ds(b * P, n), :], res[0:n, u, :]).then_inc(res_stored[u], 16)
            pairs(sp, block_of)
            for u in range(2):
                sp.wait_ge(res_stored[u], 16 * ((NB + 1 - u) // 2))

        def pool_tail(pool):
            pool.wait_ge(zero_stored, 16 * (NT * MT // P // BZ))
            pool.wait_ge(slots_ready, 1)

            def scatter(b, u, i):
                n = rows_in_block(b)
                after(pool, scattered[u], 32 * i)
                pool.tensor_copy(idx2[:, u, :], slots[:, ds(b, 1), :].rearrange("p o k -> p (o k)")).then_inc(pair_idx, 1)
                pool.wait_ge(pair_idx, b + 1)
                pool.wait_ge(scat_ready, b + 1)
                pool.sem_inc(waits_passed, 1)
                for k in range(2):
                    pool.indirect_dma_start(out=bucket, out_offset=bass.IndirectOffsetOnAxis(ap=idx2[0:n, u, k:k + 1], axis=0),
                                            in_=scat[0:n, u, :], in_offset=None).then_inc(scattered[u], 16)
            pairs(pool, scatter)

            def expert(e, u):
                pool.dma_start(we1[u], W1[ds(e, 1), :, :].rearrange("o (k p) h -> p (o k) h", p=P)).then_inc(experts_in[u], 16)
                pool.dma_start(we2[u], W2[ds(e, 1), :, :].rearrange("o (k p) d -> p (o k) d", p=P)).then_inc(experts_in[u], 16)
                pool.dma_start(eparm[u][:, 0:KH], b1[ds(e, 1), :].rearrange("o (k p) -> p (o k)", p=P),
                               allow_slow_non_contiguous=True).then_inc(experts_in[u], 16)
                pool.dma_start(eparm[u][:, KH:KH + KD], ln_g[ds(e, 1), :].rearrange("o (k p) -> p (o k)", p=P),
                               allow_slow_non_contiguous=True).then_inc(experts_in[u], 16)
                pool.dma_start(eparm[u][:, KH + KD:EP], ln_b[ds(e, 1), :].rearrange("o (k p) -> p (o k)", p=P),
                               allow_slow_non_contiguous=True).then_inc(experts_in[u], 16)
                pool.dma_start(eb2[u], b2[ds(e, 1), :].rearrange("o d -> (o d)").partition_broadcast(P)).then_inc(experts_in[u], 16)
            expert(0, 0)
            expert(1, 1)
            with pool.Fori(1, NEX // 2) as i:
                for u in range(2):
                    pool.wait_ge(expert_used, 2 * i + u - 1)
                    pool.sem_inc(waits_passed, 1)
                    expert(2 * i + u, u)
            pool.wait_ge(answers_there, 1)

            def gather(b, u, i):
                n = rows_in_block(b)
                if not isinstance(b, int) or b >= 2:
                    pool.wait_ge(res_ready, b - 1)
                pool.tensor_copy(idx2[:, u, :], slots[:, ds(b, 1), :].rearrange("p o k -> p (o k)")).then_inc(pair_idx, 1)
                pool.wait_ge(pair_idx, NB + b + 1)
                pool.sem_inc(waits_passed, 1)
                for k in range(2):
                    pool.indirect_dma_start(out=got[0:n, u, k, :], out_offset=None, in_=answers,
                                            in_offset=bass.IndirectOffsetOnAxis(ap=idx2[0:n, u, k:k + 1], axis=0)).then_inc(got_in[u], 16)
            pairs(pool, gather)

        def dve_tail(dve, ch0):
            ch = Chain(dve, tail_own)
            with dve.Fori(0, NC) as c:
                dve.wait_ge(gelu_ready, c + 1)
                for i in range(GB):
                    dve.bn_stats(stats[:, ds(c * GB + i, 1), :].rearrange("p o s -> p (o s)"), row_of(agg, c * GB + i)).then_inc(tail_own, 1)
            ch.at(NB)
            dve.wait_ge(tail_own, NB)

            def aggregate():
                mean_and_variance(dve, ch)

            def numbers():
                rsqrt_steps(dve, ch, mv[:, :, 1], LN_EPS, rstd[:, 1, :], rstd[:, 0, :], rstd[:, 2, :])
                ch.link(dve.scalar_tensor_tensor(rstd[:, 2, :], mv[:, :, 0], -1.0, rstd[:, 0, :], ALU.mult, ALU.mult))
            aggregate()
            numbers()
            dve.sem_inc(gnn_numbers, 1)
            base = ch.n
            with dve.Fori(0, NC) as c:
                ch.at(base + c * (3 + GB))
                v = agg[:, ds(c * GB, GB), :]
                dve.wait_ge(gnn_normed, GB * (c + 1))
                ch.link(dve.tensor_tensor(v, v, gamma_b.unsqueeze(1).to_broadcast([P, GB, D]), ALU.mult))
                ch.link(dve.tensor_tensor(v, v, beta_b.unsqueeze(1).to_broadcast([P, GB, D]), ALU.add))
                ch.link(dve.tensor_tensor(v, v, xt_all[:, ds(c * GB, GB), :], ALU.add))
                for i in range(GB):
                    dve.bn_stats(stats[:, ds(c * GB + i, 1), :].rearrange("p o s -> p (o s)"), row_of(agg, c * GB + i)).then_inc(tail_own, 1)
            ch.at(base + NC * (3 + GB))
            dve.wait_ge(tail_own, ch.n)
            aggregate()
            numbers()
            dve.sem_inc(x2_numbers, 1)

            def block_of(b, u, i):
                dve.wait_ge(xt_ready, b + 1)
                dve.bn_stats(stats[:, ds(b, 1), :].rearrange("p o s -> p (o s)"), xtb[:, u, :]).then_inc(xt_counted, 1)
                dve.wait_ge(xtT_up, b + 1)
                dve.tensor_copy(xtT[:, u, :, :].rearrange("p k n -> p (k n)"), bank[T_BANK][:, 0:D]).then_inc(xtT_ready, 1)
                dve.wait_ge(logit_up, b + 1)
                dve.tensor_tensor(row_of(logit, b), bank[KV_BANK][:, 0:NEX], br_b, ALU.add).then_inc(logit_ready, 1)
            pairs(dve, block_of)
            dve.wait_ge(xt_counted, NB)
            dve.wait_ge(logit_ready, NB)
            dve.wait_ge(xt_kept, NB)
            aggregate()
            numbers()

            def e8(t):
                return t.unsqueeze(2).to_broadcast([P, NB, NEX])
            mx, sm, m1v, m2v, f1, f2, s12 = (tmp1[:, i, :] for i in range(7))
            ch.link(dve.tensor_reduce(mx, logit, AX.X, ALU.max))
            ch.link(dve.tensor_tensor(logit, logit, e8(mx), ALU.subtract))
            dve.sem_inc(shifted_ready, 1)
            dve.wait_ge(exp_ready, 1)
            ch.link(dve.tensor_reduce(sm, prob, AX.X, ALU.add))
            ch.link(dve.reciprocal(sm, sm))
            ch.link(dve.tensor_tensor(prob, prob, e8(sm), ALU.mult))

            def best(of, value, first, pick):
                ch.link(dve.tensor_reduce(value, of, AX.X, ALU.max))
                ch.link(dve.tensor_tensor(pick, of, e8(value), ALU.is_equal))
                ch.link(dve.tensor_scalar(pick, pick, -float(NEX), float(NEX), ALU.mult, ALU.add))
                ch.link(dve.tensor_tensor(cand, pick, iota_f[:, 0:NEX].unsqueeze(1).to_broadcast([P, NB, NEX]), ALU.add))
                ch.link(dve.tensor_reduce(first, cand, AX.X, ALU.min))
                ch.link(dve.tensor_tensor(pick, cand, e8(first), ALU.is_equal))
            best(prob, m1v, f1, pick1)
            ch.link(dve.tensor_scalar(tmp8, pick1, -2.0, None, ALU.mult))
            ch.link(dve.tensor_tensor(prob, prob, tmp8, ALU.add))
            best(prob, m2v, f2, pick2)
            ch.link(dve.tensor_tensor(s12, m1v, m2v, ALU.add))
            ch.link(dve.reciprocal(s12, s12))
            ch.link(dve.tensor_tensor(gates[:, :, 0], m1v, s12, ALU.mult))
            ch.link(dve.tensor_tensor(gates[:, :, 1], m2v, s12, ALU.mult))
            ch.link(dve.tensor_tensor(cand, pick1, pick2, ALU.add))
            ch.link(dve.tensor_tensor(cand, cand, e8(valid[:, :]), ALU.mult))
            dve.sem_inc(picks_ready, 1)
            dve.wait_ge(ranks_up, 1)
            flat8 = "p b e -> p (b e)"
            ch.link(dve.tensor_copy(rank.rearrange(flat8), bank[A_BANKS[0]][:, 0:W8]))
            ch.link(dve.tensor_copy(tmp8.rearrange(flat8), bank[A_BANKS[1]][:, 0:W8]))
            for e in range(NEX):
                ch.link(dve.tensor_tensor_scan(index[:, :, e], tmp8[:, :, e], tmp8[:, :, e], 0.0, ALU.add, ALU.max))
            cnt, ntile, upto_e, start_e = (small[:, i, :] for i in range(4))
            ch.link(dve.tensor_scalar(cnt, index[:, NB - 1, :], float(MT - 1), None, ALU.add))
            ch.link(dve.tensor_copy(small_i, cnt))
            ch.link(dve.tensor_scalar(small_i, small_i, MT.bit_length() - 1, None, ALU.arith_shift_right))
            ch.link(dve.tensor_copy(ntile, small_i))
            ch.link(dve.tensor_scalar(ntile, ntile, 1.0, None, ALU.max))
            ch.link(dve.tensor_tensor_scan(upto_e, ntile, ntile, 0.0, ALU.add, ALU.max))
            ch.link(dve.tensor_tensor(start_e, upto_e, ntile, ALU.subtract))
            ch.link(dve.tensor_copy(starts[:, 0:NEX], start_e[0:1, :]))
            ch.link(dve.tensor_copy(starts[:, NEX:NEX + 1], upto_e[0:1, NEX - 1:NEX]))
            ch.link(dve.tensor_scalar(start_e, start_e, float(MT), None, ALU.mult))
            ch.link(dve.tensor_tensor(index, index, tmp8, ALU.subtract))
            ch.link(dve.tensor_tensor(index, index, rank, ALU.add))
            ch.link(dve.tensor_tensor(index, index, start_e.unsqueeze(1).to_broadcast([P, NB, NEX]), ALU.add))
            for k, pick in enumerate((pick1, pick2)):
                ch.link(dve.tensor_tensor(tmp8, index, pick, ALU.mult))
                ch.link(dve.tensor_reduce(slot_f[:, :, k], tmp8, AX.X, ALU.add))
            ch.link(dve.tensor_copy(slots, slot_f))
            dve.sem_inc(slots_ready, 1)
            dve.sem_inc(res_part, 1)
            dve.sem_inc(hidden_ready, 4)
            dve.sem_inc(answer_ready, 1)

            def scatter(b, u, i):
                after(dve, scattered[u], 32 * i)
                dve.tensor_scalar(scat[:, u, :], row_of(xt_all, b), rstd[:, 0, ds(b, 1)], rstd[:, 2, ds(b, 1)],
                                  ALU.mult, ALU.add).then_inc(scat_ready, 1)
            pairs(dve, scatter)

            def expert(e, u, i):
                dve.wait_ge(experts_in[u], 96 * (i + 1))
                dve.sem_inc(waits_passed, 1)
                lo = dve.value_load(starts[:, ds(e, 1)], min_val=0, max_val=NT - 1)
                hi = dve.value_load(starts[:, ds(e + 1, 1)], min_val=1, max_val=NT)
                with dve.Fori(lo, hi) as j:
                    dve.wait_ge(answer_up, j + 1)
                    dve.wait_ge(answer_stored, 16 * (j + 1))
                    for h in range(MH):
                        m = dve.tensor_tensor(yb[:, h, :], bank[A_BANKS[h]][:, 0:D], eb2[u], ALU.add)
                    m.then_inc(answer_ready, 1)
                dve.wait_ge(answer_ready, hi + 1)
                dve.sem_inc(expert_used, 1)
            with dve.Fori(0, NEX // 2) as i:
                expert(2 * i, 0, i)
                expert(2 * i + 1, 1, i)

            def combine(b, u, i):
                dve.wait_ge(got_in[u], 32 * (i + 1))
                after(dve, res_stored[u], 16 * i)
                dve.scalar_tensor_tensor(res[:, u, :], got[:, u, 0, :], gates[:, ds(b, 1), 0], row_of(agg, b),
                                         ALU.mult, ALU.add).then_inc(res_part, 1)
                dve.wait_ge(res_part, b + 2)
                dve.scalar_tensor_tensor(res[:, u, :], got[:, u, 1, :], gates[:, ds(b, 1), 1], res[:, u, :],
                                         ALU.mult, ALU.add).then_inc(res_ready, 1)
            pairs(dve, combine)


        @block.sync
        def _(sp):
            sp_program(sp)

        @block.gpsimd
        def _(pool):
            pool_program(pool)

        @block.tensor
        def _(pe):
            pe_program(pe)

        @block.scalar
        def _(act):
            act_program(act)

        @block.vector
        def _(dve):
            dve_program(dve)


NAMES = ["x", "src", "dst", "edge_type_8", "L0_gnn_basis", "L0_gnn_comp", "L0_gnn_loop_w", "L0_gnn_h_bias",
         "L0_gnn_ln_gamma", "L0_gnn_ln_beta", "L0_mix_Wq", "L0_mix_Wk", "L0_mix_Wv", "L0_mix_Wm", "L0_mix_W1",
         "L0_mix_W2", "L0_mix_g1", "L0_mix_b1", "L0_mix_g2", "L0_mix_b2", "L0_ffn_Wr", "L0_ffn_br", "L0_ffn_ln_g",
         "L0_ffn_ln_b", "L0_ffn_W1", "L0_ffn_b1", "L0_ffn_W2", "L0_ffn_b2"]


def kernel(**inputs):
    import numpy as np
    import concourse.bacc as bacc
    from concourse.bass_utils import run_bass_kernel_spmd

    nc = bacc.Bacc("TRN2", target_bir_lowering=False, num_devices=1)
    arrays, args = {}, []
    for name in NAMES:
        a = np.ascontiguousarray(inputs[name])
        arrays[f"in_{name}"] = a
        args.append(nc.dram_tensor(f"in_{name}", a.shape, mybir.dt.from_np(a.dtype), kind="ExternalInput").ap())
    out = nc.dram_tensor("out_x", inputs["x"].shape, F32, kind="ExternalOutput").ap()
    bass_gps_layer(nc, *args, out)
    r = run_bass_kernel_spmd(nc, [arrays], core_ids=[0])
    return r.results[0]["out_x"]
```

```python
from contextlib import ExitStack

import concourse.bass as bass
from concourse import mybir

F32 = mybir.dt.float32
I32 = mybir.dt.int32
ALU = mybir.AluOpType
ACT = mybir.ActivationFunctionType
AX = mybir.AxisListType

P = 128
ds = bass.ds


class Chain:

    def __init__(self, eng, sem):
        self.eng, self.sem, self.n = eng, sem, 0

    def at(self, value):
        self.n = value

    def link(self, ins):
        ins.then_inc(self.sem, 1)
        self.n = self.n + 1
        self.eng.wait_ge(self.sem, self.n)


def rsqrt_steps(dve, chain, var, eps, x, y, t):
    chain.link(dve.tensor_scalar(x, var, eps, None, ALU.add))
    chain.link(dve.tensor_scalar(t.bitcast(I32), x.bitcast(I32), 1, None, ALU.logical_shift_right))
    chain.link(dve.tensor_scalar(y.bitcast(I32), t.bitcast(I32), -1.0, float(0x5F3759DF), ALU.mult, ALU.add))
    for _ in range(3):
        chain.link(dve.tensor_tensor(t, y, y, ALU.mult))
        chain.link(dve.tensor_tensor(t, t, x, ALU.mult))
        chain.link(dve.tensor_scalar(t, t, -0.5, 1.5, ALU.mult, ALU.add))
        chain.link(dve.tensor_tensor(y, y, t, ALU.mult))



def rsqrt_column(dve, chain, var, eps, x, y, t, h):
    chain.link(dve.tensor_scalar(x, var, eps, None, ALU.add))
    dve.tensor_scalar(h, var, eps, -0.5, ALU.add, ALU.mult).then_inc(chain.sem, 1)
    chain.n = chain.n + 1
    chain.link(dve.tensor_scalar(t.bitcast(I32), x.bitcast(I32), 1, None, ALU.logical_shift_right))
    chain.link(dve.tensor_scalar(y.bitcast(I32), t.bitcast(I32), -1.0, float(0x5F3759DF), ALU.mult, ALU.add))
    for _ in range(3):
        chain.link(dve.tensor_scalar(t, y, y, h, ALU.mult, ALU.mult))
        chain.link(dve.scalar_tensor_tensor(y, t, 1.5, y, ALU.add, ALU.mult))


def numbered(i, per_turn, c):
    return per_turn * i + c, c % 4, (per_turn // 4) * i + c // 4


def after(eng, s, n):
    if not (isinstance(n, int) and n <= 0):
        eng.wait_ge(s, n)


def row_of(t, b):
    return t[:, ds(b, 1), :].rearrange("p o d -> p (o d)")


def bass_gps_layer(nc, x, src, dst, etype, basis, comp, loop_w, h_bias, gamma, beta,
                   Wq, Wk, Wv, Wm, W1m, W2m, g1, b1m, g2, b2m,
                   Wr, br, ln_g, ln_b, W1, b1, W2, b2, out):
    N, D = x.shape
    E = src.shape[0]
    NB = -(-N // P)
    NP = NB * P
    LAST = N - (NB - 1) * P
    KD = D // P
    NREL, NBASE = comp.shape
    HEADS = 8
    HD = D // HEADS
    NEX, HID = b1.shape
    KH = HID // P
    LN_EPS, ATT_EPS = 1e-5, 1e-6
    GT = 4
    GE = GT * P
    NG = -(-E // GE)
    GC = -(-NG // P)
    NGP = GC * P
    FULLC = (E // GE) // P
    LASTC_FULL = E // GE - FULLC * P
    LASTC_REST = E - (E // GE) * GE
    SLOTS = 4
    GA, GB2 = 2, 6
    A_TOT = NB * GA
    REST = NG - NB * (GA + GB2)
    assert 2 * GA % SLOTS == 0 and 2 * GB2 % SLOTS == 0 and REST >= GB2
    MT = 256
    NT = (2 * N + NEX * MT) // MT + 1
    NT_LEAST = -(-2 * N // MT)
    MH = MT // P
    BZ = 6

    h_table = nc.dram_tensor("h_table", (NP * NREL, D), F32).ap()
    xn_rows = nc.dram_tensor("xn_rows", (NB, P, D), F32).ap()
    xn_cols = nc.dram_tensor("xn_cols", (NB, P, D), F32).ap()
    bucket = nc.dram_tensor("bucket", (NT * MT, D), F32).ap()
    answers = nc.dram_tensor("answers", (NT * MT, D), F32).ap()

    with ExitStack() as ctx:
        def sb(name, shape, dt=F32):
            return ctx.enter_context(nc.sbuf_tensor(name, shape, dt))

        def sem(name):
            return ctx.enter_context(nc.semaphore(name))

        agg = sb("agg", [P, NB, D])
        xt_all = sb("xt_all", [P, NB, D])
        big = sb("big", [P, 10 * 1024])
        ring = sb("ring", [P, SLOTS, GT, D])
        w_rel = big[:, 0:4096].rearrange("p (k n) -> p k n", k=KD)
        wkv = big[:, 4096:5120].rearrange("p (k n) -> p k n", k=KD)
        wq = big[:, 5120:5632].rearrange("p (k n) -> p k n", k=KD)
        wm = big[:, 5632:6144].rearrange("p (k n) -> p k n", k=KD)
        w1m = big[:, 6144:8192].rearrange("p (k n) -> p k n", k=2 * KD)
        w2m = big[:, 8192:9216].rearrange("p (k n) -> p k n", k=2 * KD)
        wloop = big[:, 9216:9728].rearrange("p (k n) -> p k n", k=KD)
        compb = big[:, 9728:9728 + NREL * NBASE].rearrange("p (r b) -> p r b", r=NREL)
        tiles = big[:, 0:4096].rearrange("p (u n) -> p u n", n=P)
        kphi, kvd, ksd, msgT, m1T = (tiles[:, KD * i:KD * i + KD, :] for i in range(5))
        h1T = tiles[:, 10:10 + 2 * KD, :]
        onehot_x = tiles[:, 14:14 + GT, :]
        kmin, kexp, den, h2n, x_rows = (big[:, 2304 + D * i:2304 + D * i + D] for i in range(5))
        vb = big[:, 2304 + 5 * D:2304 + 5 * D + KD * (P + 2)].rearrange("p (k n) -> p k n", k=KD)
        we1 = [big[:, 4096 * i:4096 * i + 2048].rearrange("p (k n) -> p k n", k=KD) for i in range(2)]
        we2 = [big[:, 4096 * i + 2048:4096 * i + 4096].rearrange("p (k n) -> p k n", k=KH) for i in range(2)]
        EP = KH + 2 * KD
        eparm = [big[:, 8192 + 1024 * i:8192 + 1024 * i + EP] for i in range(2)]
        eb2 = [big[:, 8192 + 1024 * i + 256:8192 + 1024 * i + 256 + D] for i in range(2)]
        stage = ring[:, :, :, :].rearrange("p s t d -> p (s t d)").rearrange("p (u n) -> p u n", u=2)
        basis_sb = stage[:, 0, 0:KD * NBASE * D].rearrange("p (k b d) -> p k b d", k=KD, b=NBASE)
        flat = xt_all[:, :, :].rearrange("p b d -> p (b d)")
        CW = GC * GE
        src_i = flat[:, 0:CW].bitcast(I32).rearrange("p (c e) -> p c e", c=GC)
        et_i = flat[:, CW:2 * CW].bitcast(I32).rearrange("p (c e) -> p c e", c=GC)
        dst_i = flat[:, 2 * CW:3 * CW].bitcast(I32).rearrange("p (c e) -> p c e", c=GC)
        row_f = flat[:, 3 * CW:4 * CW].rearrange("p (c e) -> p c e", c=GC)
        dst_f = flat[:, 4 * CW:5 * CW].rearrange("p (c e) -> p c e", c=GC)
        low_f = flat[:, 5 * CW:5 * CW + GE]
        dcol = sb("dcol", [P, NG, GT])
        icol = sb("icol", [P, NG, GT], I32)
        group_tab = sb("group_tab", [1, 3, NGP], I32)
        tab_f = flat[0:1, 5 * CW + GE:5 * CW + GE + 3 * NGP].rearrange("o (t g) -> o t g", t=3)
        span = sb("span", [P, 8, GC])
        span_i = sb("span_i", [P, 2, GC], I32)

        ident = sb("ident", [P, P])
        upper = sb("upper", [P, P])
        ones = sb("ones", [P, P])
        zeros = sb("zeros", [P, D])
        heads = sb("heads", [P, P])
        iota_f = sb("iota_f", [P, P])
        valid = sb("valid", [P, NB])
        rows = sb("rows", [P, 6, D])
        hbias_b, gamma_b, beta_b, g2_b, b2m_b = (rows[:, i, :] for i in range(5))
        wr_sb = rows[:, 5, 0:KD * NEX].rearrange("p (k e) -> p k e", k=KD)
        br_b = rows[:, 5, 64:64 + NEX]
        g1c = rows[:, 5, 80:80 + KD]
        b1c = rows[:, 5, 84:84 + KD]
        eps_c = rows[:, 5, 88:89]
        stats = sb("stats", [P, NB, 6])
        mv = sb("mv", [P, NB, 2])
        rstd = sb("rstd", [P, 3, NB])
        rs1 = sb("rs1", [P, 12])
        idx_now = sb("idx_now", [P, 2, SLOTS, GT], I32)
        onehot = sb("onehot", [P, 4, GT, P])
        drel_x = sb("drel_x", [P, GT])
        xnb = sb("xnb", [P, 2, D])
        xTb = sb("xTb", [P, 2, KD, P])
        m1 = xnb[:, 1, :]
        mst = sb("mst", [P, 8])
        block_off = sb("block_off", [P, NB])

        bank = [ctx.enter_context(nc.psum_tensor(f"bank{i}", [P, 512], F32)) for i in range(8)]

        block = ctx.enter_context(nc.Block())

        x_in = [sem(f"x_in{i}") for i in range(7)]
        edges_in = sem("edges_in")
        weights_in = sem("weights_in")
        small_in = sem("small_in")
        pads_set = sem("pads_set")
        consts_set = sem("consts_set")
        rel_ready = sem("rel_ready")
        dve_own = sem("dve_own")
        edge_rows_ready = sem("edge_rows_ready")
        edge_cols_up = sem("edge_cols_up")
        edge_cols_down = sem("edge_cols_down")
        tables_ready = sem("tables_ready")
        xn_ready = sem("xn_ready")
        xn_free = sem("xn_free")
        xT_up = sem("xT_up")
        xT_ready = sem("xT_ready")
        xT_stored = [sem(f"xT_stored{i}") for i in range(2)]
        xn_stored = [sem(f"xn_stored{i}") for i in range(2)]
        table_up = sem("table_up")
        table_down_a = sem("table_down_a")
        table_down_d = sem("table_down_d")
        stage_stored = [sem(f"stage_stored{i}") for i in range(2)]
        kv_up = sem("kv_up")
        kmin_ready = sem("kmin_ready")
        kexp_ready = sem("kexp_ready")
        kphi_ready = sem("kphi_ready")
        v_ready = sem("v_ready")
        vones_ready = sem("vones_ready")
        agg_init = sem("agg_init")
        kv_used = sem("kv_used")
        kvd_ready = sem("kvd_ready")
        zero_stored = sem("zero_stored")

        idx_ready = sem("idx_ready")
        slot_seen = sem("slot_seen")
        waits_passed = sem("waits_passed")
        rows_in = [sem(f"rows_in{i}") for i in range(SLOTS)]
        onehot_ready = sem("onehot_ready")
        sum_up = sem("sum_up")
        sum_down = sem("sum_down")
        extra_onehot = sem("extra_onehot")
        extra_up = sem("extra_up")
        extra_down = sem("extra_down")
        extra_rel = sem("extra_rel")
        cols_in = [sem(f"cols_in{i}") for i in range(2)]
        self_up = sem("self_up")
        self_added = sem("self_added")
        mix_rows_in = sem("mix_rows_in")
        mix_own = sem("mix_own")
        q_up = sem("q_up")
        qmin_ready = sem("qmin_ready")
        qexp_ready = sem("qexp_ready")
        qphi_ready = sem("qphi_ready")
        nd_up = sem("nd_up")
        den_ready = sem("den_ready")
        msg_ready = sem("msg_ready")
        m_up = sem("m_up")
        m_stats = sem("m_stats")
        m1_ready = sem("m1_ready")
        m1T_up = sem("m1T_up")
        m1T_ready = sem("m1T_ready")
        f_up = sem("f_up")
        h1_ready = sem("h1_ready")
        h2_up = sem("h2_up")
        h2_stats = sem("h2_stats")
        h2n_ready = sem("h2n_ready")
        mix_ready = sem("mix_ready")

        def pairs(eng, body):
            body(0, 0, 0)
            body(1, 1, 0)
            with eng.Fori(1, NB // 2) as i:
                body(2 * i, 0, i)
                body(2 * i + 1, 1, i)
            body(NB - 1, 0, NB // 2)

        def is_number(b, n):
            return isinstance(b, int) and b == n

        def rows_in_block(b):
            return LAST if is_number(b, NB - 1) else P

        def at_a(b, u, i, j):
            return numbered(i, 2 * GA, u * GA + j)

        def at_b(b, u, i, j):
            return numbered(i, 2 * GB2, A_TOT + u * GB2 + j)

        def row_dram(t, b):
            return t[ds(b, 1), :, :].rearrange("o p d -> (o p) d")

        def sp_program(sp):
            for i in range(6):
                sp.dma_start(agg[:, 8 * i:8 * i + 8, :],
                             x[1024 * i:1024 * i + 1024, :].rearrange("(b p) d -> p b d", p=P)).then_inc(x_in[i], 16)
            sp.wait_ge(pads_set, 4)
            sp.dma_start(agg[0:LAST, NB - 1, :], x[(NB - 1) * P:N, :]).then_inc(x_in[6], 16)
            for k in range(KD):
                sp.dma_start(basis_sb[:, k, :, :], basis[:, k * P:(k + 1) * P, :].rearrange("b p o -> p b o")).then_inc(weights_in, 16)
            sp.dma_start(compb, comp.rearrange("r b -> (r b)").partition_broadcast(P)
                         .rearrange("p (r b) -> p r b", r=NREL)).then_inc(weights_in, 16)
            sp.dma_start(wloop, loop_w.rearrange("(k p) o -> p k o", p=P)).then_inc(weights_in, 16)
            sp.dma_start(wkv[:, :, 0:D], Wk.rearrange("(k p) o -> p k o", p=P)).then_inc(weights_in, 16)
            sp.dma_start(wkv[:, :, D:2 * D], Wv.rearrange("(k p) o -> p k o", p=P)).then_inc(weights_in, 16)
            sp.dma_start(wq, Wq.rearrange("(k p) o -> p k o", p=P)).then_inc(weights_in, 16)
            sp.dma_start(wm, Wm.rearrange("(k p) o -> p k o", p=P)).then_inc(weights_in, 16)
            sp.dma_start(w1m, W1m.rearrange("(k p) o -> p k o", p=P)).then_inc(weights_in, 16)
            sp.dma_start(w2m, W2m.rearrange("(k p) o -> p k o", p=P)).then_inc(weights_in, 16)
            for row, vec in ((hbias_b, h_bias), (gamma_b, gamma), (beta_b, beta), (g2_b, g2), (b2m_b, b2m), (br_b, br)):
                sp.dma_start(row, vec.partition_broadcast(P)).then_inc(small_in, 16)
            sp.dma_start(wr_sb, Wr.rearrange("(k p) e -> p k e", p=P)).then_inc(small_in, 16)
            sp.dma_start(g1c, g1.rearrange("(k p) -> p k", p=P), allow_slow_non_contiguous=True).then_inc(small_in, 16)
            sp.dma_start(b1c, b1m.rearrange("(k p) -> p k", p=P), allow_slow_non_contiguous=True).then_inc(small_in, 16)
            def store_block(b, u, i):
                sp.wait_ge(xn_ready, b + 1)
                sp.dma_start(row_dram(xn_rows, b), xnb[:, u, :]).then_inc(xn_stored[u], 16)
                sp.wait_ge(xT_ready, b + 1)
                sp.dma_start(row_dram(xn_cols, b), xTb[:, u, :, :].rearrange("p k n -> p (k n)")).then_inc(xT_stored[u], 16)
                sp.wait_ge(table_down_a, 2 * b + 2)
                sp.wait_ge(table_down_d, 2 * b + 2)
                sp.dma_start(h_table[ds(b * (P * NREL), P * NREL), :].rearrange("(p r) d -> p (r d)", r=NREL),
                             stage[:, u, :]).then_inc(stage_stored[u], 16)
            store_block(0, 0, 0)
            store_block(1, 1, 0)
            with sp.Fori(1, NB // 2) as i:
                store_block(2 * i, 0, i)
                store_block(2 * i + 1, 1, i)
            store_block(NB - 1, 0, NB // 2)
            sp_mix(sp)
            sp_tail(sp)

        def pool_program(pool):
            pool.memset(agg[:, NB - 1, :], 0.0).then_inc(pads_set, 1)
            for t in (src_i, et_i):
                pool.memset(t[:, GC - 1, :], 0).then_inc(pads_set, 1)
            pool.memset(dst_i[:, GC - 1, :], -1).then_inc(pads_set, 1)
            pool.memset(ident[:, :], 0.0).then_inc(consts_set, 1)
            pool.memset(ones[:, :], 1.0).then_inc(consts_set, 1)
            pool.memset(zeros[:, :], 0.0).then_inc(consts_set, 1)
            pool.memset(eps_c, ATT_EPS).then_inc(consts_set, 1)
            pool.iota(iota_f[:, :], [[1, P]], base=0, channel_multiplier=0,
                      allow_small_or_imprecise_dtypes=True).then_inc(consts_set, 1)
            pool.iota(block_off[:, :], [[P, NB]], base=0, channel_multiplier=0,
                      allow_small_or_imprecise_dtypes=True).then_inc(consts_set, 1)
            pool.wait_ge(consts_set, 6)
            pool.affine_select(out=ident[:, :], in_=ident[:, :], pattern=[[-1, P]], compare_op=ALU.not_equal,
                               fill=1.0, base=0, channel_multiplier=1).then_inc(consts_set, 1)
            pool.affine_select(out=upper[:, :], in_=ones[:, :], pattern=[[1, P]], compare_op=ALU.is_gt,
                               fill=0.0, base=0, channel_multiplier=-1).then_inc(consts_set, 1)
            pool.affine_select(out=heads[:, :], in_=ones[:, :], pattern=[[-HD, P // HD], [0, HD]], compare_op=ALU.is_ge,
                               fill=0.0, base=0, channel_multiplier=1).then_inc(consts_set, 1)
            pool.affine_select(out=valid[:, :], in_=ones[:, 0:NB], pattern=[[-P, NB]], compare_op=ALU.is_ge,
                               fill=0.0, base=N - 1, channel_multiplier=-1).then_inc(consts_set, 1)
            pool.wait_ge(consts_set, 10)
            pool.affine_select(out=heads[:, :], in_=heads[:, :], pattern=[[HD, P // HD], [0, HD]], compare_op=ALU.is_ge,
                               fill=0.0, base=HD - 1, channel_multiplier=-1).then_inc(consts_set, 1)
            for t, a in ((src_i, src), (et_i, etype), (dst_i, dst)):
                full = FULLC * P * GE
                pool.dma_start(t[:, 0:FULLC, :], a[0:full].rearrange("(c p e) -> p c e", p=P, e=GE)).then_inc(edges_in, 16)
                pool.wait_ge(pads_set, 4)
                more = full + LASTC_FULL * GE
                pool.dma_start(t[0:LASTC_FULL, GC - 1, :], a[full:more].rearrange("(p e) -> p e", e=GE)).then_inc(edges_in, 16)
                pool.dma_start(t[LASTC_FULL:LASTC_FULL + 1, GC - 1, 0:LASTC_REST],
                               a[more:E].rearrange("(p e) -> p e", p=1)).then_inc(edges_in, 16)
            pool.wait_ge(consts_set, 11)
            with pool.Fori(0, NT * MT // P // BZ) as i:
                pool.dma_start(bucket[ds(i * P * BZ, P * BZ), :].rearrange("(u p) d -> p u d", p=P),
                               zeros[:, :].unsqueeze(1).to_broadcast([P, BZ, D])).then_inc(zero_stored, 16)
            gather_rows(pool)
            pool_tail(pool)

        GTOT = NG

        def gather_rows(pool):
            pool.wait_ge(stage_stored[0], 16 * ((NB + 1) // 2))
            pool.wait_ge(stage_stored[1], 16 * (NB // 2))
            pool.wait_ge(tables_ready, 1)

            def turn(g0, w, half, k):
                pool.tensor_copy(idx_now[:, half, 0:k, :], icol[:, ds(g0, k), :]).then_inc(idx_ready, 1)
                pool.wait_ge(idx_ready, w + 1)
                pool.sem_inc(slot_seen, 1)
                for s in range(k):
                    if not (isinstance(g0, int) and g0 < SLOTS):
                        pool.wait_ge(sum_up, g0 + s - SLOTS + 1)
                        pool.sem_inc(slot_seen, 1)
                    for q in range(GT):
                        pool.indirect_dma_start(
                            out=ring[:, s, q, :], out_offset=None, in_=h_table,
                            in_offset=bass.IndirectOffsetOnAxis(ap=idx_now[:, half, s, q:q + 1], axis=0),
                        ).then_inc(rows_in[s], 16)

            turns = NG // SLOTS
            turn(0, 0, 0, SLOTS)
            turn(SLOTS, 1, 1, SLOTS)
            with pool.Fori(1, turns // 2) as i:
                turn(i * (2 * SLOTS), 2 * i, 0, SLOTS)
                turn(i * (2 * SLOTS) + SLOTS, 2 * i + 1, 1, SLOTS)
            assert turns % 2 == 0
            turn(turns * SLOTS, turns, 0, NG % SLOTS)

        def sp_mix(sp):
            for u in range(2):
                n = 16 * ((NB + 1 - u) // 2)
                sp.wait_ge(xT_stored[u], n)
                sp.wait_ge(xn_stored[u], n)
            sp.wait_ge(table_up, 4 * NB)
            sp.wait_ge(agg_init, NB)

            def columns(b, u):
                sp.dma_start(xTb[:, u, :, :].rearrange("p k n -> p (k n)"), row_dram(xn_cols, b)).then_inc(cols_in[u], 16)

            def keys(b, u, i):
                after(sp, self_up, b - 1)
                columns(b, u)
            pairs(sp, keys)
            sp.wait_ge(self_up, NB)

            def queries(b, u, i):
                after(sp, f_up, b - 1)
                columns(b, u)
                after(sp, mix_ready, b)
                sp.dma_start(xnb[:, 0, :], row_dram(xn_rows, b)).then_inc(mix_rows_in, 16)
                n = rows_in_block(b)
                sp.dma_start(x_rows[0:n, :], x[ds(b * P, n), :]).then_inc(mix_rows_in, 16)
            pairs(sp, queries)

        H_BANKS, T_BANK, KV_BANK, A_BANKS = (0, 1, 2, 3), 4, 5, (6, 7)
        KEY_BANK, SELF_BANK, SUM_BANKS = 0, 1, (2, 3)
        TAB_BANKS = (5, 6)
        QM_BANK, ND_BANK, F_BANK, MT_BANK, G_BANK = 0, 1, 2, 3, 7
        S_BANKS, X_BANK = (4, 5), 6
        psT = bank[T_BANK][:, 0:D]

        def pe_tables(pe):
            pe.wait_ge(consts_set, 11)
            pe.wait_ge(edge_rows_ready, 1)
            n = 0
            for c in range(GC):
                for a in (dst_f, row_f):
                    if n >= 4:
                        pe.wait_ge(edge_cols_down, n - 3)
                    for q in range(GT):
                        m = pe.transpose(bank[H_BANKS[n % 4]][:, q * P:(q + 1) * P], a[:, c, q * P:(q + 1) * P],
                                         ident[:, :])
                    m.then_inc(edge_cols_up, 1)
                    n += 1
            for j in range(2):
                for c in range(GC):
                    m = pe.matmul(bank[TAB_BANKS[j]][0:1, c * P:(c + 1) * P], span[:, 4 + j, c:c + 1], ident[:, :],
                                  start=True, stop=True)
            m.then_inc(edge_cols_up, 1)

        NTAB = 2 * GC + 1

        def pe_columns(pe, b, u):
            pe.wait_ge(xn_ready, b + 1)
            after(pe, xT_ready, b)
            for k in range(KD):
                m = pe.transpose(psT[:, k * P:(k + 1) * P], xnb[:, u, k * P:(k + 1) * P], ident[:, :])
            m.then_inc(xT_up, 1)

        def pe_table(pe, b, u):
            pe.wait_ge(xT_ready, b + 1)
            for j in range(4):
                after(pe, table_down_d if j % 2 else table_down_a, 2 * (b - 1) + j // 2 + 1)
                for k in range(KD):
                    m = pe.matmul(bank[H_BANKS[j]][:, :], xTb[:, u, k, :], w_rel[:, k, 512 * j:512 * j + 512],
                                  start=k == 0, stop=k == KD - 1)
                m.then_inc(table_up, 1)

        def pe_extra(pe, g, s, n):
            with pe.If(n > 1):
                before = pe.value_load(group_tab[0:1, 2, ds(g, 1)], min_val=0, max_val=NGP * NB)
                with pe.Fori(1, n) as k:
                    pe.wait_ge(extra_onehot, before + k)
                    pe.wait_ge(extra_down, before + k)
                    for q in range(GT):
                        m = pe.matmul(bank[X_BANK][:, 0:D], onehot_x[:, q, :], ring[:, s, q, :],
                                      start=q == 0, stop=q == GT - 1)
                    m.then_inc(extra_up, 1)

        def group_numbers(eng, kind, row, least, most):
            have = {}

            def get(item, key):
                g, at, _ = item
                if key not in have:
                    _, values = nc.values_load_multi_w_load_instructions(
                        group_tab[0:1, row, ds(g, 4)], engines=[kind], min_val=least, max_val=most)
                    have.clear()
                    have.update({key + n: v for n, v in enumerate(values)})
                return have[key]
            return get

        def pe_group(pe, item, n):
            g, s, use = item
            pe.wait_ge(rows_in[s], 16 * GT * (use + 1))
            pe_extra(pe, g, s, n)
            pe.wait_ge(onehot_ready, g + 1)
            after(pe, sum_down, g - 1)
            for q in range(GT):
                m = pe.matmul(bank[S_BANKS[s % 2]][:, 0:D], onehot[:, s, q, :], ring[:, s, q, :],
                              start=q == 0, stop=q == GT - 1)
            m.then_inc(sum_up, 1)

        def pe_mix(pe):
            PE_ = mybir.EngineType.PE
            pe.wait_ge(table_down_a, 2 * NB)
            pe.wait_ge(table_down_d, 2 * NB)
            for h in range(KD):
                pe.matmul(bank[SUM_BANKS[h]][:, 0:P + 2], zeros[:, 0:P], zeros[:, 0:P + 2], start=True, stop=False,
                          skip_group_check=True)

            def keys(b, u, i):
                counts = group_numbers(pe, PE_, 1, 1, NB)
                def group(j):
                    item = at_a(b, u, i, j)
                    pe_group(pe, item, counts(item, j))
                pe.wait_ge(cols_in[u], 16 * (i + 1))
                after(pe, kphi_ready, b)
                after(pe, v_ready, b)
                for k in range(KD):
                    m = pe.matmul(bank[KEY_BANK][:, :], xTb[:, u, k, :], wkv[:, k, :], start=k == 0, stop=k == KD - 1)
                m.then_inc(kv_up, 1)
                after(pe, self_added, b)
                for k in range(KD):
                    m = pe.matmul(bank[SELF_BANK][:, 0:D], xTb[:, u, k, :], wloop[:, k, :], start=k == 0, stop=k == KD - 1)
                m.then_inc(self_up, 1)
                group(0)
                pe.wait_ge(kphi_ready, b + 1)
                pe.wait_ge(v_ready, b + 1)
                pe.wait_ge(vones_ready, b + 1)
                for h in range(KD):
                    m = pe.matmul(bank[SUM_BANKS[h]][:, 0:P + 2], kphi[:, h, :], vb[:, h, :], start=False, stop=False,
                                  skip_group_check=True)
                m.then_inc(kv_used, 1)
                group(1)
            pairs(pe, keys)
            for h in range(KD):
                m = pe.matmul(bank[SUM_BANKS[h]][:, 0:P + 2], zeros[:, 0:P], zeros[:, 0:P + 2], start=False, stop=True,
                              skip_group_check=True)
            m.then_inc(kv_used, 1)
            pe.wait_ge(kvd_ready, 2 * KD)
            pe.wait_ge(self_added, NB)

            psQ, psM = bank[QM_BANK][:, 0:D], bank[QM_BANK][:, D:2 * D]
            psT2, psG = bank[MT_BANK][:, 0:D], bank[G_BANK][:, 0:D]

            def queries(b, u, i):
                counts = group_numbers(pe, PE_, 1, 1, NB)
                this, last = not is_number(b, NB), not is_number(b, 0)

                def group(j):
                    item = at_b(b, u, i, j)
                    pe_group(pe, item, counts(item, j))
                if last:
                    pe.wait_ge(m1_ready, b)
                    for k in range(KD):
                        m = pe.transpose(psT2[:, k * P:(k + 1) * P], m1[:, k * P:(k + 1) * P], ident[:, :])
                    m.then_inc(m1T_up, 1)
                group(0)
                if this:
                    pe.wait_ge(cols_in[u], 16 * ((NB + 1 - u) // 2) + 16 * (i + 1))
                    after(pe, m1_ready, b)
                    for o in range(KD):
                        for k in range(KD):
                            m = pe.matmul(psQ[:, o * P:(o + 1) * P], wq[:, k, o * P:(o + 1) * P], xTb[:, u, k, :],
                                          start=k == 0, stop=k == KD - 1)
                    m.then_inc(q_up, 1)
                group(1)
                if last:
                    pe.wait_ge(m1T_ready, b)
                    after(pe, h1_ready, b - 1)
                    for o in range(2 * KD):
                        for k in range(2 * KD):
                            m = pe.matmul(bank[F_BANK][:, o * P:(o + 1) * P], w1m[:, k, o * P:(o + 1) * P],
                                          xTb[:, 1 - u, k, :] if k < KD else m1T[:, k - KD, :],
                                          start=k == 0, stop=k == 2 * KD - 1)
                    m.then_inc(f_up, 1)
                group(2)
                if this:
                    pe.wait_ge(qphi_ready, b + 1)
                    after(pe, msg_ready, b)
                    for o in range(KD):
                        pe.matmul(bank[ND_BANK][:, D + o * P:D + (o + 1) * P], ksd[:, o, :], kphi[:, o, :],
                                  start=True, stop=True)
                    for o in range(KD):
                        m = pe.matmul(bank[ND_BANK][:, o * P:(o + 1) * P], kvd[:, o, :], kphi[:, o, :],
                                      start=True, stop=True)
                    m.then_inc(nd_up, 1)
                group(3)
                if last:
                    pe.wait_ge(h1_ready, b)
                    after(pe, h2n_ready, b - 1)
                    for k in range(2 * KD):
                        m = pe.matmul(psG, h1T[:, k, :], w2m[:, k, :], start=k == 0, stop=k == 2 * KD - 1)
                    m.then_inc(h2_up, 1)
                group(4)
                if this:
                    pe.wait_ge(msg_ready, b + 1)
                    for k in range(KD):
                        m = pe.matmul(psM, msgT[:, k, :], wm[:, k, :], start=k == 0, stop=k == KD - 1)
                    m.then_inc(m_up, 1)
                group(5)
            pairs(pe, queries)
            queries(NB, 1, NB // 2)
            counts = group_numbers(pe, PE_, 1, 1, NB)
            for j in range(GB2, REST):
                item = at_b(NB, 1, NB // 2, j)
                if NG - item[0] < 4:
                    item_n = pe.value_load(group_tab[0:1, 1, item[0]:item[0] + 1], min_val=1, max_val=NB)
                else:
                    item_n = counts(item, j)
                pe_group(pe, item, item_n)

        def pe_program(pe):
            pe_tables(pe)
            pe.wait_ge(rel_ready, 1)
            pe.wait_ge(weights_in, 16 * 10)
            pe.wait_ge(edge_cols_down, NTAB)
            pe_columns(pe, 0, 0)

            def block_of(b, u, i):
                if not is_number(b, NB - 1):
                    pe_columns(pe, b + 1, 1 - u)
                pe_table(pe, b, u)
            pairs(pe, block_of)
            pe_mix(pe)
            pe_tail(pe)

        def act_columns(act, b, u, i):
            act.wait_ge(xT_up, b + 1)
            after(act, table_up, 4 * (b - 1))
            after(act, xT_stored[u], 16 * i)
            act.copy(xTb[:, u, :, :].rearrange("p k n -> p (k n)"), psT).then_inc(xT_ready, 1)

        def act_table(act, b, u, i):
            after(act, stage_stored[u], 16 * i)
            for j in (0, 2):
                act.wait_ge(table_up, 4 * b + j + 1)
                act.copy(stage[:, u, 512 * j:512 * j + 512], bank[H_BANKS[j]][:, :]).then_inc(table_down_a, 1)

        def act_program(act):
            act.wait_ge(consts_set, 11)
            act.wait_ge(rel_ready, 1)
            act_columns(act, 0, 0, 0)

            def block_of(b, u, i):
                if not is_number(b, NB - 1):
                    act_columns(act, b + 1, 1 - u, i + u)
                act_table(act, b, u, i)
            pairs(act, block_of)
            act_mix(act)
            act_tail(act)

        def act_mix(act):
            def keys(b, u, i):
                act.wait_ge(kmin_ready, b + 1)
                after(act, kphi_ready, b)
                act.activation(kexp[:, :], kmin[:, :], ACT.Exp).then_inc(kexp_ready, 1)
                act.wait_ge(kv_up, b + 1)
                after(act, kv_used, b)
                act.activation(vb[:, :, 0:P], bank[KEY_BANK][:, D:2 * D].rearrange("p (k n) -> p k n", k=KD),
                               ACT.Copy, scale=valid[:, ds(b, 1)]).then_inc(v_ready, 1)
            pairs(act, keys)

            def queries(b, u, i):
                this, last = not is_number(b, NB), not is_number(b, 0)
                if this:
                    act.wait_ge(qmin_ready, b + 1)
                    act.activation(kexp[:, :], kmin[:, :], ACT.Exp).then_inc(qexp_ready, 1)
                if last:
                    act.wait_ge(f_up, b)
                    after(act, h2_up, b - 1)
                    act.activation(h1T[:, :, :].rearrange("p k n -> p (k n)"), bank[F_BANK][:, :], ACT.Relu).then_inc(h1_ready, 1)
                if this:
                    act.wait_ge(nd_up, b + 1)
                    after(act, msg_ready, b)
                    act.activation(den[:, :], bank[ND_BANK][:, D:2 * D], ACT.Identity, bias=eps_c).then_inc(den_ready, 1)
                if last:
                    act.wait_ge(h2_stats, b)
                    after(act, mix_ready, b - 1)
                    act.activation(h2n[:, :], bank[G_BANK][:, 0:D], ACT.Identity, scale=rs1[:, 7:8],
                                   bias=rs1[:, 9:10]).then_inc(h2n_ready, 1)
                if this:
                    act.wait_ge(m_stats, b + 1)
                    after(act, m1T_up, b)
                    act.activation(m1, bank[QM_BANK][:, D:2 * D], ACT.Identity, scale=rs1[:, 1:2],
                                   bias=rs1[:, 3:4]).then_inc(m1_ready, 1)
            pairs(act, queries)
            queries(NB, 1, NB // 2)

        def one_hot(dve, out, columns, done):
            dve.tensor_tensor(out, columns.unsqueeze(2).to_broadcast([P, GT, P]),
                              iota_f[:, :].unsqueeze(1).to_broadcast([P, GT, P]), ALU.is_equal).then_inc(done, 1)

        def dve_onehot(dve, item):
            g, s, _ = item
            after(dve, sum_up, g - 3)
            one_hot(dve, onehot[:, s, :, :], dcol[:, ds(g, 1), :].rearrange("p o t -> p (o t)"), onehot_ready)

        def dve_extra(dve, item, n, first):
            g = item[0]
            with dve.If(n > 1):
                before = dve.value_load(group_tab[0:1, 2, ds(g, 1)], min_val=0, max_val=NGP * NB)
                with dve.Fori(1, n) as k:
                    dve.wait_ge(extra_down, before + k)
                    dve.tensor_scalar(drel_x[:, :], dcol[:, ds(g, 1), :].rearrange("p o t -> p (o t)"),
                                      block_off[:, ds(k, 1)], None, ALU.subtract).then_inc(extra_rel, 1)
                    dve.wait_ge(extra_rel, before + k)
                    one_hot(dve, onehot_x[:, :, :], drel_x[:, :], extra_onehot)
                    dve.wait_ge(extra_up, before + k)
                    after(dve, sum_down, g - 1)
                    at = row_of(agg, nc.s_assert_within(first + k, 0, NB - 1))
                    dve.tensor_tensor(at, at, bank[X_BANK][:, 0:D], ALU.add).then_inc(extra_down, 1)
                dve.wait_ge(extra_down, before + n)
                dve.sem_inc(waits_passed, 1)

        def dve_sum(dve, g, s, first):
            dve.wait_ge(sum_up, g + 1)
            after(dve, sum_down, g)
            dve.tensor_tensor(row_of(agg, first), row_of(agg, first), bank[S_BANKS[s % 2]][:, 0:D], ALU.add).then_inc(sum_down, 1)

        LEAD = 2

        def dve_groups(dve, place):
            counts = group_numbers(dve, mybir.EngineType.DVE, 1, 1, NB)
            firsts = group_numbers(dve, mybir.EngineType.DVE, 0, 0, NB - 1)

            def one(item, key, row, least, most, get):
                if isinstance(item[0], int) and NG - item[0] < 4:
                    return dve.value_load(group_tab[0:1, row, item[0]:item[0] + 1], min_val=least, max_val=most)
                return get(item, key)

            def step(j):
                item = place(j)
                g, s, _ = item
                begin = is_number(g, 0)
                if begin:
                    for a in range(LEAD):
                        dve_onehot(dve, place(a))
                n = one(item, j, 1, 1, NB, counts)
                low = None if begin else one(place(j - 1), j - 1, 0, 0, NB - 1, firsts)
                first = one(item, j, 0, 0, NB - 1, firsts)
                dve_extra(dve, item, n, first)
                if not (isinstance(g, int) and g + LEAD >= NG):
                    dve_onehot(dve, place(j + LEAD))
                if not begin:
                    dve_sum(dve, g - 1, (s - 1) % 4, low)
            return step

        def norm_numbers(dve, ch, ps, c, done):
            x, r, t, shift, h = (rs1[:, c + n:c + n + 1] for n in range(5))
            ch.link(dve.bn_stats(mst[:, 0:6], ps))
            dve.sem_inc(waits_passed, 1)
            ch.link(dve.bn_aggr(mst[:, 6:8], mst[:, 0:6]))
            rsqrt_column(dve, ch, mst[:, 7:8], LN_EPS, x, r, t, h)
            dve.scalar_tensor_tensor(shift, mst[:, 6:7], -1.0, r, ALU.mult, ALU.mult).then_inc(done, 1)

        def dve_mix(dve):
            ch = Chain(dve, mix_own)
            dve.sem_inc(extra_down, 1)

            def keys(b, u, i):
                step = dve_groups(dve, lambda j: at_a(b, u, i, j))
                k = bank[KEY_BANK][:, 0:D]
                dve.wait_ge(kv_up, b + 1)
                dve.tensor_scalar(kmin[:, :], k, 0.0, None, ALU.min).then_inc(kmin_ready, 1)
                after(dve, kv_used, b)
                dve.tensor_copy(vb[:, :, P:P + 2], valid[:, ds(b, 1)].unsqueeze(2).to_broadcast([P, KD, 2])).then_inc(vones_ready, 1)
                dve.wait_ge(kexp_ready, b + 1)
                dve.wait_ge(v_ready, b + 1)
                dve.scalar_tensor_tensor(kphi[:, :, :].rearrange("p k n -> p (k n)"), k, 0.0, kexp[:, :],
                                         ALU.max, ALU.add).then_inc(kphi_ready, 1)
                step(0)
                dve.wait_ge(self_up, b + 1)
                after(dve, sum_down, at_a(b, u, i, 0)[0])
                dve.tensor_tensor(row_of(agg, b), row_of(agg, b), bank[SELF_BANK][:, 0:D], ALU.add).then_inc(self_added, 1)
                dve.wait_ge(self_added, b + 1)
                dve.sem_inc(waits_passed, 1)
                step(1)
            pairs(dve, keys)
            dve.wait_ge(kv_used, NB + 1)
            for h in range(KD):
                dve.tensor_tensor(kvd[:, h, :], heads[:, :], bank[SUM_BANKS[h]][:, 0:P], ALU.mult).then_inc(kvd_ready, 1)
                dve.tensor_scalar(ksd[:, h, :], heads[:, :], bank[SUM_BANKS[h]][:, P:P + 1], None, ALU.mult).then_inc(kvd_ready, 1)

            def queries(b, u, i):
                this, last = not is_number(b, NB), not is_number(b, 0)
                step = dve_groups(dve, lambda j: at_b(b, u, i, j))
                if last:
                    dve.wait_ge(m1T_up, b)
                    for k in range(KD):
                        m = dve.tensor_scalar(m1T[:, k, :], bank[MT_BANK][:, k * P:(k + 1) * P], g1c[:, k:k + 1],
                                              b1c[:, k:k + 1], ALU.mult, ALU.add)
                    m.then_inc(m1T_ready, 1)
                step(0)
                q = bank[QM_BANK][:, 0:D]
                if this:
                    dve.wait_ge(q_up, b + 1)
                    dve.tensor_scalar(kmin[:, :], q, 0.0, None, ALU.min).then_inc(qmin_ready, 1)
                step(1)
                if this:
                    dve.wait_ge(qexp_ready, b + 1)
                    dve.scalar_tensor_tensor(kphi[:, :, :].rearrange("p k n -> p (k n)"), q, 0.0, kexp[:, :],
                                             ALU.max, ALU.add).then_inc(qphi_ready, 1)
                step(2)
                if this:
                    dve.wait_ge(den_ready, b + 1)
                    ch.link(dve.reciprocal(den[:, :], den[:, :]))
                    dve.tensor_tensor(msgT[:, :, :].rearrange("p k n -> p (k n)"), bank[ND_BANK][:, 0:D], den[:, :],
                                      ALU.mult).then_inc(msg_ready, 1)
                step(3)
                if last:
                    dve.wait_ge(h2_up, b)
                    after(dve, h2n_ready, b - 1)
                    norm_numbers(dve, ch, bank[G_BANK][:, 0:D], 6, h2_stats)
                step(4)
                if this:
                    dve.wait_ge(m_up, b + 1)
                    after(dve, m1_ready, b)
                    norm_numbers(dve, ch, bank[QM_BANK][:, D:2 * D], 0, m_stats)
                if last:
                    dve.wait_ge(h2n_ready, b)
                    ch.link(dve.tensor_tensor(h2n[:, :], h2n[:, :], g2_b, ALU.mult))
                    ch.link(dve.tensor_tensor(h2n[:, :], h2n[:, :], b2m_b, ALU.add))
                    dve.wait_ge(mix_rows_in, 32 * b)
                    ch.link(dve.tensor_tensor(h2n[:, :], h2n[:, :], xnb[:, 0, :], ALU.add))
                    dve.tensor_tensor(row_of(xt_all, b - 1), h2n[:, :], x_rows[:, :], ALU.add).then_inc(mix_ready, 1)
                step(5)
            queries(0, 0, 0)
            first_turn = ch.n
            queries(1, 1, 0)
            a_turn = ch.n - first_turn
            with dve.Fori(1, NB // 2) as i:
                for u in range(2):
                    ch.at(first_turn + (2 * i + u - 1) * a_turn)
                    queries(2 * i + u, u, i)
            ch.at(first_turn + (NB - 2) * a_turn)
            queries(NB - 1, 0, NB // 2)
            queries(NB, 1, NB // 2)
            step = dve_groups(dve, lambda j: at_b(NB, 1, NB // 2, j))
            for j in range(GB2, REST):
                step(j)
            last_first = dve.value_load(group_tab[0:1, 0, NG - 1:NG], min_val=0, max_val=NB - 1)
            dve_sum(dve, NG - 1, (NG - 1) % 4, last_first)

        def mean_and_variance(dve, ch):
            mean, var, t = mv[:, :, 0], mv[:, :, 1], rstd[:, 2, :]
            ch.link(dve.tensor_tensor(t, stats[:, :, 1], stats[:, :, 4], ALU.subtract))
            ch.link(dve.tensor_scalar(t, t, 0.5, None, ALU.mult))
            ch.link(dve.tensor_tensor(t, t, t, ALU.mult))
            ch.link(dve.tensor_tensor(var, stats[:, :, 2], stats[:, :, 5], ALU.add))
            ch.link(dve.scalar_tensor_tensor(var, var, 1.0 / D, t, ALU.mult, ALU.add))
            ch.link(dve.tensor_tensor(mean, stats[:, :, 1], stats[:, :, 4], ALU.add))
            ch.link(dve.tensor_scalar(mean, mean, 0.5, None, ALU.mult))

        def dve_setup(dve, ch):
            dve.wait_ge(weights_in, 16 * 10)
            for r in range(NREL):
                o = w_rel[:, :, D * r:D * r + D]
                ch.link(dve.tensor_scalar(o, basis_sb[:, :, 0, :], compb[:, r, 0:1], None, ALU.mult))
                for i in range(1, NBASE):
                    ch.link(dve.scalar_tensor_tensor(o, basis_sb[:, :, i, :], compb[:, r, i:i + 1], o, ALU.mult, ALU.add))
            dve.wait_ge(edges_in, 16 * 9)
            dve.scalar_tensor_tensor(row_f, src_i, float(NREL), et_i, ALU.mult, ALU.add).then_inc(dve_own, 1)
            ch.n += 1
            ch.link(dve.tensor_copy(dst_f, dst_i))
            ch.link(dve.tensor_scalar(low_f, dst_f[:, GC - 1, :], 0.0, 1e6, ALU.is_lt, ALU.mult))
            ch.link(dve.tensor_tensor(low_f, low_f, dst_f[:, GC - 1, :], ALU.add))
            ch.link(dve.tensor_reduce(span[:, 0, 0:GC - 1], dst_f[:, 0:GC - 1, :], AX.X, ALU.min))
            ch.link(dve.tensor_reduce(span[:, 0, GC - 1:GC], low_f, AX.X, ALU.min))
            ch.link(dve.tensor_reduce(span[:, 1, :], dst_f, AX.X, ALU.max))
            ch.link(dve.tensor_copy(span_i[:, :, :], span[:, 0:2, :]))
            ch.link(dve.tensor_scalar(span_i[:, :, :], span_i[:, :, :], 7, None, ALU.arith_shift_right))
            ch.link(dve.tensor_copy(span[:, 2:4, :], span_i[:, :, :]))
            ch.link(dve.tensor_copy(span[:, 4, :], span[:, 2, :]))
            ch.link(dve.tensor_tensor(span[:, 5, :], span[:, 3, :], span[:, 2, :], ALU.subtract))
            ch.link(dve.tensor_scalar(span[:, 5, :], span[:, 5, :], 1.0, None, ALU.add))
            ch.link(dve.tensor_scalar(span[:, 6, :], span[:, 2, :], float(P), None, ALU.mult))
            for c in range(GC):
                m = dve.tensor_scalar(dst_f[:, c, :], dst_f[:, c, :], span[:, 6, c:c + 1], None, ALU.subtract)
                m.then_inc(dve_own, 1)
                ch.n += 1
            dve.wait_ge(dve_own, ch.n)
            dve.sem_inc(edge_rows_ready, 1)
            n = 0
            for c in range(GC):
                for o in (dcol, icol):
                    dve.wait_ge(edge_cols_up, n + 1)
                    k = min(P, NG - c * P)
                    dve.tensor_copy(o[:, c * P:c * P + k, :],
                                    bank[H_BANKS[n % 4]][:, :].rearrange("p (q g) -> p g q", q=GT)[:, 0:k, :]).then_inc(edge_cols_down, 1)
                    n += 1
            dve.wait_ge(edge_cols_up, n + 1)
            for j in range(2):
                ch.link(dve.tensor_copy(tab_f[:, j, :], bank[TAB_BANKS[j]][0:1, :]))
            ch.link(dve.tensor_copy(group_tab[:, 0:2, :], tab_f[:, 0:2, :]))
            ch.link(dve.tensor_scalar(tab_f[:, 1, :], tab_f[:, 1, :], -1.0, None, ALU.add))
            ch.link(dve.memset(tab_f[:, 2, 0:1], 0.0))
            ch.link(dve.tensor_tensor_scan(tab_f[:, 2, 1:NGP], tab_f[:, 1, 0:NGP - 1], tab_f[:, 1, 0:NGP - 1], 0.0,
                                           ALU.add, ALU.max))
            ch.link(dve.tensor_copy(group_tab[:, 2, :], tab_f[:, 2, :]))
            dve.sem_inc(edge_cols_down, 1)
            dve.sem_inc(tables_ready, 1)
            for i in range(7):
                dve.wait_ge(x_in[i], 16)
                for b in range(8 * i, min(8 * i + 8, NB)):
                    m = dve.bn_stats(stats[:, b, :], agg[:, b, :])
                    m.then_inc(dve_own, 1)
                    ch.n += 1
            dve.wait_ge(dve_own, ch.n)
            mean_and_variance(dve, ch)
            rsqrt_steps(dve, ch, mv[:, :, 1], LN_EPS, rstd[:, 1, :], rstd[:, 0, :], rstd[:, 2, :])

        def dve_normalise(dve, b, u, i):
            after(dve, xn_stored[u], 16 * i)
            after(dve, xT_up, b - 1)
            after(dve, agg_init, b - 1)
            dve.tensor_scalar(xnb[:, u, :], row_of(agg, b), mv[:, ds(b, 1), 0], rstd[:, 0, ds(b, 1)],
                              ALU.subtract, ALU.mult).then_inc(xn_ready, 1)

        def dve_block(dve, b, u, i):
            dve.wait_ge(xn_ready, b + 1)
            dve.tensor_tensor(row_of(agg, b), xnb[:, u, :], hbias_b, ALU.add).then_inc(agg_init, 1)
            after(dve, stage_stored[u], 16 * i)
            for j in (1, 3):
                dve.wait_ge(table_up, 4 * b + j + 1)
                dve.tensor_copy(stage[:, u, 512 * j:512 * j + 512], bank[H_BANKS[j]][:, :]).then_inc(table_down_d, 1)

        def dve_program(dve):
            ch = Chain(dve, dve_own)
            dve_setup(dve, ch)
            dve.sem_inc(rel_ready, 1)
            dve.wait_ge(small_in, 16 * 9)
            dve.wait_ge(consts_set, 11)
            dve_normalise(dve, 0, 0, 0)
            dve_normalise(dve, 1, 1, 0)

            def block_of(b, u, i):
                dve_block(dve, b, u, i)
                if not (isinstance(b, int) and b >= NB - 2):
                    dve_normalise(dve, b + 2, u, i + 1)
            block_of(0, 0, 0)
            block_of(1, 1, 0)
            with dve.Fori(1, NB // 2 - 1) as i:
                block_of(2 * i, 0, i)
                block_of(2 * i + 1, 1, i)
            block_of(NB - 3, 0, NB // 2 - 1)
            block_of(NB - 2, 1, NB // 2 - 1)
            block_of(NB - 1, 0, NB // 2)
            dve.wait_ge(agg_init, NB)
            dve_mix(dve)
            dve_tail(dve, ch)

        GB = 7
        NC = NB // GB
        assert NB % GB == 0
        temps = ring[:, :, :, :].rearrange("p s t d -> p (s t d)")
        W8 = NB * NEX
        logit, prob, pick1, pick2, cand, rank, index, tmp8 = (
            temps[:, W8 * i:W8 * (i + 1)].rearrange("p (b e) -> p b e", e=NEX) for i in range(8))
        tmp1 = temps[:, W8 * 8:W8 * 8 + 8 * NB].rearrange("p (i b) -> p i b", i=8)
        small = temps[:, W8 * 9:W8 * 9 + 8 * NEX].rearrange("p (i e) -> p i e", i=8)
        small_i = small[:, 7, :].bitcast(I32)
        keep = dcol[:, :, :].rearrange("p g t -> p (g t)")
        gates = keep[:, 0:2 * NB].rearrange("p (b k) -> p b k", k=2)
        slot_f = keep[:, 2 * NB:4 * NB].rearrange("p (b k) -> p b k", k=2)
        slots = keep[:, 4 * NB:6 * NB].bitcast(I32).rearrange("p (b k) -> p b k", k=2)
        starts = group_tab[0:1, 0, 0:NEX + 1]
        xtb = xnb
        xtT = xTb
        scat = onehot[:, :, :, :].rearrange("p u t n -> p (u t n)")[:, 0:2 * D].rearrange("p (u d) -> p u d", u=2)
        idx2 = idx_now[:, :, 0, 0:2]
        xg = xnb
        xgT = xTb[:, :, :, :].rearrange("p u k n -> p (u k n)").rearrange("p (k n) -> p k n", k=KD)
        hT = temps[:, 0:KH * MT].rearrange("p (k n) -> p k n", k=KH)
        yb = temps[:, KH * MT:KH * MT + MH * D].rearrange("p (m d) -> p m d", m=MH)
        got = onehot[:, :, :, :].rearrange("p u t n -> p (u t n)").rearrange("p (u k d) -> p u k d", k=2, d=D)
        res = xnb

        gelu_ready = sem("gelu_ready")
        tail_own = sem("tail_own")
        gnn_numbers = sem("gnn_numbers")
        gnn_normed = sem("gnn_normed")
        x2_numbers = sem("x2_numbers")
        xt_ready = sem("xt_ready")
        xt_kept = sem("xt_kept")
        xt_counted = sem("xt_counted")
        xtT_up = sem("xtT_up")
        xtT_ready = sem("xtT_ready")
        logit_up = sem("logit_up")
        logit_ready = sem("logit_ready")
        shifted_ready = sem("shifted_ready")
        exp_ready = sem("exp_ready")
        picks_ready = sem("picks_ready")
        ranks_up = sem("ranks_up")
        slots_ready = sem("slots_ready")
        scat_ready = sem("scat_ready")
        pair_idx = sem("pair_idx")
        scattered = [sem(f"scattered{i}") for i in range(2)]
        experts_in = [sem(f"experts_in{i}") for i in range(2)]
        expert_used = sem("expert_used")
        bucket_in = sem("bucket_in")
        bucketT_up = sem("bucketT_up")
        bucketT_ready = sem("bucketT_ready")
        hidden_up = sem("hidden_up")
        hidden_ready = sem("hidden_ready")
        answer_up = sem("answer_up")
        answer_ready = sem("answer_ready")
        answer_stored = sem("answer_stored")
        got_in = [sem(f"got_in{i}") for i in range(2)]
        res_part = sem("res_part")
        answers_there = sem("answers_there")
        res_ready = sem("res_ready")
        res_stored = [sem(f"res_stored{i}") for i in range(2)]

        def act_tail(act):
            act.wait_ge(sum_down, NG)
            with act.Fori(0, NC) as c:
                v = agg[:, ds(c * GB, GB), :]
                act.activation(v, v, ACT.Gelu).then_inc(gelu_ready, 1)
            act.wait_ge(gnn_numbers, 1)
            with act.Fori(0, NB) as b:
                act.activation(row_of(agg, b), row_of(agg, b), ACT.Identity, scale=rstd[:, 0, ds(b, 1)],
                               bias=rstd[:, 2, ds(b, 1)]).then_inc(gnn_normed, 1)
            act.wait_ge(x2_numbers, 1)

            def block_of(b, u, i):
                after(act, xt_counted, b - 1)
                after(act, xtT_up, b - 1)
                act.activation(xtb[:, u, :], row_of(agg, b), ACT.Identity, scale=rstd[:, 0, ds(b, 1)],
                               bias=rstd[:, 2, ds(b, 1)]).then_inc(xt_ready, 1)
                act.activation(row_of(xt_all, b), row_of(agg, b), ACT.Identity, scale=rstd[:, 0, ds(b, 1)],
                               bias=rstd[:, 2, ds(b, 1)]).then_inc(xt_kept, 1)
            pairs(act, block_of)
            act.wait_ge(shifted_ready, 1)
            act.activation(prob, logit, ACT.Exp).then_inc(exp_ready, 1)
            act.wait_ge(slots_ready, 1)
            act.wait_ge(res_part, 1)
            def expert(e, u, i):
                act.wait_ge(experts_in[u], 96 * (i + 1))
                act.sem_inc(waits_passed, 1)
                lo = act.value_load(starts[:, ds(e, 1)], min_val=0, max_val=NT - 1)
                hi = act.value_load(starts[:, ds(e + 1, 1)], min_val=1, max_val=NT)
                with act.Fori(lo, hi) as j:
                    act.wait_ge(bucketT_up, j + 1)
                    for k in range(KD):
                        m = act.activation(xgT[:, k, :], bank[T_BANK][:, k * MT:(k + 1) * MT], ACT.Identity,
                                           scale=eparm[u][:, KH + k:KH + k + 1],
                                           bias=eparm[u][:, KH + KD + k:KH + KD + k + 1])
                    m.then_inc(bucketT_ready, 1)
                    for c in range(KH):
                        act.wait_ge(hidden_up, KH * j + c + 1)
                        act.activation(hT[:, c, :], bank[H_BANKS[c % 4]][:, 0:MT], ACT.Gelu,
                                       bias=eparm[u][:, c:c + 1]).then_inc(hidden_ready, 1)
            with act.Fori(0, NEX // 2) as i:
                expert(2 * i, 0, i)
                expert(2 * i + 1, 1, i)

        def pe_tail(pe):
            psX = bank[T_BANK][:, 0:D]
            psR = bank[KV_BANK][:, 0:NEX]
            pe.wait_ge(x2_numbers, 1)

            def block_of(b, u, i):
                pe.wait_ge(xt_ready, b + 1)
                after(pe, xtT_ready, b)
                for k in range(KD):
                    m = pe.transpose(psX[:, k * P:(k + 1) * P], xtb[:, u, k * P:(k + 1) * P], ident[:, :])
                m.then_inc(xtT_up, 1)
                pe.wait_ge(xtT_ready, b + 1)
                after(pe, logit_ready, b)
                for k in range(KD):
                    m = pe.matmul(psR, xtT[:, u, k, :], wr_sb[:, k, :], start=k == 0, stop=k == KD - 1)
                m.then_inc(logit_up, 1)
            pairs(pe, block_of)
            pe.wait_ge(picks_ready, 1)
            cf = cand.rearrange("p b e -> p (b e)")
            pe.matmul(bank[A_BANKS[0]][:, 0:W8], upper[:, :], cf, start=True, stop=True)
            pe.matmul(bank[A_BANKS[1]][:, 0:W8], ones[:, :], cf, start=True, stop=True).then_inc(ranks_up, 1)
            pe.wait_ge(slots_ready, 1)

            def expert(e, u, i):
                pe.wait_ge(experts_in[u], 96 * (i + 1))
                pe.sem_inc(waits_passed, 1)
                lo = pe.value_load(starts[:, ds(e, 1)], min_val=0, max_val=NT - 1)
                hi = pe.value_load(starts[:, ds(e + 1, 1)], min_val=1, max_val=NT)
                with pe.Fori(lo, hi) as j:
                    pe.wait_ge(bucket_in, 16 * (j + 1))
                    for h in range(MH):
                        for k in range(KD):
                            m = pe.transpose(bank[T_BANK][:, k * MT + h * P:k * MT + (h + 1) * P],
                                             xg[:, h, k * P:(k + 1) * P], ident[:, :])
                    m.then_inc(bucketT_up, 1)
                    pe.wait_ge(bucketT_ready, j + 1)

                    def first_layer(c):
                        pe.wait_ge(hidden_ready, KH * j + c + 1)
                        for k in range(KD):
                            m = pe.matmul(bank[H_BANKS[c % 4]][:, 0:MT], we1[u][:, k, c * P:(c + 1) * P], xgT[:, k, :],
                                          start=k == 0, stop=k == KD - 1)
                        m.then_inc(hidden_up, 1)

                    def second_layer(c):
                        pe.wait_ge(hidden_ready, KH * j + c + 5)
                        if c == 0:
                            pe.wait_ge(answer_ready, j + 1)
                        for h in range(MH):
                            m = pe.matmul(bank[A_BANKS[h]][:, 0:D], hT[:, c, h * P:(h + 1) * P], we2[u][:, c, :],
                                          start=c == 0, stop=c == KH - 1)
                        return m
                    AHEAD = 3
                    for c in range(AHEAD):
                        first_layer(c)
                    for c in range(KH):
                        m = second_layer(c)
                        if c + AHEAD < KH:
                            first_layer(c + AHEAD)
                    m.then_inc(answer_up, 1)
            with pe.Fori(0, NEX // 2) as i:
                expert(2 * i, 0, i)
                expert(2 * i + 1, 1, i)

        def sp_tail(sp):
            sp.dma_start(answers[NT_LEAST * MT:NT * MT, :].rearrange("(u p) d -> p u d", p=P),
                         zeros[:, :].unsqueeze(1).to_broadcast([P, (NT - NT_LEAST) * MH, D])).then_inc(answer_stored, 16)
            sp.wait_ge(answer_stored, 16)
            for u in range(2):
                sp.wait_ge(scattered[u], 32 * ((NB + 1 - u) // 2))
            sp.wait_ge(logit_up, NB)
            total = sp.value_load(starts[:, NEX:NEX + 1], min_val=NEX, max_val=NT)

            def load(j):
                sp.dma_start(xg[:, :, :], bucket[ds(j * MT, MT), :].rearrange("(m p) d -> p m d", p=P)).then_inc(bucket_in, 16)

            def store(j):
                sp.dma_start(answers[ds(j * MT, MT), :].rearrange("(m p) d -> p m d", p=P), yb).then_inc(answer_stored, 16)
            load(0)
            with sp.Fori(1, total) as j:
                sp.wait_ge(bucketT_up, j)
                load(j)
                sp.wait_ge(answer_ready, j + 1)
                store(j - 1)
            sp.wait_ge(answer_ready, total + 1)
            store(total - 1)
            sp.wait_ge(answer_stored, total * 16 + 16)
            sp.sem_inc(answers_there, 1)

            def block_of(b, u, i):
                n = rows_in_block(b)
                sp.wait_ge(res_ready, b + 1)
                sp.dma_start(out[ds(b * P, n), :], res[0:n, u, :]).then_inc(res_stored[u], 16)
            pairs(sp, block_of)
            for u in range(2):
                sp.wait_ge(res_stored[u], 16 * ((NB + 1 - u) // 2))

        def pool_tail(pool):
            pool.wait_ge(zero_stored, 16 * (NT * MT // P // BZ))
            pool.wait_ge(slots_ready, 1)

            def scatter(b, u, i):
                n = rows_in_block(b)
                after(pool, scattered[u], 32 * i)
                pool.tensor_copy(idx2[:, u, :], slots[:, ds(b, 1), :].rearrange("p o k -> p (o k)")).then_inc(pair_idx, 1)
                pool.wait_ge(pair_idx, b + 1)
                pool.wait_ge(scat_ready, b + 1)
                pool.sem_inc(waits_passed, 1)
                for k in range(2):
                    pool.indirect_dma_start(out=bucket, out_offset=bass.IndirectOffsetOnAxis(ap=idx2[0:n, u, k:k + 1], axis=0),
                                            in_=scat[0:n, u, :], in_offset=None).then_inc(scattered[u], 16)
            pairs(pool, scatter)

            def expert(e, u):
                pool.dma_start(we1[u], W1[ds(e, 1), :, :].rearrange("o (k p) h -> p (o k) h", p=P)).then_inc(experts_in[u], 16)
                pool.dma_start(we2[u], W2[ds(e, 1), :, :].rearrange("o (k p) d -> p (o k) d", p=P)).then_inc(experts_in[u], 16)
                pool.dma_start(eparm[u][:, 0:KH], b1[ds(e, 1), :].rearrange("o (k p) -> p (o k)", p=P),
                               allow_slow_non_contiguous=True).then_inc(experts_in[u], 16)
                pool.dma_start(eparm[u][:, KH:KH + KD], ln_g[ds(e, 1), :].rearrange("o (k p) -> p (o k)", p=P),
                               allow_slow_non_contiguous=True).then_inc(experts_in[u], 16)
                pool.dma_start(eparm[u][:, KH + KD:EP], ln_b[ds(e, 1), :].rearrange("o (k p) -> p (o k)", p=P),
                               allow_slow_non_contiguous=True).then_inc(experts_in[u], 16)
                pool.dma_start(eb2[u], b2[ds(e, 1), :].rearrange("o d -> (o d)").partition_broadcast(P)).then_inc(experts_in[u], 16)
            expert(0, 0)
            expert(1, 1)
            with pool.Fori(1, NEX // 2) as i:
                for u in range(2):
                    pool.wait_ge(expert_used, 2 * i + u - 1)
                    pool.sem_inc(waits_passed, 1)
                    expert(2 * i + u, u)
            pool.wait_ge(answers_there, 1)

            def gather(b, u, i):
                n = rows_in_block(b)
                if not isinstance(b, int) or b >= 2:
                    pool.wait_ge(res_ready, b - 1)
                pool.tensor_copy(idx2[:, u, :], slots[:, ds(b, 1), :].rearrange("p o k -> p (o k)")).then_inc(pair_idx, 1)
                pool.wait_ge(pair_idx, NB + b + 1)
                pool.sem_inc(waits_passed, 1)
                for k in range(2):
                    pool.indirect_dma_start(out=got[0:n, u, k, :], out_offset=None, in_=answers,
                                            in_offset=bass.IndirectOffsetOnAxis(ap=idx2[0:n, u, k:k + 1], axis=0)).then_inc(got_in[u], 16)
            pairs(pool, gather)

        def dve_tail(dve, ch0):
            ch = Chain(dve, tail_own)
            with dve.Fori(0, NC) as c:
                dve.wait_ge(gelu_ready, c + 1)
                for i in range(GB):
                    dve.bn_stats(stats[:, ds(c * GB + i, 1), :].rearrange("p o s -> p (o s)"), row_of(agg, c * GB + i)).then_inc(tail_own, 1)
            ch.at(NB)
            dve.wait_ge(tail_own, NB)

            def aggregate():
                mean_and_variance(dve, ch)

            def numbers():
                rsqrt_steps(dve, ch, mv[:, :, 1], LN_EPS, rstd[:, 1, :], rstd[:, 0, :], rstd[:, 2, :])
                ch.link(dve.scalar_tensor_tensor(rstd[:, 2, :], mv[:, :, 0], -1.0, rstd[:, 0, :], ALU.mult, ALU.mult))
            aggregate()
            numbers()
            dve.sem_inc(gnn_numbers, 1)
            base = ch.n
            with dve.Fori(0, NC) as c:
                ch.at(base + c * (3 + GB))
                v = agg[:, ds(c * GB, GB), :]
                dve.wait_ge(gnn_normed, GB * (c + 1))
                ch.link(dve.tensor_tensor(v, v, gamma_b.unsqueeze(1).to_broadcast([P, GB, D]), ALU.mult))
                ch.link(dve.tensor_tensor(v, v, beta_b.unsqueeze(1).to_broadcast([P, GB, D]), ALU.add))
                ch.link(dve.tensor_tensor(v, v, xt_all[:, ds(c * GB, GB), :], ALU.add))
                for i in range(GB):
                    dve.bn_stats(stats[:, ds(c * GB + i, 1), :].rearrange("p o s -> p (o s)"), row_of(agg, c * GB + i)).then_inc(tail_own, 1)
            ch.at(base + NC * (3 + GB))
            dve.wait_ge(tail_own, ch.n)
            aggregate()
            numbers()
            dve.sem_inc(x2_numbers, 1)

            def block_of(b, u, i):
                dve.wait_ge(xt_ready, b + 1)
                dve.bn_stats(stats[:, ds(b, 1), :].rearrange("p o s -> p (o s)"), xtb[:, u, :]).then_inc(xt_counted, 1)
                dve.wait_ge(xtT_up, b + 1)
                dve.tensor_copy(xtT[:, u, :, :].rearrange("p k n -> p (k n)"), bank[T_BANK][:, 0:D]).then_inc(xtT_ready, 1)
                dve.wait_ge(logit_up, b + 1)
                dve.tensor_tensor(row_of(logit, b), bank[KV_BANK][:, 0:NEX], br_b, ALU.add).then_inc(logit_ready, 1)
            pairs(dve, block_of)
            dve.wait_ge(xt_counted, NB)
            dve.wait_ge(logit_ready, NB)
            dve.wait_ge(xt_kept, NB)
            aggregate()
            numbers()

            def e8(t):
                return t.unsqueeze(2).to_broadcast([P, NB, NEX])
            mx, sm, m1v, m2v, f1, f2, s12 = (tmp1[:, i, :] for i in range(7))
            ch.link(dve.tensor_reduce(mx, logit, AX.X, ALU.max))
            ch.link(dve.tensor_tensor(logit, logit, e8(mx), ALU.subtract))
            dve.sem_inc(shifted_ready, 1)
            dve.wait_ge(exp_ready, 1)
            ch.link(dve.tensor_reduce(sm, prob, AX.X, ALU.add))
            ch.link(dve.reciprocal(sm, sm))
            ch.link(dve.tensor_tensor(prob, prob, e8(sm), ALU.mult))

            def best(of, value, first, pick):
                ch.link(dve.tensor_reduce(value, of, AX.X, ALU.max))
                ch.link(dve.tensor_tensor(pick, of, e8(value), ALU.is_equal))
                ch.link(dve.tensor_scalar(pick, pick, -float(NEX), float(NEX), ALU.mult, ALU.add))
                ch.link(dve.tensor_tensor(cand, pick, iota_f[:, 0:NEX].unsqueeze(1).to_broadcast([P, NB, NEX]), ALU.add))
                ch.link(dve.tensor_reduce(first, cand, AX.X, ALU.min))
                ch.link(dve.tensor_tensor(pick, cand, e8(first), ALU.is_equal))
            best(prob, m1v, f1, pick1)
            ch.link(dve.tensor_scalar(tmp8, pick1, -2.0, None, ALU.mult))
            ch.link(dve.tensor_tensor(prob, prob, tmp8, ALU.add))
            best(prob, m2v, f2, pick2)
            ch.link(dve.tensor_tensor(s12, m1v, m2v, ALU.add))
            ch.link(dve.reciprocal(s12, s12))
            ch.link(dve.tensor_tensor(gates[:, :, 0], m1v, s12, ALU.mult))
            ch.link(dve.tensor_tensor(gates[:, :, 1], m2v, s12, ALU.mult))
            ch.link(dve.tensor_tensor(cand, pick1, pick2, ALU.add))
            ch.link(dve.tensor_tensor(cand, cand, e8(valid[:, :]), ALU.mult))
            dve.sem_inc(picks_ready, 1)
            dve.wait_ge(ranks_up, 1)
            flat8 = "p b e -> p (b e)"
            ch.link(dve.tensor_copy(rank.rearrange(flat8), bank[A_BANKS[0]][:, 0:W8]))
            ch.link(dve.tensor_copy(tmp8.rearrange(flat8), bank[A_BANKS[1]][:, 0:W8]))
            for e in range(NEX):
                ch.link(dve.tensor_tensor_scan(index[:, :, e], tmp8[:, :, e], tmp8[:, :, e], 0.0, ALU.add, ALU.max))
            cnt, ntile, upto_e, start_e = (small[:, i, :] for i in range(4))
            ch.link(dve.tensor_scalar(cnt, index[:, NB - 1, :], float(MT - 1), None, ALU.add))
            ch.link(dve.tensor_copy(small_i, cnt))
            ch.link(dve.tensor_scalar(small_i, small_i, MT.bit_length() - 1, None, ALU.arith_shift_right))
            ch.link(dve.tensor_copy(ntile, small_i))
            ch.link(dve.tensor_scalar(ntile, ntile, 1.0, None, ALU.max))
            ch.link(dve.tensor_tensor_scan(upto_e, ntile, ntile, 0.0, ALU.add, ALU.max))
            ch.link(dve.tensor_tensor(start_e, upto_e, ntile, ALU.subtract))
            ch.link(dve.tensor_copy(starts[:, 0:NEX], start_e[0:1, :]))
            ch.link(dve.tensor_copy(starts[:, NEX:NEX + 1], upto_e[0:1, NEX - 1:NEX]))
            ch.link(dve.tensor_scalar(start_e, start_e, float(MT), None, ALU.mult))
            ch.link(dve.tensor_tensor(index, index, tmp8, ALU.subtract))
            ch.link(dve.tensor_tensor(index, index, rank, ALU.add))
            ch.link(dve.tensor_tensor(index, index, start_e.unsqueeze(1).to_broadcast([P, NB, NEX]), ALU.add))
            for k, pick in enumerate((pick1, pick2)):
                ch.link(dve.tensor_tensor(tmp8, index, pick, ALU.mult))
                ch.link(dve.tensor_reduce(slot_f[:, :, k], tmp8, AX.X, ALU.add))
            ch.link(dve.tensor_copy(slots, slot_f))
            dve.sem_inc(slots_ready, 1)
            dve.sem_inc(res_part, 1)
            dve.sem_inc(hidden_ready, 4)
            dve.sem_inc(answer_ready, 1)

            def scatter(b, u, i):
                after(dve, scattered[u], 32 * i)
                dve.tensor_scalar(scat[:, u, :], row_of(xt_all, b), rstd[:, 0, ds(b, 1)], rstd[:, 2, ds(b, 1)],
                                  ALU.mult, ALU.add).then_inc(scat_ready, 1)
            pairs(dve, scatter)

            def expert(e, u, i):
                dve.wait_ge(experts_in[u], 96 * (i + 1))
                dve.sem_inc(waits_passed, 1)
                lo = dve.value_load(starts[:, ds(e, 1)], min_val=0, max_val=NT - 1)
                hi = dve.value_load(starts[:, ds(e + 1, 1)], min_val=1, max_val=NT)
                with dve.Fori(lo, hi) as j:
                    dve.wait_ge(answer_up, j + 1)
                    dve.wait_ge(answer_stored, 16 * (j + 1))
                    for h in range(MH):
                        m = dve.tensor_tensor(yb[:, h, :], bank[A_BANKS[h]][:, 0:D], eb2[u], ALU.add)
                    m.then_inc(answer_ready, 1)
                dve.wait_ge(answer_ready, hi + 1)
                dve.sem_inc(expert_used, 1)
            with dve.Fori(0, NEX // 2) as i:
                expert(2 * i, 0, i)
                expert(2 * i + 1, 1, i)

            def combine(b, u, i):
                dve.wait_ge(got_in[u], 32 * (i + 1))
                after(dve, res_stored[u], 16 * i)
                dve.scalar_tensor_tensor(res[:, u, :], got[:, u, 0, :], gates[:, ds(b, 1), 0], row_of(agg, b),
                                         ALU.mult, ALU.add).then_inc(res_part, 1)
                dve.wait_ge(res_part, b + 2)
                dve.scalar_tensor_tensor(res[:, u, :], got[:, u, 1, :], gates[:, ds(b, 1), 1], res[:, u, :],
                                         ALU.mult, ALU.add).then_inc(res_ready, 1)
            pairs(dve, combine)


        @block.sync
        def _(sp):
            sp_program(sp)

        @block.gpsimd
        def _(pool):
            pool_program(pool)

        @block.tensor
        def _(pe):
            pe_program(pe)

        @block.scalar
        def _(act):
            act_program(act)

        @block.vector
        def _(dve):
            dve_program(dve)


NAMES = ["x", "src", "dst", "edge_type_8", "L0_gnn_basis", "L0_gnn_comp", "L0_gnn_loop_w", "L0_gnn_h_bias",
         "L0_gnn_ln_gamma", "L0_gnn_ln_beta", "L0_mix_Wq", "L0_mix_Wk", "L0_mix_Wv", "L0_mix_Wm", "L0_mix_W1",
         "L0_mix_W2", "L0_mix_g1", "L0_mix_b1", "L0_mix_g2", "L0_mix_b2", "L0_ffn_Wr", "L0_ffn_br", "L0_ffn_ln_g",
         "L0_ffn_ln_b", "L0_ffn_W1", "L0_ffn_b1", "L0_ffn_W2", "L0_ffn_b2"]


def kernel(**inputs):
    import numpy as np
    import concourse.bacc as bacc
    from concourse.bass_utils import run_bass_kernel_spmd

    nc = bacc.Bacc("TRN2", target_bir_lowering=False, num_devices=1)
    arrays, args = {}, []
    for name in NAMES:
        a = np.ascontiguousarray(inputs[name])
        arrays[f"in_{name}"] = a
        args.append(nc.dram_tensor(f"in_{name}", a.shape, mybir.dt.from_np(a.dtype), kind="ExternalInput").ap())
    out = nc.dram_tensor("out_x", inputs["x"].shape, F32, kind="ExternalOutput").ap()
    bass_gps_layer(nc, *args, out)
    r = run_bass_kernel_spmd(nc, [arrays], core_ids=[0])
    return r.results[0]["out_x"]
```

```python
from contextlib import ExitStack

import concourse.bass as bass
from concourse import mybir

F32 = mybir.dt.float32
I32 = mybir.dt.int32
ALU = mybir.AluOpType
ACT = mybir.ActivationFunctionType
AX = mybir.AxisListType

P = 128
ds = bass.ds


class Chain:

    def __init__(self, eng, sem):
        self.eng, self.sem, self.n = eng, sem, 0

    def at(self, value):
        self.n = value

    def link(self, ins):
        ins.then_inc(self.sem, 1)
        self.n = self.n + 1
        self.eng.wait_ge(self.sem, self.n)


def rsqrt_steps(dve, chain, var, eps, x, y, t):
    chain.link(dve.tensor_scalar(x, var, eps, None, ALU.add))
    chain.link(dve.tensor_scalar(t.bitcast(I32), x.bitcast(I32), 1, None, ALU.logical_shift_right))
    chain.link(dve.tensor_scalar(y.bitcast(I32), t.bitcast(I32), -1.0, float(0x5F3759DF), ALU.mult, ALU.add))
    for _ in range(3):
        chain.link(dve.tensor_tensor(t, y, y, ALU.mult))
        chain.link(dve.tensor_tensor(t, t, x, ALU.mult))
        chain.link(dve.tensor_scalar(t, t, -0.5, 1.5, ALU.mult, ALU.add))
        chain.link(dve.tensor_tensor(y, y, t, ALU.mult))


def numbered(i, per_turn, c):
    return per_turn * i + c, c % 4, (per_turn // 4) * i + c // 4


def after(eng, s, n):
    if not (isinstance(n, int) and n <= 0):
        eng.wait_ge(s, n)


def row_of(t, b):
    return t[:, ds(b, 1), :].rearrange("p o d -> p (o d)")


def bass_gps_layer(nc, x, src, dst, etype, basis, comp, loop_w, h_bias, gamma, beta,
                   Wq, Wk, Wv, Wm, W1m, W2m, g1, b1m, g2, b2m,
                   Wr, br, ln_g, ln_b, W1, b1, W2, b2, out):
    N, D = x.shape
    E = src.shape[0]
    NB = -(-N // P)
    NP = NB * P
    LAST = N - (NB - 1) * P
    KD = D // P
    NREL, NBASE = comp.shape
    HEADS = 8
    HD = D // HEADS
    NEX, HID = b1.shape
    KH = HID // P
    LN_EPS, ATT_EPS = 1e-5, 1e-6
    GT = 4
    GE = GT * P
    NG = -(-E // GE)
    GC = -(-NG // P)
    NGP = GC * P
    FULLC = (E // GE) // P
    LASTC_FULL = E // GE - FULLC * P
    LASTC_REST = E - (E // GE) * GE
    SLOTS = 4
    GA, GB2 = 2, 6
    A_TOT = NB * GA
    REST = NG - NB * (GA + GB2)
    PACK, FIELD_BITS = 4, 6
    FIELD = 1 << FIELD_BITS
    STEP_UNIT = 512
    assert NG < STEP_UNIT and NG * (NB - 1) * STEP_UNIT < 1 << 24
    assert NB <= FIELD and PACK * FIELD_BITS <= 24 and NG + PACK <= NGP + 1
    assert 2 * GA % SLOTS == 0 and 2 * GB2 % SLOTS == 0 and REST >= GB2
    MT = 256
    NT = (2 * N + NEX * MT) // MT + 1
    NT_LEAST = -(-2 * N // MT)
    MH = MT // P
    NH = NT * MH
    assert NH <= P

    h_table = nc.dram_tensor("h_table", (NP * NREL, D), F32).ap()
    base_dram = nc.dram_tensor("base_dram", (NB, P, D), F32).ap()
    xn_cols = nc.dram_tensor("xn_cols", (NB, P, D), F32).ap()
    token_rows = nc.dram_tensor("token_rows", (N, D), F32).ap()
    answers = nc.dram_tensor("answers", (NT * MT, D), F32).ap()

    with ExitStack() as ctx:
        def sb(name, shape, dt=F32):
            return ctx.enter_context(nc.sbuf_tensor(name, shape, dt))

        def sem(name):
            return ctx.enter_context(nc.semaphore(name))

        agg = sb("agg", [P, NB, D])
        xt_all = sb("xt_all", [P, NB, D])
        big = sb("big", [P, 10 * 1024])
        ring = sb("ring", [P, SLOTS, GT, D])
        w_rel = big[:, 0:4096].rearrange("p (k n) -> p k n", k=KD)
        wkv = big[:, 4096:5120].rearrange("p (k n) -> p k n", k=KD)
        wq = big[:, 5120:5632].rearrange("p (k n) -> p k n", k=KD)
        wm = big[:, 5632:6144].rearrange("p (k n) -> p k n", k=KD)
        w1m = big[:, 6144:8192].rearrange("p (k n) -> p k n", k=2 * KD)
        w2m = big[:, 8192:9216].rearrange("p (k n) -> p k n", k=2 * KD)
        wloop = big[:, 9216:9728].rearrange("p (k n) -> p k n", k=KD)
        compb = big[:, 9728:9728 + NREL * NBASE].rearrange("p (r b) -> p r b", r=NREL)
        tiles = big[:, 0:4096].rearrange("p (u n) -> p u n", n=P)
        kphi, kvd, ksd, msgT, m1T = (tiles[:, KD * i:KD * i + KD, :] for i in range(5))
        h1T = tiles[:, 10:10 + 2 * KD, :]
        kmin, kexp, den, h2n = (big[:, 1792 + D * i:1792 + D * i + D] for i in range(4))
        vb = big[:, 1792 + 4 * D:1792 + 4 * D + KD * (P + 2)].rearrange("p (k n) -> p k n", k=KD)
        onehot_x = [big[:, 3080:3080 + GT * P].rearrange("p (q n) -> p q n", q=GT)] + [
            sb(f"onehot_x{i}", [P, GT, P])[:, :, :] for i in range(1, SLOTS)]
        we1 = [big[:, 4096 * i:4096 * i + 2048].rearrange("p (k n) -> p k n", k=KD) for i in range(2)]
        we2 = [big[:, 4096 * i + 2048:4096 * i + 4096].rearrange("p (k n) -> p k n", k=KH) for i in range(2)]
        EP = KH + 2 * KD
        eparm = [big[:, 8192 + 1024 * i:8192 + 1024 * i + EP] for i in range(2)]
        eb2 = [big[:, 8192 + 1024 * i + 256:8192 + 1024 * i + 256 + D] for i in range(2)]
        stage = ring[:, :, :, :].rearrange("p s t d -> p (s t d)").rearrange("p (u n) -> p u n", u=2)
        basis_sb = stage[:, 0, 0:KD * NBASE * D].rearrange("p (k b d) -> p k b d", k=KD, b=NBASE)
        flat = xt_all[:, :, :].rearrange("p b d -> p (b d)")
        CW = GC * GE
        src_i = flat[:, 0:CW].bitcast(I32).rearrange("p (c e) -> p c e", c=GC)
        et_i = flat[:, CW:2 * CW].bitcast(I32).rearrange("p (c e) -> p c e", c=GC)
        dst_i = flat[:, 2 * CW:3 * CW].bitcast(I32).rearrange("p (c e) -> p c e", c=GC)
        row_f = flat[:, 3 * CW:4 * CW].rearrange("p (c e) -> p c e", c=GC)
        dst_f = flat[:, 4 * CW:5 * CW].rearrange("p (c e) -> p c e", c=GC)
        low_f = flat[:, 5 * CW:5 * CW + GE]
        dcol = sb("dcol", [P, NG, GT])
        icol = sb("icol", [P, NG, GT], I32)
        group_tab = sb("group_tab", [1, 3, NGP], I32)
        tab_f = flat[0:1, 5 * CW + GE:5 * CW + GE + 3 * NGP].rearrange("o (t g) -> o t g", t=3)
        words_f = flat[0:1, 0:2 * NGP].rearrange("o (t g) -> o t g", t=2)
        span = sb("span", [P, 8, GC])
        span_i = sb("span_i", [P, 2, GC], I32)

        ident = sb("ident", [P, P])
        upper = sb("upper", [P, P])
        ones = sb("ones", [P, P])
        zeros = sb("zeros", [P, D])
        heads = sb("heads", [P, P])
        iota_f = sb("iota_f", [P, P])
        valid = sb("valid", [P, NB])
        rows = sb("rows", [P, 6, D])
        hbias_b, gamma_b, beta_b, g2_b, ends_b = (rows[:, i, :] for i in range(5))
        wr_sb = rows[:, 5, 0:KD * NEX].rearrange("p (k e) -> p k e", k=KD)
        br_b = rows[:, 5, 64:64 + NEX]
        g1c = rows[:, 5, 80:80 + KD]
        b1c = rows[:, 5, 84:84 + KD]
        eps_c, three_halves_c = (rows[:, 5, 88 + i:89 + i] for i in range(2))
        stats = sb("stats", [P, NB, 6])
        mv = sb("mv", [P, NB, 2])
        rstd = sb("rstd", [P, 3, NB])
        norm_cols = sb("norm_cols", [P, 2, 8])
        idx_now = sb("idx_now", [P, 2, SLOTS, GT], I32)
        onehot = sb("onehot", [P, 4, GT, P])
        drel_x = sb("drel_x", [P, SLOTS, GT])
        xnb = sb("xnb", [P, 2, D])
        xTb = sb("xTb", [P, 2, KD, P])
        m1 = xnb[:, 1, :]
        mst = sb("mst", [P, 2, 12])
        base_rows = sb("base_rows", [P, 2, D])
        block_off = sb("block_off", [P, NB])

        bank = [ctx.enter_context(nc.psum_tensor(f"bank{i}", [P, 512], F32)) for i in range(8)]

        block = ctx.enter_context(nc.Block())

        x_in = [sem(f"x_in{i}") for i in range(7)]
        edges_in = sem("edges_in")
        basis_in = sem("basis_in")
        weights_in = sem("weights_in")
        small_in = sem("small_in")
        pads_set = sem("pads_set")
        consts_set = sem("consts_set")
        rel_ready = sem("rel_ready")
        dve_own = sem("dve_own")
        edge_rows_ready = sem("edge_rows_ready")
        edge_cols_up = sem("edge_cols_up")
        edge_cols_down = sem("edge_cols_down")
        tables_ready = sem("tables_ready")
        xn_ready = sem("xn_ready")
        xT_up = sem("xT_up")
        xT_ready = sem("xT_ready")
        xT_stored = [sem(f"xT_stored{i}") for i in range(2)]
        base_part = sem("base_part")
        base_ready = sem("base_ready")
        base_stored = [sem(f"base_stored{i}") for i in range(2)]
        table_up = sem("table_up")
        table_down_a = sem("table_down_a")
        table_down_d = sem("table_down_d")
        stage_stored = [sem(f"stage_stored{i}") for i in range(2)]
        kv_up = sem("kv_up")
        kmin_ready = sem("kmin_ready")
        kexp_ready = sem("kexp_ready")
        kphi_ready = sem("kphi_ready")
        v_ready = sem("v_ready")
        vones_ready = sem("vones_ready")
        agg_init = sem("agg_init")
        kv_used = sem("kv_used")
        kvd_ready = sem("kvd_ready")

        idx_ready = sem("idx_ready")
        slot_seen = sem("slot_seen")
        waits_passed = sem("waits_passed")
        rows_in = [sem(f"rows_in{i}") for i in range(SLOTS)]
        onehot_ready = sem("onehot_ready")
        sum_up = sem("sum_up")
        sum_down = sem("sum_down")
        near_onehot = sem("near_onehot")
        near_rel = sem("near_rel")
        far_onehot = sem("far_onehot")
        extra_up = sem("extra_up")
        extra_down = sem("extra_down")
        far_rel = sem("far_rel")
        cols_in = [sem(f"cols_in{i}") for i in range(2)]
        self_up = sem("self_up")
        self_added = sem("self_added")
        base_in = [sem(f"base_in{i}") for i in range(2)]
        mix_own = sem("mix_own")
        norm_own = [sem(f"norm_own{k}") for k in range(2)]
        q_up = sem("q_up")
        qmin_ready = sem("qmin_ready")
        qexp_ready = sem("qexp_ready")
        qphi_ready = sem("qphi_ready")
        nd_up = sem("nd_up")
        den_ready = sem("den_ready")
        msg_ready = sem("msg_ready")
        m_up = sem("m_up")
        m_stats = sem("m_stats")
        m1_ready = sem("m1_ready")
        m1T_up = sem("m1T_up")
        m1T_ready = sem("m1T_ready")
        f_up = sem("f_up")
        h1_ready = sem("h1_ready")
        h2_up = sem("h2_up")
        h2_stats = sem("h2_stats")
        h2n_ready = sem("h2n_ready")
        h2_scaled = sem("h2_scaled")
        mix_ready = sem("mix_ready")

        def pairs(eng, body):
            body(0, 0, 0)
            body(1, 1, 0)
            with eng.Fori(1, NB // 2) as i:
                body(2 * i, 0, i)
                body(2 * i + 1, 1, i)
            body(NB - 1, 0, NB // 2)

        def fours(eng, body):
            assert NB % 4 == 1
            for u in range(4):
                body(u, u, 0)
            with eng.Fori(1, NB // 4) as i:
                for u in range(4):
                    body(4 * i + u, u, i)
            body(NB - 1, 0, NB // 4)

        def is_number(b, n):
            return isinstance(b, int) and b == n

        def rows_in_block(b):
            return LAST if is_number(b, NB - 1) else P

        def at_a(b, u, i, j):
            return numbered(i, 2 * GA, u * GA + j)

        def at_b(b, u, i, j):
            return numbered(i, 2 * GB2, A_TOT + u * GB2 + j)

        def row_dram(t, b):
            return t[ds(b, 1), :, :].rearrange("o p d -> (o p) d")

        def sp_program(sp):
            for k in range(KD):
                sp.dma_start(basis_sb[:, k, :, :], basis[:, k * P:(k + 1) * P, :].rearrange("b p o -> p b o")).then_inc(basis_in, 16)
            sp.dma_start(compb, comp.rearrange("r b -> (r b)").partition_broadcast(P)
                         .rearrange("p (r b) -> p r b", r=NREL)).then_inc(basis_in, 16)
            for i in range(6):
                sp.dma_start(agg[:, 8 * i:8 * i + 8, :],
                             x[1024 * i:1024 * i + 1024, :].rearrange("(b p) d -> p b d", p=P)).then_inc(x_in[i], 16)
            sp.wait_ge(pads_set, 4)
            sp.dma_start(agg[0:LAST, NB - 1, :], x[(NB - 1) * P:N, :]).then_inc(x_in[6], 16)
            sp.dma_start(wloop, loop_w.rearrange("(k p) o -> p k o", p=P)).then_inc(weights_in, 16)
            sp.dma_start(wkv[:, :, 0:D], Wk.rearrange("(k p) o -> p k o", p=P)).then_inc(weights_in, 16)
            sp.dma_start(wkv[:, :, D:2 * D], Wv.rearrange("(k p) o -> p k o", p=P)).then_inc(weights_in, 16)
            sp.dma_start(wq, Wq.rearrange("(k p) o -> p k o", p=P)).then_inc(weights_in, 16)
            sp.dma_start(wm, Wm.rearrange("(k p) o -> p k o", p=P)).then_inc(weights_in, 16)
            sp.dma_start(w1m, W1m.rearrange("(k p) o -> p k o", p=P)).then_inc(weights_in, 16)
            sp.dma_start(w2m, W2m.rearrange("(k p) o -> p k o", p=P)).then_inc(weights_in, 16)
            for row, vec in ((hbias_b, h_bias), (gamma_b, gamma), (beta_b, beta), (g2_b, g2), (ends_b, b2m), (br_b, br)):
                sp.dma_start(row, vec.partition_broadcast(P)).then_inc(small_in, 16)
            sp.dma_start(wr_sb, Wr.rearrange("(k p) e -> p k e", p=P)).then_inc(small_in, 16)
            sp.dma_start(g1c, g1.rearrange("(k p) -> p k", p=P), allow_slow_non_contiguous=True).then_inc(small_in, 16)
            sp.dma_start(b1c, b1m.rearrange("(k p) -> p k", p=P), allow_slow_non_contiguous=True).then_inc(small_in, 16)
            def store_block(b, u, i):
                sp.wait_ge(base_ready, b + 1)
                sp.dma_start(row_dram(base_dram, b), base_rows[:, u, :]).then_inc(base_stored[u], 16)
                sp.wait_ge(xT_ready, b + 1)
                sp.dma_start(row_dram(xn_cols, b), xTb[:, u, :, :].rearrange("p k n -> p (k n)")).then_inc(xT_stored[u], 16)
                sp.wait_ge(table_down_a, 2 * b + 2)
                sp.wait_ge(table_down_d, 2 * b + 2)
                sp.dma_start(h_table[ds(b * (P * NREL), P * NREL), :].rearrange("(p r) d -> p (r d)", r=NREL),
                             stage[:, u, :]).then_inc(stage_stored[u], 16)
            store_block(0, 0, 0)
            store_block(1, 1, 0)
            with sp.Fori(1, NB // 2) as i:
                store_block(2 * i, 0, i)
                store_block(2 * i + 1, 1, i)
            store_block(NB - 1, 0, NB // 2)
            sp_mix(sp)
            sp_tail(sp)

        def pool_program(pool):
            pool.memset(agg[:, NB - 1, :], 0.0).then_inc(pads_set, 1)
            for t in (src_i, et_i):
                pool.memset(t[:, GC - 1, :], 0).then_inc(pads_set, 1)
            pool.memset(dst_i[:, GC - 1, :], -1).then_inc(pads_set, 1)
            pool.memset(ident[:, :], 0.0).then_inc(consts_set, 1)
            pool.memset(ones[:, :], 1.0).then_inc(consts_set, 1)
            pool.memset(zeros[:, :], 0.0).then_inc(consts_set, 1)
            pool.memset(eps_c, ATT_EPS).then_inc(consts_set, 1)
            pool.iota(iota_f[:, :], [[1, P]], base=0, channel_multiplier=0,
                      allow_small_or_imprecise_dtypes=True).then_inc(consts_set, 1)
            pool.iota(block_off[:, :], [[P, NB]], base=0, channel_multiplier=0,
                      allow_small_or_imprecise_dtypes=True).then_inc(consts_set, 1)
            pool.wait_ge(consts_set, 6)
            pool.affine_select(out=ident[:, :], in_=ident[:, :], pattern=[[-1, P]], compare_op=ALU.not_equal,
                               fill=1.0, base=0, channel_multiplier=1).then_inc(consts_set, 1)
            pool.affine_select(out=upper[:, :], in_=ones[:, :], pattern=[[1, P]], compare_op=ALU.is_gt,
                               fill=0.0, base=0, channel_multiplier=-1).then_inc(consts_set, 1)
            pool.affine_select(out=heads[:, :], in_=ones[:, :], pattern=[[-HD, P // HD], [0, HD]], compare_op=ALU.is_ge,
                               fill=0.0, base=0, channel_multiplier=1).then_inc(consts_set, 1)
            pool.affine_select(out=valid[:, :], in_=ones[:, 0:NB], pattern=[[-P, NB]], compare_op=ALU.is_ge,
                               fill=0.0, base=N - 1, channel_multiplier=-1).then_inc(consts_set, 1)
            pool.wait_ge(consts_set, 10)
            pool.affine_select(out=heads[:, :], in_=heads[:, :], pattern=[[HD, P // HD], [0, HD]], compare_op=ALU.is_ge,
                               fill=0.0, base=HD - 1, channel_multiplier=-1).then_inc(consts_set, 1)
            for t, a in ((src_i, src), (et_i, etype), (dst_i, dst)):
                full = FULLC * P * GE
                pool.dma_start(t[:, 0:FULLC, :], a[0:full].rearrange("(c p e) -> p c e", p=P, e=GE)).then_inc(edges_in, 16)
                pool.wait_ge(pads_set, 4)
                more = full + LASTC_FULL * GE
                pool.dma_start(t[0:LASTC_FULL, GC - 1, :], a[full:more].rearrange("(p e) -> p e", e=GE)).then_inc(edges_in, 16)
                pool.dma_start(t[LASTC_FULL:LASTC_FULL + 1, GC - 1, 0:LASTC_REST],
                               a[more:E].rearrange("(p e) -> p e", p=1)).then_inc(edges_in, 16)
            gather_rows(pool)
            pool_tail(pool)

        def gather_rows(pool):
            pool.wait_ge(stage_stored[0], 16 * ((NB + 1) // 2))
            pool.wait_ge(stage_stored[1], 16 * (NB // 2))
            pool.wait_ge(tables_ready, 1)

            def turn(g0, w, half, k):
                pool.tensor_copy(idx_now[:, half, 0:k, :], icol[:, ds(g0, k), :]).then_inc(idx_ready, 1)
                pool.wait_ge(idx_ready, w + 1)
                pool.sem_inc(slot_seen, 1)
                for s in range(k):
                    if not (isinstance(g0, int) and g0 < SLOTS):
                        pool.wait_ge(sum_up, g0 + s - SLOTS + 1)
                        pool.sem_inc(slot_seen, 1)
                    for q in range(GT):
                        pool.indirect_dma_start(
                            out=ring[:, s, q, :], out_offset=None, in_=h_table,
                            in_offset=bass.IndirectOffsetOnAxis(ap=idx_now[:, half, s, q:q + 1], axis=0),
                        ).then_inc(rows_in[s], 16)

            turns = NG // SLOTS
            turn(0, 0, 0, SLOTS)
            turn(SLOTS, 1, 1, SLOTS)
            with pool.Fori(1, turns // 2) as i:
                turn(i * (2 * SLOTS), 2 * i, 0, SLOTS)
                turn(i * (2 * SLOTS) + SLOTS, 2 * i + 1, 1, SLOTS)
            assert turns % 2 == 0
            turn(turns * SLOTS, turns, 0, NG % SLOTS)

        def sp_mix(sp):
            for u in range(2):
                n = 16 * ((NB + 1 - u) // 2)
                sp.wait_ge(xT_stored[u], n)
                sp.wait_ge(base_stored[u], n)
            sp.wait_ge(table_up, 4 * NB)
            sp.wait_ge(agg_init, NB)

            def columns(b, u):
                sp.dma_start(xTb[:, u, :, :].rearrange("p k n -> p (k n)"), row_dram(xn_cols, b)).then_inc(cols_in[u], 16)

            def keys(b, u, i):
                after(sp, self_up, b - 1)
                columns(b, u)
            pairs(sp, keys)
            sp.wait_ge(self_up, NB)

            def queries(b, u, i):
                after(sp, f_up, b - 1)
                columns(b, u)
                after(sp, mix_ready, b - 1)
                sp.dma_start(base_rows[:, u, :], row_dram(base_dram, b)).then_inc(base_in[u], 16)
            pairs(sp, queries)

        H_BANKS, T_BANK, A_BANKS = (0, 1, 2, 3), 4, (6, 7)
        KEY_BANK, SELF_BANK, SUM_BANKS = 0, 1, (2, 3)
        EDGE_BANKS, TAB_BANKS = (5, 6), (7, 5)
        Q_BANK, ND_BANK, F_BANK, MT_BANK, G_BANK = 0, 1, 2, 3, 7
        S_BANKS, X_BANK = (4, 5), 6
        psT = bank[T_BANK][:, 0:D]

        def pe_tables(pe):
            pe.wait_ge(edge_rows_ready, 1)
            n = 0
            for c in range(GC):
                for a in (dst_f, row_f):
                    if n >= 2:
                        pe.wait_ge(edge_cols_down, n - 1)
                    for q in range(GT):
                        m = pe.transpose(bank[EDGE_BANKS[n % 2]][:, q * P:(q + 1) * P], a[:, c, q * P:(q + 1) * P],
                                         ident[:, :])
                    m.then_inc(edge_cols_up, 1)
                    n += 1
            pe.wait_ge(edge_cols_down, n - 1)
            for j in range(2):
                for c in range(GC):
                    m = pe.matmul(bank[TAB_BANKS[j]][0:1, c * P:(c + 1) * P], span[:, 4 + j, c:c + 1], ident[:, :],
                                  start=True, stop=True)
            m.then_inc(edge_cols_up, 1)

        def pe_columns(pe, b, u):
            pe.wait_ge(xn_ready, b + 1)
            after(pe, xT_ready, b)
            for k in range(KD):
                m = pe.transpose(psT[:, k * P:(k + 1) * P], xnb[:, u, k * P:(k + 1) * P], ident[:, :])
            m.then_inc(xT_up, 1)

        def pe_table(pe, b, u):
            pe.wait_ge(xT_ready, b + 1)
            for j in range(4):
                after(pe, table_down_d if j % 2 else table_down_a, 2 * (b - 1) + j // 2 + 1)
                for k in range(KD):
                    m = pe.matmul(bank[H_BANKS[j]][:, :], xTb[:, u, k, :], w_rel[:, k, 512 * j:512 * j + 512],
                                  start=k == 0, stop=k == KD - 1)
                m.then_inc(table_up, 1)

        def steps_before(eng, g):
            word = eng.value_load(group_tab[0:1, 2, ds(g, 1)], min_val=0, max_val=(1 << 24) - 1)
            far = (word >> (STEP_UNIT.bit_length() - 1)).with_bounds(min_val=0, max_val=NG * NB)
            near = (word & (STEP_UNIT - 1)).with_bounds(min_val=0, max_val=NG)
            return far + near, near, far

        def pe_extra(pe, g, s, more):
            def products():
                for q in range(GT):
                    m = pe.matmul(bank[X_BANK][:, 0:D], onehot_x[s][:, q, :], ring[:, s, q, :],
                                  start=q == 0, stop=q == GT - 1)
                m.then_inc(extra_up, 1)

            with pe.If(more > 0):
                steps, near, far = steps_before(pe, g)
                pe.wait_ge(near_onehot, near + 1)
                pe.wait_ge(extra_down, steps + 1)
                products()
                with pe.If(more > 1):
                    with pe.Fori(2, more + 1) as k:
                        pe.wait_ge(far_onehot, far + (k - 1))
                        pe.wait_ge(extra_down, steps + k)
                        products()

        def group_numbers(eng, row):
            word = [None, 0]

            def get(item, key):
                if word[0] is None or key >= word[1] + PACK:
                    word[0] = eng.value_load(group_tab[0:1, row, ds(item[0], 1)], min_val=0, max_val=FIELD ** PACK - 1)
                    word[1] = key
                field = (word[0] >> (FIELD_BITS * (key - word[1]))) & (FIELD - 1)
                return field.with_bounds(min_val=0, max_val=NB - 1)
            return get

        def pe_group(pe, item, more):
            g, s, use = item
            pe.wait_ge(rows_in[s], 16 * GT * (use + 1))
            pe_extra(pe, g, s, more)
            pe.wait_ge(onehot_ready, g + 1)
            after(pe, sum_down, g - 1)
            for q in range(GT):
                m = pe.matmul(bank[S_BANKS[s % 2]][:, 0:D], onehot[:, s, q, :], ring[:, s, q, :],
                              start=q == 0, stop=q == GT - 1)
            m.then_inc(sum_up, 1)

        def pe_mix(pe):
            pe.wait_ge(table_down_a, 2 * NB)
            pe.wait_ge(table_down_d, 2 * NB)
            pe.wait_ge(weights_in, 16 * 7)
            pe.wait_ge(tables_ready, 1)
            for h in range(KD):
                pe.matmul(bank[SUM_BANKS[h]][:, 0:P + 2], zeros[:, 0:P], zeros[:, 0:P + 2], start=True, stop=False,
                          skip_group_check=True)

            def keys(b, u, i):
                counts = group_numbers(pe, 1)
                def group(j):
                    item = at_a(b, u, i, j)
                    pe_group(pe, item, counts(item, j))
                pe.wait_ge(cols_in[u], 16 * (i + 1))
                after(pe, kphi_ready, b)
                after(pe, v_ready, b)
                for k in range(KD):
                    m = pe.matmul(bank[KEY_BANK][:, :], xTb[:, u, k, :], wkv[:, k, :], start=k == 0, stop=k == KD - 1)
                m.then_inc(kv_up, 1)
                after(pe, self_added, b)
                for k in range(KD):
                    m = pe.matmul(bank[SELF_BANK][:, 0:D], xTb[:, u, k, :], wloop[:, k, :], start=k == 0, stop=k == KD - 1)
                m.then_inc(self_up, 1)
                group(0)
                pe.wait_ge(kphi_ready, b + 1)
                pe.wait_ge(v_ready, b + 1)
                pe.wait_ge(vones_ready, b + 1)
                for h in range(KD):
                    m = pe.matmul(bank[SUM_BANKS[h]][:, 0:P + 2], kphi[:, h, :], vb[:, h, :], start=False, stop=False,
                                  skip_group_check=True)
                m.then_inc(kv_used, 1)
                group(1)
            pairs(pe, keys)
            for h in range(KD):
                m = pe.matmul(bank[SUM_BANKS[h]][:, 0:P + 2], zeros[:, 0:P], zeros[:, 0:P + 2], start=False, stop=True,
                              skip_group_check=True)
            m.then_inc(kv_used, 1)
            pe.wait_ge(kvd_ready, 2 * KD)
            pe.wait_ge(self_added, NB)

            psQ, psM = bank[Q_BANK][:, 0:D], bank[ND_BANK][:, 0:D]
            psT2, psG = bank[MT_BANK][:, 0:D], bank[G_BANK][:, 0:D]

            def queries(b, u, i):
                counts = group_numbers(pe, 1)
                this, last = not is_number(b, NB), not is_number(b, 0)

                def group(j):
                    item = at_b(b, u, i, j)
                    pe_group(pe, item, counts(item, j))
                group(0)
                if this:
                    pe.wait_ge(cols_in[u], 16 * ((NB + 1 - u) // 2) + 16 * (i + 1))
                    for o in range(KD):
                        for k in range(KD):
                            m = pe.matmul(psQ[:, o * P:(o + 1) * P], wq[:, k, o * P:(o + 1) * P], xTb[:, u, k, :],
                                          start=k == 0, stop=k == KD - 1)
                    m.then_inc(q_up, 1)
                group(1)
                group(2)
                if last:
                    pe.wait_ge(m1_ready, b)
                    after(pe, m1T_ready, b - 1)
                    for k in range(KD):
                        m = pe.transpose(psT2[:, k * P:(k + 1) * P], m1[:, k * P:(k + 1) * P], ident[:, :])
                    m.then_inc(m1T_up, 1)
                if this:
                    pe.wait_ge(qphi_ready, b + 1)
                    after(pe, m1_ready, b)
                    for o in range(KD):
                        pe.matmul(bank[ND_BANK][:, D + o * P:D + (o + 1) * P], ksd[:, o, :], kphi[:, o, :],
                                  start=True, stop=True)
                    for o in range(KD):
                        m = pe.matmul(bank[ND_BANK][:, o * P:(o + 1) * P], kvd[:, o, :], kphi[:, o, :],
                                      start=True, stop=True)
                    m.then_inc(nd_up, 1)
                group(3)
                if last:
                    pe.wait_ge(m1T_ready, b)
                    after(pe, h1_ready, b - 1)
                    for o in range(2 * KD):
                        for k in range(2 * KD):
                            m = pe.matmul(bank[F_BANK][:, o * P:(o + 1) * P], w1m[:, k, o * P:(o + 1) * P],
                                          xTb[:, 1 - u, k, :] if k < KD else m1T[:, k - KD, :],
                                          start=k == 0, stop=k == 2 * KD - 1)
                    m.then_inc(f_up, 1)
                group(4)
                group(5)
                if last:
                    pe.wait_ge(h1_ready, b)
                    after(pe, h2n_ready, b - 1)
                    for k in range(2 * KD):
                        m = pe.matmul(psG, h1T[:, k, :], w2m[:, k, :], start=k == 0, stop=k == 2 * KD - 1)
                    m.then_inc(h2_up, 1)
                if this:
                    pe.wait_ge(msg_ready, b + 1)
                    for k in range(KD):
                        m = pe.matmul(psM, msgT[:, k, :], wm[:, k, :], start=k == 0, stop=k == KD - 1)
                    m.then_inc(m_up, 1)
            pairs(pe, queries)
            queries(NB, 1, NB // 2)
            counts = group_numbers(pe, 1)
            for j in range(GB2, REST):
                item = at_b(NB, 1, NB // 2, j)
                pe_group(pe, item, counts(item, j))

        def pe_program(pe):
            pe.wait_ge(consts_set, 11)
            pe.wait_ge(rel_ready, 1)
            pe_columns(pe, 0, 0)

            def block_of(b, u, i):
                if is_number(b, NB - 1):
                    pe_tables(pe)
                else:
                    pe_columns(pe, b + 1, 1 - u)
                pe_table(pe, b, u)
            pairs(pe, block_of)
            pe_mix(pe)
            pe_tail(pe)

        def act_columns(act, b, u, i):
            act.wait_ge(xT_up, b + 1)
            after(act, table_up, 4 * (b - 1))
            after(act, xT_stored[u], 16 * i)
            act.copy(xTb[:, u, :, :].rearrange("p k n -> p (k n)"), psT).then_inc(xT_ready, 1)

        def act_table(act, b, u, i):
            after(act, stage_stored[u], 16 * i)
            for j in (0, 2):
                act.wait_ge(table_up, 4 * b + j + 1)
                act.copy(stage[:, u, 512 * j:512 * j + 512], bank[H_BANKS[j]][:, :]).then_inc(table_down_a, 1)

        def act_program(act):
            act.wait_ge(consts_set, 11)
            act.wait_ge(rel_ready, 1)
            act_columns(act, 0, 0, 0)

            def block_of(b, u, i):
                if not is_number(b, NB - 1):
                    act_columns(act, b + 1, 1 - u, i + u)
                act_table(act, b, u, i)
            pairs(act, block_of)
            act_mix(act)
            act_tail(act)

        def act_norm(act, n, out, ps, k, done):
            ch = Chain(act, norm_own[k])
            ch.at(n * NORM_LINKS)
            half, minus, guess = (mst[:, k, n:n + 1] for n in (9, 10, 11))
            square, factor, root, shift = (norm_cols[:, k, n:n + 1] for n in range(4))
            for last in (guess, root, root):
                ch.link(act.activation(square, last, ACT.Square))
                ch.link(act.activation(factor, square, ACT.Identity, scale=half, bias=three_halves_c))
                ch.link(act.activation(root, last, ACT.Copy, scale=factor))
            ch.link(act.activation(shift, minus, ACT.Copy, scale=root))
            act.activation(out, ps, ACT.Identity, scale=root, bias=shift).then_inc(done, 1)
        NORM_LINKS = 10

        def act_mix(act):
            def keys(b, u, i):
                act.wait_ge(kmin_ready, b + 1)
                after(act, kphi_ready, b)
                act.activation(kexp[:, :], kmin[:, :], ACT.Exp).then_inc(kexp_ready, 1)
                act.wait_ge(kv_up, b + 1)
                after(act, kv_used, b)
                act.activation(vb[:, :, 0:P], bank[KEY_BANK][:, D:2 * D].rearrange("p (k n) -> p k n", k=KD),
                               ACT.Copy, scale=valid[:, ds(b, 1)]).then_inc(v_ready, 1)
            pairs(act, keys)

            def second_norm(b):
                act.wait_ge(h2_stats, b - 1)
                after(act, mix_ready, b - 2)
                act_norm(act, b - 2, h2n[:, :], bank[G_BANK][:, 0:D], 1, h2n_ready)

            def queries(b, u, i):
                this, last = not is_number(b, NB), not is_number(b, 0)
                if last:
                    act.wait_ge(m_stats, b)
                    after(act, m1T_up, b - 1)
                    act_norm(act, b - 1, m1, bank[ND_BANK][:, 0:D], 0, m1_ready)
                if this:
                    act.wait_ge(qmin_ready, b + 1)
                    act.activation(kexp[:, :], kmin[:, :], ACT.Exp).then_inc(qexp_ready, 1)
                if not (isinstance(b, int) and b < 2):
                    second_norm(b)
                if this:
                    act.wait_ge(nd_up, b + 1)
                    after(act, msg_ready, b)
                    act.activation(den[:, :], bank[ND_BANK][:, D:2 * D], ACT.Identity, bias=eps_c).then_inc(den_ready, 1)
                if last:
                    act.wait_ge(f_up, b)
                    after(act, h2_up, b - 1)
                    act.activation(h1T[:, :, :].rearrange("p k n -> p (k n)"), bank[F_BANK][:, :], ACT.Relu).then_inc(h1_ready, 1)
            pairs(act, queries)
            queries(NB, 1, NB // 2)
            second_norm(NB + 1)

        def one_hot(dve, out, columns, done):
            dve.tensor_tensor(out, columns.unsqueeze(2).to_broadcast([P, GT, P]),
                              iota_f[:, :].unsqueeze(1).to_broadcast([P, GT, P]), ALU.is_equal).then_inc(done, 1)

        def dve_onehot(dve, item):
            g, s, _ = item
            after(dve, sum_up, g - 3)
            one_hot(dve, onehot[:, s, :, :], dcol[:, ds(g, 1), :].rearrange("p o t -> p (o t)"), onehot_ready)

        def dve_near_onehot(dve, item, more):
            g, s, _ = item
            with dve.If(more > 0):
                _, near, _ = steps_before(dve, g)
                dve.tensor_scalar(drel_x[:, s, :], dcol[:, ds(g, 1), :].rearrange("p o t -> p (o t)"),
                                  float(P), None, ALU.subtract).then_inc(near_rel, 1)
                dve.wait_ge(near_rel, near + 1)
                one_hot(dve, onehot_x[s], drel_x[:, s, :], near_onehot)

        def dve_extra_add(dve, at, step):
            dve.wait_ge(extra_up, step)
            at = row_of(agg, at.with_bounds(min_val=0, max_val=NB - 1))
            dve.tensor_tensor(at, at, bank[X_BANK][:, 0:D], ALU.add).then_inc(extra_down, 1)
            dve.wait_ge(extra_down, step + 1)
            dve.sem_inc(waits_passed, 1)

        def dve_extra(dve, item, more, first):
            g, s, _ = item
            with dve.If(more > 0):
                steps, _, far = steps_before(dve, g)
                after(dve, sum_down, g)
                dve_extra_add(dve, first + 1, steps + 1)
                with dve.If(more > 1):
                    with dve.Fori(2, more + 1) as k:
                        dve.tensor_scalar(drel_x[:, s, :], dcol[:, ds(g, 1), :].rearrange("p o t -> p (o t)"),
                                          block_off[:, ds(k, 1)], None, ALU.subtract).then_inc(far_rel, 1)
                        dve.wait_ge(far_rel, far + (k - 1))
                        one_hot(dve, onehot_x[s], drel_x[:, s, :], far_onehot)
                        dve_extra_add(dve, first + k, steps + k)

        def dve_sum(dve, g, s, first):
            dve.wait_ge(sum_up, g + 1)
            after(dve, sum_down, g)
            dve.tensor_tensor(row_of(agg, first), row_of(agg, first), bank[S_BANKS[s % 2]][:, 0:D], ALU.add).then_inc(sum_down, 1)

        LEAD = 3

        def dve_groups(dve, place):
            counts, counts_ahead = group_numbers(dve, 1), group_numbers(dve, 1)
            firsts = group_numbers(dve, 0)

            held = {}

            def step(j):
                item = place(j)
                g, s, _ = item
                begin = is_number(g, 0)
                if begin:
                    for a in range(LEAD):
                        dve_onehot(dve, place(a))
                        held[j + a] = counts(place(a), j + a)
                        dve_near_onehot(dve, place(a), held[j + a])
                low = None if begin else firsts(place(j - 1), j - 1)
                first = firsts(item, j)
                more = held[j] if j in held else counts(item, j)
                if not (isinstance(g, int) and g + LEAD >= NG):
                    ahead = place(j + LEAD)
                    dve_onehot(dve, ahead)
                    held[j + LEAD] = counts_ahead(ahead, j + LEAD)
                    dve_near_onehot(dve, ahead, held[j + LEAD])
                if not begin:
                    dve_sum(dve, g - 1, (s - 1) % 4, low)
                dve_extra(dve, item, more, first)
            return step

        def norm_stats(dve, ch, ps, k, done):
            mean, var, x, half, minus, root = (mst[:, k, 6 + n:7 + n] for n in range(6))
            ch.link(dve.bn_stats(mst[:, k, 0:6], ps))
            dve.sem_inc(waits_passed, 1)
            ch.link(dve.bn_aggr(mst[:, k, 6:8], mst[:, k, 0:6]))
            ch.link(dve.tensor_scalar(x, var, LN_EPS, None, ALU.add))
            ch.link(dve.tensor_scalar(root.bitcast(I32), x.bitcast(I32), 1, None, ALU.logical_shift_right))
            ch.link(dve.tensor_scalar(half, x, -0.5, None, ALU.mult))
            ch.link(dve.tensor_scalar(minus, mean, -1.0, None, ALU.mult))
            dve.tensor_scalar(root.bitcast(I32), root.bitcast(I32), -1.0, float(0x5F3759DF), ALU.mult, ALU.add).then_inc(done, 1)

        def dve_mix(dve):
            ch = Chain(dve, mix_own)
            dve.sem_inc(extra_down, 1)

            def keys(b, u, i):
                step = dve_groups(dve, lambda j: at_a(b, u, i, j))
                k = bank[KEY_BANK][:, 0:D]
                dve.wait_ge(kv_up, b + 1)
                dve.tensor_scalar(kmin[:, :], k, 0.0, None, ALU.min).then_inc(kmin_ready, 1)
                after(dve, kv_used, b)
                dve.tensor_copy(vb[:, :, P:P + 2], valid[:, ds(b, 1)].unsqueeze(2).to_broadcast([P, KD, 2])).then_inc(vones_ready, 1)
                dve.wait_ge(kexp_ready, b + 1)
                dve.wait_ge(v_ready, b + 1)
                dve.scalar_tensor_tensor(kphi[:, :, :].rearrange("p k n -> p (k n)"), k, 0.0, kexp[:, :],
                                         ALU.max, ALU.add).then_inc(kphi_ready, 1)
                step(0)
                dve.wait_ge(self_up, b + 1)
                after(dve, sum_down, at_a(b, u, i, 0)[0])
                dve.tensor_tensor(row_of(agg, b), row_of(agg, b), bank[SELF_BANK][:, 0:D], ALU.add).then_inc(self_added, 1)
                dve.wait_ge(self_added, b + 1)
                dve.sem_inc(waits_passed, 1)
                step(1)
            pairs(dve, keys)
            dve.wait_ge(kv_used, NB + 1)
            for h in range(KD):
                dve.tensor_tensor(kvd[:, h, :], heads[:, :], bank[SUM_BANKS[h]][:, 0:P], ALU.mult).then_inc(kvd_ready, 1)
                dve.tensor_scalar(ksd[:, h, :], heads[:, :], bank[SUM_BANKS[h]][:, P:P + 1], None, ALU.mult).then_inc(kvd_ready, 1)

            def finish(b, u, i):
                dve.wait_ge(h2n_ready, b - 1)
                dve.tensor_tensor(h2n[:, :], h2n[:, :], g2_b, ALU.mult).then_inc(h2_scaled, 1)
                dve.wait_ge(base_in[u], 16 * i)
                dve.wait_ge(h2_scaled, b - 1)
                dve.tensor_tensor(row_of(xt_all, b - 2), h2n[:, :], base_rows[:, u, :], ALU.add).then_inc(mix_ready, 1)

            def queries(b, u, i):
                this, last = not is_number(b, NB), not is_number(b, 0)
                step = dve_groups(dve, lambda j: at_b(b, u, i, j))
                step(0)
                if last:
                    dve.wait_ge(m_up, b)
                    after(dve, m1_ready, b - 1)
                    norm_stats(dve, ch, bank[ND_BANK][:, 0:D], 0, m_stats)
                q = bank[Q_BANK][:, 0:D]
                if this:
                    dve.wait_ge(q_up, b + 1)
                    dve.tensor_scalar(kmin[:, :], q, 0.0, None, ALU.min).then_inc(qmin_ready, 1)
                step(1)
                if this:
                    dve.wait_ge(qexp_ready, b + 1)
                    dve.scalar_tensor_tensor(kphi[:, :, :].rearrange("p k n -> p (k n)"), q, 0.0, kexp[:, :],
                                             ALU.max, ALU.add).then_inc(qphi_ready, 1)
                step(2)
                if last:
                    dve.wait_ge(m1T_up, b)
                    for k in range(KD):
                        m = dve.tensor_scalar(m1T[:, k, :], bank[MT_BANK][:, k * P:(k + 1) * P], g1c[:, k:k + 1],
                                              b1c[:, k:k + 1], ALU.mult, ALU.add)
                    m.then_inc(m1T_ready, 1)
                if not (isinstance(b, int) and b < 2):
                    finish(b, u, i)
                step(3)
                step(4)
                if this:
                    dve.wait_ge(den_ready, b + 1)
                    ch.link(dve.reciprocal(den[:, :], den[:, :]))
                    dve.tensor_tensor(msgT[:, :, :].rearrange("p k n -> p (k n)"), bank[ND_BANK][:, 0:D], den[:, :],
                                      ALU.mult).then_inc(msg_ready, 1)
                step(5)
                if last:
                    dve.wait_ge(h2_up, b)
                    after(dve, h2n_ready, b - 1)
                    norm_stats(dve, ch, bank[G_BANK][:, 0:D], 1, h2_stats)
            queries(0, 0, 0)
            first_turn = ch.n
            queries(1, 1, 0)
            a_turn = ch.n - first_turn
            with dve.Fori(1, NB // 2) as i:
                for u in range(2):
                    ch.at(first_turn + (2 * i + u - 1) * a_turn)
                    queries(2 * i + u, u, i)
            ch.at(first_turn + (NB - 2) * a_turn)
            queries(NB - 1, 0, NB // 2)
            queries(NB, 1, NB // 2)
            finish(NB + 1, 0, NB // 2 + 1)
            step = dve_groups(dve, lambda j: at_b(NB, 1, NB // 2, j))
            for j in range(GB2, REST):
                step(j)
            last_first = group_numbers(dve, 0)((NG - 1,), 0)
            dve_sum(dve, NG - 1, (NG - 1) % 4, last_first)

        def mean_and_variance(dve, ch):
            mean, var, t = mv[:, :, 0], mv[:, :, 1], rstd[:, 2, :]
            ch.link(dve.tensor_tensor(t, stats[:, :, 1], stats[:, :, 4], ALU.subtract))
            ch.link(dve.tensor_scalar(t, t, 0.5, None, ALU.mult))
            ch.link(dve.tensor_tensor(t, t, t, ALU.mult))
            ch.link(dve.tensor_tensor(var, stats[:, :, 2], stats[:, :, 5], ALU.add))
            ch.link(dve.scalar_tensor_tensor(var, var, 1.0 / D, t, ALU.mult, ALU.add))
            ch.link(dve.tensor_tensor(mean, stats[:, :, 1], stats[:, :, 4], ALU.add))
            ch.link(dve.tensor_scalar(mean, mean, 0.5, None, ALU.mult))

        def dve_setup(dve, ch):
            ch.link(dve.memset(three_halves_c, 1.5))
            dve.wait_ge(basis_in, 16 * (KD + 1))
            for r in range(NREL):
                o = w_rel[:, :, D * r:D * r + D]
                ch.link(dve.tensor_scalar(o, basis_sb[:, :, 0, :], compb[:, r, 0:1], None, ALU.mult))
                for i in range(1, NBASE):
                    ch.link(dve.scalar_tensor_tensor(o, basis_sb[:, :, i, :], compb[:, r, i:i + 1], o, ALU.mult, ALU.add))
            for i in range(7):
                dve.wait_ge(x_in[i], 16)
                for b in range(8 * i, min(8 * i + 8, NB)):
                    m = dve.bn_stats(stats[:, b, :], agg[:, b, :])
                    m.then_inc(dve_own, 1)
                    ch.n += 1
            dve.wait_ge(dve_own, ch.n)
            mean_and_variance(dve, ch)
            rsqrt_steps(dve, ch, mv[:, :, 1], LN_EPS, rstd[:, 1, :], rstd[:, 0, :], rstd[:, 2, :])

        def dve_edge_rows(dve, ch):
            dve.wait_ge(edges_in, 16 * 9)
            dve.scalar_tensor_tensor(row_f, src_i, float(NREL), et_i, ALU.mult, ALU.add).then_inc(dve_own, 1)
            ch.n += 1
            ch.link(dve.tensor_copy(dst_f, dst_i))
            ch.link(dve.tensor_scalar(low_f, dst_f[:, GC - 1, :], 0.0, 1e6, ALU.is_lt, ALU.mult))
            ch.link(dve.tensor_tensor(low_f, low_f, dst_f[:, GC - 1, :], ALU.add))
            ch.link(dve.tensor_reduce(span[:, 0, 0:GC - 1], dst_f[:, 0:GC - 1, :], AX.X, ALU.min))
            ch.link(dve.tensor_reduce(span[:, 0, GC - 1:GC], low_f, AX.X, ALU.min))
            ch.link(dve.tensor_reduce(span[:, 1, :], dst_f, AX.X, ALU.max))
            ch.link(dve.tensor_copy(span_i[:, :, :], span[:, 0:2, :]))
            ch.link(dve.tensor_scalar(span_i[:, :, :], span_i[:, :, :], 7, None, ALU.arith_shift_right))
            ch.link(dve.tensor_copy(span[:, 2:4, :], span_i[:, :, :]))
            ch.link(dve.tensor_copy(span[:, 4, :], span[:, 2, :]))
            ch.link(dve.tensor_tensor(span[:, 5, :], span[:, 3, :], span[:, 2, :], ALU.subtract))
            ch.link(dve.tensor_scalar(span[:, 6, :], span[:, 2, :], float(P), None, ALU.mult))
            for c in range(GC):
                m = dve.tensor_scalar(dst_f[:, c, :], dst_f[:, c, :], span[:, 6, c:c + 1], None, ALU.subtract)
                m.then_inc(dve_own, 1)
                ch.n += 1
            dve.wait_ge(dve_own, ch.n)
            dve.sem_inc(edge_rows_ready, 1)

        def dve_edge_columns(dve):
            n = 0
            for c in range(GC):
                for o in (dcol, icol):
                    dve.wait_ge(edge_cols_up, n + 1)
                    k = min(P, NG - c * P)
                    dve.tensor_copy(o[:, c * P:c * P + k, :],
                                    bank[EDGE_BANKS[n % 2]][:, :].rearrange("p (q g) -> p g q", q=GT)[:, 0:k, :]).then_inc(edge_cols_down, 1)
                    n += 1

        def dve_group_table(dve, ch):
            dve.wait_ge(edge_cols_up, 2 * GC + 1)
            for j in range(2):
                ch.link(dve.tensor_scalar(tab_f[:, j, :], bank[TAB_BANKS[j]][0:1, :], 0.0, float(NB - 1), ALU.max, ALU.min))
            full = NGP - PACK + 1
            for n in range(PACK - 1, 0, -1):
                high = tab_f[:, 0:2, n:n + full] if n == PACK - 1 else words_f[:, :, 0:full]
                ch.link(dve.scalar_tensor_tensor(words_f[:, :, 0:full], high, float(FIELD),
                                                 tab_f[:, 0:2, n - 1:n - 1 + full], ALU.mult, ALU.add))
            ch.link(dve.tensor_copy(group_tab[:, 0:2, 0:full], words_f[:, :, 0:full]))
            ch.link(dve.tensor_scalar(tab_f[:, 0, :], tab_f[:, 1, :], 1.0, None, ALU.min))
            ch.link(dve.tensor_tensor(tab_f[:, 1, :], tab_f[:, 1, :], tab_f[:, 0, :], ALU.subtract))
            ch.link(dve.scalar_tensor_tensor(tab_f[:, 1, :], tab_f[:, 1, :], float(STEP_UNIT), tab_f[:, 0, :], ALU.mult, ALU.add))
            ch.link(dve.memset(tab_f[:, 2, 0:1], 0.0))
            ch.link(dve.tensor_tensor_scan(tab_f[:, 2, 1:NGP], tab_f[:, 1, 0:NGP - 1], tab_f[:, 1, 0:NGP - 1], 0.0,
                                           ALU.add, ALU.max))
            ch.link(dve.tensor_copy(group_tab[:, 2, :], tab_f[:, 2, :]))
            dve.sem_inc(tables_ready, 1)

        def dve_normalise(dve, b, u, i):
            after(dve, xT_up, b - 1)
            after(dve, agg_init, b - 1)
            dve.tensor_scalar(xnb[:, u, :], row_of(agg, b), mv[:, ds(b, 1), 0], rstd[:, 0, ds(b, 1)],
                              ALU.subtract, ALU.mult).then_inc(xn_ready, 1)

        def dve_block(dve, b, u, i):
            dve.wait_ge(xn_ready, b + 1)
            after(dve, base_stored[u], 16 * i)
            dve.tensor_tensor(base_rows[:, u, :], row_of(agg, b), xnb[:, u, :], ALU.add).then_inc(base_part, 1)
            dve.wait_ge(base_part, b + 1)
            dve.tensor_tensor(base_rows[:, u, :], base_rows[:, u, :], ends_b, ALU.add).then_inc(base_ready, 1)
            dve.tensor_tensor(row_of(agg, b), xnb[:, u, :], hbias_b, ALU.add).then_inc(agg_init, 1)
            after(dve, stage_stored[u], 16 * i)
            for j in (1, 3):
                dve.wait_ge(table_up, 4 * b + j + 1)
                dve.tensor_copy(stage[:, u, 512 * j:512 * j + 512], bank[H_BANKS[j]][:, :]).then_inc(table_down_d, 1)
                if j == 1 and not (isinstance(b, int) and b >= NB - 2):
                    dve_normalise(dve, b + 2, u, i + 1)

        def dve_program(dve):
            ch = Chain(dve, dve_own)
            dve_setup(dve, ch)
            dve.sem_inc(rel_ready, 1)
            dve.wait_ge(small_in, 16 * 9)
            dve.wait_ge(consts_set, 11)
            ch.link(dve.tensor_tensor(ends_b, ends_b, beta_b, ALU.add))
            dve_normalise(dve, 0, 0, 0)
            dve_normalise(dve, 1, 1, 0)
            dve_block(dve, 0, 0, 0)
            dve_block(dve, 1, 1, 0)
            dve_edge_rows(dve, ch)
            with dve.Fori(1, NB // 2 - 1) as i:
                dve_block(dve, 2 * i, 0, i)
                dve_block(dve, 2 * i + 1, 1, i)
            dve_block(dve, NB - 3, 0, NB // 2 - 1)
            dve_block(dve, NB - 2, 1, NB // 2 - 1)
            dve_edge_columns(dve)
            dve_block(dve, NB - 1, 0, NB // 2)
            dve_group_table(dve, ch)
            dve.wait_ge(agg_init, NB)
            dve_mix(dve)
            dve_tail(dve, ch)

        GB = 7
        NC = NB // GB
        assert NB % GB == 0
        temps = ring[:, :, :, :].rearrange("p s t d -> p (s t d)")
        W8 = NB * NEX
        logit, prob, pick1, pick2, cand, rank, index, tmp8 = (
            temps[:, W8 * i:W8 * (i + 1)].rearrange("p (b e) -> p b e", e=NEX) for i in range(8))
        tmp1 = temps[:, W8 * 8:W8 * 8 + 8 * NB].rearrange("p (i b) -> p i b", i=8)
        small = temps[:, W8 * 9:W8 * 9 + 8 * NEX].rearrange("p (i e) -> p i e", i=8)
        small_i = small[:, 7, :].bitcast(I32)
        keep = dcol[:, :, :].rearrange("p g t -> p (g t)")
        gates = keep[:, 0:2 * NB].rearrange("p (b k) -> p b k", k=2)
        slot_f = keep[:, 2 * NB:4 * NB].rearrange("p (b k) -> p b k", k=2)
        slots = keep[:, 4 * NB:6 * NB].bitcast(I32).rearrange("p (b k) -> p b k", k=2)
        first_norm = keep[:, 6 * NB:8 * NB].rearrange("p (k b) -> p k b", k=2)
        high_f, slot_low_f = (keep[:, (8 + 2 * n) * NB:(10 + 2 * n) * NB].rearrange("p (b k) -> p b k", k=2) for n in range(2))
        token_f = keep[:, 12 * NB:13 * NB]
        high_i = keep[:, 13 * NB:15 * NB].bitcast(I32).rearrange("p (b k) -> p b k", k=2)
        slot_token = keep[:, 15 * NB:15 * NB + NH].bitcast(I32)
        low_hot, high_token = onehot_x[1], onehot_x[2][:, :, 0:NH]
        starts = group_tab[0:1, 0, 0:NEX + 1]
        xtb = xnb
        xtT = xTb
        token_buf = onehot[:, :, :, :].rearrange("p u t n -> p (u t n)")[:, 0:4 * D].rearrange("p (u d) -> p u d", u=4)
        pair_now = idx_now[:, :, :, 0:2]
        xg = xnb
        xgT = xTb[:, :, :, :].rearrange("p u k n -> p (u k n)").rearrange("p (k n) -> p k n", k=KD)
        hT = temps[:, 0:KH * MT].rearrange("p (k n) -> p k n", k=KH)
        yb = temps[:, KH * MT:KH * MT + MH * D].rearrange("p (m d) -> p m d", m=MH)
        got = onehot[:, :, :, :].rearrange("p u t n -> p (u t n)").rearrange("p (u k d) -> p u k d", k=2, d=D)
        res = temps[:, 0:4 * D].rearrange("p (u d) -> p u d", u=4)

        LOGIT_BANK, XT_BANKS = 5, (3, 4)
        assert NB * NEX <= 512

        gelu_ready = sem("gelu_ready")
        tail_own = sem("tail_own")
        gnn_numbers = sem("gnn_numbers")
        gnn_normed = sem("gnn_normed")
        gamma_in = sem("gamma_in")
        x2_numbers = sem("x2_numbers")
        xt_ready = sem("xt_ready")
        xt_counted = sem("xt_counted")
        xtT_up = sem("xtT_up")
        xtT_ready = sem("xtT_ready")
        logit_up = sem("logit_up")
        shifted_ready = sem("shifted_ready")
        exp_ready = sem("exp_ready")
        picks_ready = sem("picks_ready")
        ranks_up = sem("ranks_up")
        slots_ready = sem("slots_ready")
        token_block_ready = sem("token_block_ready")
        pair_idx = sem("pair_idx")
        both_norms = sem("both_norms")
        tokens_stored = [sem(f"tokens_stored{i}") for i in range(4)]
        token_numbers = sem("token_numbers")
        low_ready = sem("low_ready")
        high_ready = sem("high_ready")
        slots_summed = sem("slots_summed")
        slot_tokens_ready = sem("slot_tokens_ready")
        tile_idx = sem("tile_idx")
        experts_in = [sem(f"experts_in{i}") for i in range(2)]
        expert_used = sem("expert_used")
        tile_rows_in = sem("tile_rows_in")
        tileT_up = sem("tileT_up")
        tileT_ready = sem("tileT_ready")
        hidden_up = sem("hidden_up")
        hidden_ready = sem("hidden_ready")
        answer_up = sem("answer_up")
        answer_ready = sem("answer_ready")
        answer_stored = sem("answer_stored")
        got_in = [sem(f"got_in{i}") for i in range(4)]
        res_part = sem("res_part")
        answers_there = sem("answers_there")
        res_ready = sem("res_ready")
        res_stored = [sem(f"res_stored{i}") for i in range(4)]

        def act_tail(act):
            act.wait_ge(sum_down, NG)
            with act.Fori(0, NC) as c:
                v = agg[:, ds(c * GB, GB), :]
                act.activation(v, v, ACT.Gelu).then_inc(gelu_ready, 1)
            act.wait_ge(gnn_numbers, 1)
            with act.Fori(0, NB) as b:
                act.activation(row_of(agg, b), row_of(agg, b), ACT.Identity, scale=rstd[:, 0, ds(b, 1)],
                               bias=rstd[:, 2, ds(b, 1)]).then_inc(gnn_normed, 1)
            act.wait_ge(x2_numbers, 1)

            def block_of(b, u, i):
                after(act, xt_counted, b - 1)
                after(act, xtT_up, b - 1)
                act.activation(xtb[:, u, :], row_of(agg, b), ACT.Identity, scale=rstd[:, 0, ds(b, 1)],
                               bias=rstd[:, 2, ds(b, 1)]).then_inc(xt_ready, 1)
            pairs(act, block_of)
            act.wait_ge(shifted_ready, 1)
            act.activation(prob, logit, ACT.Exp).then_inc(exp_ready, 1)
            act.wait_ge(both_norms, 1)

            def token_block(b, u, i):
                after(act, tokens_stored[u], 16 * i)
                act.activation(token_buf[:, u, :], row_of(agg, b), ACT.Identity, scale=rstd[:, 0, ds(b, 1)],
                               bias=rstd[:, 2, ds(b, 1)]).then_inc(token_block_ready, 1)
            fours(act, token_block)
            act.wait_ge(slots_ready, 1)
            act.wait_ge(res_part, 1)
            def expert(e, u, i):
                act.wait_ge(experts_in[u], 96 * (i + 1))
                act.sem_inc(waits_passed, 1)
                lo = act.value_load(starts[:, ds(e, 1)], min_val=0, max_val=NT - 1)
                hi = act.value_load(starts[:, ds(e + 1, 1)], min_val=1, max_val=NT)
                with act.Fori(lo, hi) as j:
                    act.wait_ge(tileT_up, j + 1)
                    for k in range(KD):
                        m = act.activation(xgT[:, k, :], bank[T_BANK][:, k * MT:(k + 1) * MT], ACT.Identity,
                                           scale=eparm[u][:, KH + k:KH + k + 1],
                                           bias=eparm[u][:, KH + KD + k:KH + KD + k + 1])
                    m.then_inc(tileT_ready, 1)
                    for c in range(KH):
                        act.wait_ge(hidden_up, KH * j + c + 1)
                        act.activation(hT[:, c, :], bank[H_BANKS[c % 4]][:, 0:MT], ACT.Gelu,
                                       bias=eparm[u][:, c:c + 1]).then_inc(hidden_ready, 1)
            with act.Fori(0, NEX // 2) as i:
                expert(2 * i, 0, i)
                expert(2 * i + 1, 1, i)

        def pe_tail(pe):
            pe.wait_ge(x2_numbers, 1)

            def logits_of(b, u):
                pe.wait_ge(xtT_ready, b + 1)
                for k in range(KD):
                    m = pe.matmul(bank[LOGIT_BANK][:, ds(b * NEX, NEX)], xtT[:, u, k, :], wr_sb[:, k, :],
                                  start=k == 0, stop=k == KD - 1)
                m.then_inc(logit_up, 1)

            def block_of(b, u, i):
                pe.wait_ge(xt_ready, b + 1)
                after(pe, xtT_ready, b - 1)
                for k in range(KD):
                    m = pe.transpose(bank[XT_BANKS[u]][:, k * P:(k + 1) * P], xtb[:, u, k * P:(k + 1) * P], ident[:, :])
                m.then_inc(xtT_up, 1)
                if not is_number(b, 0):
                    logits_of(b - 1, 1 - u)
            pairs(pe, block_of)
            logits_of(NB - 1, 0)
            pe.wait_ge(picks_ready, 1)
            cf = cand.rearrange("p b e -> p (b e)")
            pe.matmul(bank[A_BANKS[0]][:, 0:W8], upper[:, :], cf, start=True, stop=True)
            pe.matmul(bank[A_BANKS[1]][:, 0:W8], ones[:, :], cf, start=True, stop=True).then_inc(ranks_up, 1)
            by_slot = bank[LOGIT_BANK][:, 0:NH]
            pe.matmul(by_slot, zeros[:, 0:P], zeros[:, 0:NH], start=True, stop=False, skip_group_check=True)

            def block_slots(b, u, i):
                pe.wait_ge(low_ready, b + 1)
                pe.wait_ge(high_ready, b + 1)
                for k in range(2):
                    m = pe.matmul(by_slot, low_hot[:, 2 * u + k, :], high_token[:, 2 * u + k, :], start=False, stop=False,
                                  skip_group_check=True)
                m.then_inc(slots_summed, 1)
            pairs(pe, block_slots)
            pe.matmul(by_slot, zeros[:, 0:P], zeros[:, 0:NH], start=False, stop=True,
                      skip_group_check=True).then_inc(slots_summed, 1)

            def tile_columns(j):
                pe.wait_ge(tile_rows_in, 32 * (j + 1))
                for h in range(MH):
                    for k in range(KD):
                        m = pe.transpose(bank[T_BANK][:, k * MT + h * P:k * MT + (h + 1) * P],
                                         xg[:, h, k * P:(k + 1) * P], ident[:, :])
                m.then_inc(tileT_up, 1)
            tile_columns(0)

            def expert(e, u, i):
                pe.wait_ge(experts_in[u], 96 * (i + 1))
                pe.sem_inc(waits_passed, 1)
                lo = pe.value_load(starts[:, ds(e, 1)], min_val=0, max_val=NT - 1)
                hi = pe.value_load(starts[:, ds(e + 1, 1)], min_val=1, max_val=NT)
                with pe.Fori(lo, hi) as j:
                    pe.wait_ge(tileT_ready, j + 1)

                    def first_layer(c):
                        pe.wait_ge(hidden_ready, KH * j + c + 1)
                        for k in range(KD):
                            m = pe.matmul(bank[H_BANKS[c % 4]][:, 0:MT], we1[u][:, k, c * P:(c + 1) * P], xgT[:, k, :],
                                          start=k == 0, stop=k == KD - 1)
                        m.then_inc(hidden_up, 1)

                    def second_layer(c):
                        pe.wait_ge(hidden_ready, KH * j + c + 5)
                        if c == 0:
                            pe.wait_ge(answer_ready, j + 1)
                        for h in range(MH):
                            m = pe.matmul(bank[A_BANKS[h]][:, 0:D], hT[:, c, h * P:(h + 1) * P], we2[u][:, c, :],
                                          start=c == 0, stop=c == KH - 1)
                        return m
                    AHEAD = 3
                    for c in range(AHEAD):
                        first_layer(c)
                    for c in range(KH):
                        m = second_layer(c)
                        if c + AHEAD < KH:
                            first_layer(c + AHEAD)
                        elif c + AHEAD == KH:
                            tile_columns(j + 1)
                    m.then_inc(answer_up, 1)
            with pe.Fori(0, NEX // 2) as i:
                expert(2 * i, 0, i)
                expert(2 * i + 1, 1, i)

        def load_expert(pool, e, u):
            pool.dma_start(we1[u], W1[ds(e, 1), :, :].rearrange("o (k p) h -> p (o k) h", p=P)).then_inc(experts_in[u], 16)
            pool.dma_start(we2[u], W2[ds(e, 1), :, :].rearrange("o (k p) d -> p (o k) d", p=P)).then_inc(experts_in[u], 16)
            pool.dma_start(eparm[u][:, 0:KH], b1[ds(e, 1), :].rearrange("o (k p) -> p (o k)", p=P),
                           allow_slow_non_contiguous=True).then_inc(experts_in[u], 16)
            pool.dma_start(eparm[u][:, KH:KH + KD], ln_g[ds(e, 1), :].rearrange("o (k p) -> p (o k)", p=P),
                           allow_slow_non_contiguous=True).then_inc(experts_in[u], 16)
            pool.dma_start(eparm[u][:, KH + KD:EP], ln_b[ds(e, 1), :].rearrange("o (k p) -> p (o k)", p=P),
                           allow_slow_non_contiguous=True).then_inc(experts_in[u], 16)
            pool.dma_start(eb2[u], b2[ds(e, 1), :].rearrange("o d -> (o d)").partition_broadcast(P)).then_inc(experts_in[u], 16)

        def sp_tail(sp):
            sp.dma_start(answers[NT_LEAST * MT:NT * MT, :].rearrange("(u p) d -> p u d", p=P),
                         zeros[:, :].unsqueeze(1).to_broadcast([P, (NT - NT_LEAST) * MH, D])).then_inc(answer_stored, 16)
            sp.wait_ge(answer_stored, 16)
            def store_tokens(b, u, i):
                n = rows_in_block(b)
                sp.wait_ge(token_block_ready, b + 1)
                sp.dma_start(token_rows[ds(b * P, n), :], token_buf[0:n, u, :]).then_inc(tokens_stored[u], 16)
            fours(sp, store_tokens)
            sp.wait_ge(slots_ready, 1)
            total = sp.value_load(starts[:, NEX:NEX + 1], min_val=NEX, max_val=NT - 1)

            def store(j):
                sp.dma_start(answers[ds(j * MT, MT), :].rearrange("(m p) d -> p m d", p=P), yb).then_inc(answer_stored, 16)
            with sp.Fori(0, total) as j:
                sp.wait_ge(answer_ready, j + 2)
                store(j)
            sp.wait_ge(answer_stored, total * 16 + 16)
            sp.sem_inc(answers_there, 1)

            def block_of(b, u, i):
                n = rows_in_block(b)
                sp.wait_ge(res_ready, b + 1)
                sp.dma_start(out[ds(b * P, n), :], res[0:n, u, :]).then_inc(res_stored[u], 16)
            fours(sp, block_of)
            for u in range(4):
                sp.wait_ge(res_stored[u], 16 * ((NB + 3 - u) // 4))

        def pool_tail(pool):
            pool.wait_ge(sum_down, NG)
            pool.wait_ge(mix_ready, NB)
            load_expert(pool, 0, 0)
            load_expert(pool, 1, 1)
            with pool.Fori(0, NC) as c:
                v = agg[:, ds(c * GB, GB), :]
                pool.wait_ge(gnn_normed, GB * (c + 1))
                pool.tensor_tensor(v, v, gamma_b.unsqueeze(1).to_broadcast([P, GB, D]), ALU.mult).then_inc(gamma_in, 1)
            pool.iota(token_f, [[P, NB]], base=0, channel_multiplier=1,
                      allow_small_or_imprecise_dtypes=True).then_inc(token_numbers, 1)
            def with_pairs(body):
                def four(b, t, half, n):
                    pool.tensor_copy(pair_now[:, half, 0:n, :], slots[:, ds(b, n), :]).then_inc(pair_idx, 1)
                    pool.wait_ge(pair_idx, t + 1)
                    pool.sem_inc(waits_passed, 1)
                    for u in range(n):
                        body(b + u, u, pair_now[:, half, u, :])
                assert NB % 8 == 1
                for half in range(2):
                    four(4 * half, half, half, 4)
                with pool.Fori(1, NB // 8) as i:
                    for half in range(2):
                        four(8 * i + 4 * half, 2 * i + half, half, 4)
                four(NB - 1, NB // 4, 0, 1)

            for u in range(4):
                pool.wait_ge(tokens_stored[u], 16 * ((NB + 3 - u) // 4))
            pool.wait_ge(slot_tokens_ready, 1)

            def gather_tile(j):
                if not is_number(j, 0):
                    pool.wait_ge(tileT_up, j)
                    pool.sem_inc(waits_passed, 1)
                pool.tensor_copy(pair_now[:, 0, 0, :], slot_token[:, ds(j * MH, MH)]).then_inc(tile_idx, 1)
                pool.wait_ge(tile_idx, j + 1)
                pool.sem_inc(waits_passed, 1)
                for h in range(MH):
                    pool.indirect_dma_start(out=xg[:, h, :], out_offset=None, in_=token_rows,
                                            in_offset=bass.IndirectOffsetOnAxis(ap=pair_now[:, 0, 0, h:h + 1], axis=0)).then_inc(tile_rows_in, 16)
            gather_tile(0)

            def expert(e, u):
                if not is_number(e, 0) and not is_number(e, NEX - 1):
                    pool.wait_ge(expert_used, e)
                    pool.sem_inc(waits_passed, 1)
                    load_expert(pool, e + 1, 1 - u)
                lo = pool.value_load(starts[:, ds(e, 1)], min_val=0, max_val=NT - 1)
                hi = pool.value_load(starts[:, ds(e + 1, 1)], min_val=1, max_val=NT - 1)
                with pool.Fori(lo, hi) as j:
                    gather_tile(j + 1)
            expert(0, 0)
            expert(1, 1)
            with pool.Fori(1, NEX // 2 - 1) as i:
                for u in range(2):
                    expert(2 * i + u, u)
            expert(NEX - 2, 0)
            expert(NEX - 1, 1)
            pool.wait_ge(answers_there, 1)

            def gather(b, u, pair):
                n = rows_in_block(b)
                if not isinstance(b, int) or b >= 4:
                    pool.wait_ge(res_ready, b - 3)
                    pool.sem_inc(waits_passed, 1)
                for k in range(2):
                    pool.indirect_dma_start(out=got[0:n, u, k, :], out_offset=None, in_=answers,
                                            in_offset=bass.IndirectOffsetOnAxis(ap=pair[0:n, k:k + 1], axis=0)).then_inc(got_in[u], 16)
            with_pairs(gather)

        def dve_tail(dve, ch0):
            ch = Chain(dve, tail_own)
            with dve.Fori(0, NC) as c:
                dve.wait_ge(gelu_ready, c + 1)
                for i in range(GB):
                    dve.bn_stats(stats[:, ds(c * GB + i, 1), :].rearrange("p o s -> p (o s)"), row_of(agg, c * GB + i)).then_inc(tail_own, 1)
            ch.at(NB)
            dve.wait_ge(tail_own, NB)

            def aggregate():
                mean_and_variance(dve, ch)

            def numbers():
                rsqrt_steps(dve, ch, mv[:, :, 1], LN_EPS, rstd[:, 1, :], rstd[:, 0, :], rstd[:, 2, :])
                ch.link(dve.scalar_tensor_tensor(rstd[:, 2, :], mv[:, :, 0], -1.0, rstd[:, 0, :], ALU.mult, ALU.mult))
            aggregate()
            numbers()
            dve.sem_inc(gnn_numbers, 1)
            base = ch.n
            with dve.Fori(0, NC) as c:
                ch.at(base + c * (1 + GB))
                v = agg[:, ds(c * GB, GB), :]
                dve.wait_ge(gamma_in, c + 1)
                ch.link(dve.tensor_tensor(v, v, xt_all[:, ds(c * GB, GB), :], ALU.add))
                for i in range(GB):
                    dve.bn_stats(stats[:, ds(c * GB + i, 1), :].rearrange("p o s -> p (o s)"), row_of(agg, c * GB + i)).then_inc(tail_own, 1)
            ch.at(base + NC * (1 + GB))
            dve.wait_ge(tail_own, ch.n)
            aggregate()
            numbers()
            dve.sem_inc(x2_numbers, 1)

            def block_of(b, u, i):
                dve.wait_ge(xt_ready, b + 1)
                dve.bn_stats(stats[:, ds(b, 1), :].rearrange("p o s -> p (o s)"), xtb[:, u, :]).then_inc(xt_counted, 1)
                dve.wait_ge(xtT_up, b + 1)
                after(dve, logit_up, b - 1)
                dve.tensor_copy(xtT[:, u, :, :].rearrange("p k n -> p (k n)"), bank[XT_BANKS[u]][:, 0:D]).then_inc(xtT_ready, 1)
            ch.link(dve.tensor_copy(first_norm, rstd[:, 0:3:2, :]))
            pairs(dve, block_of)
            dve.wait_ge(xt_counted, NB)
            aggregate()
            numbers()
            ch.link(dve.tensor_tensor(first_norm[:, 1, :], first_norm[:, 1, :], rstd[:, 0, :], ALU.mult))
            ch.link(dve.tensor_tensor(rstd[:, 2, :], rstd[:, 2, :], first_norm[:, 1, :], ALU.add))
            ch.link(dve.tensor_tensor(rstd[:, 0, :], rstd[:, 0, :], first_norm[:, 0, :], ALU.mult))
            dve.sem_inc(both_norms, 1)
            dve.wait_ge(logit_up, NB)
            ch.link(dve.tensor_tensor(logit, bank[LOGIT_BANK][:, 0:W8].rearrange("p (b e) -> p b e", e=NEX),
                                      br_b.unsqueeze(1).to_broadcast([P, NB, NEX]), ALU.add))

            def e8(t):
                return t.unsqueeze(2).to_broadcast([P, NB, NEX])
            mx, sm, m1v, m2v, f1, f2, s12 = (tmp1[:, i, :] for i in range(7))
            ch.link(dve.tensor_reduce(mx, logit, AX.X, ALU.max))
            ch.link(dve.tensor_tensor(logit, logit, e8(mx), ALU.subtract))
            dve.sem_inc(shifted_ready, 1)
            dve.wait_ge(exp_ready, 1)
            ch.link(dve.tensor_reduce(sm, prob, AX.X, ALU.add))
            ch.link(dve.reciprocal(sm, sm))
            ch.link(dve.tensor_tensor(prob, prob, e8(sm), ALU.mult))

            def best(of, value, first, pick):
                ch.link(dve.tensor_reduce(value, of, AX.X, ALU.max))
                ch.link(dve.tensor_tensor(pick, of, e8(value), ALU.is_equal))
                ch.link(dve.tensor_scalar(pick, pick, -float(NEX), float(NEX), ALU.mult, ALU.add))
                ch.link(dve.tensor_tensor(cand, pick, iota_f[:, 0:NEX].unsqueeze(1).to_broadcast([P, NB, NEX]), ALU.add))
                ch.link(dve.tensor_reduce(first, cand, AX.X, ALU.min))
                ch.link(dve.tensor_tensor(pick, cand, e8(first), ALU.is_equal))
            best(prob, m1v, f1, pick1)
            ch.link(dve.tensor_scalar(tmp8, pick1, -2.0, None, ALU.mult))
            ch.link(dve.tensor_tensor(prob, prob, tmp8, ALU.add))
            best(prob, m2v, f2, pick2)
            ch.link(dve.tensor_tensor(s12, m1v, m2v, ALU.add))
            ch.link(dve.reciprocal(s12, s12))
            ch.link(dve.tensor_tensor(gates[:, :, 0], m1v, s12, ALU.mult))
            ch.link(dve.tensor_tensor(gates[:, :, 1], m2v, s12, ALU.mult))
            ch.link(dve.tensor_tensor(cand, pick1, pick2, ALU.add))
            ch.link(dve.tensor_tensor(cand, cand, e8(valid[:, :]), ALU.mult))
            dve.sem_inc(picks_ready, 1)
            dve.wait_ge(ranks_up, 1)
            flat8 = "p b e -> p (b e)"
            ch.link(dve.tensor_copy(rank.rearrange(flat8), bank[A_BANKS[0]][:, 0:W8]))
            ch.link(dve.tensor_copy(tmp8.rearrange(flat8), bank[A_BANKS[1]][:, 0:W8]))
            for e in range(NEX):
                ch.link(dve.tensor_tensor_scan(index[:, :, e], tmp8[:, :, e], tmp8[:, :, e], 0.0, ALU.add, ALU.max))
            cnt, ntile, upto_e, start_e = (small[:, i, :] for i in range(4))
            ch.link(dve.tensor_scalar(cnt, index[:, NB - 1, :], float(MT - 1), None, ALU.add))
            ch.link(dve.tensor_copy(small_i, cnt))
            ch.link(dve.tensor_scalar(small_i, small_i, MT.bit_length() - 1, None, ALU.arith_shift_right))
            ch.link(dve.tensor_copy(ntile, small_i))
            ch.link(dve.tensor_scalar(ntile, ntile, 1.0, None, ALU.max))
            ch.link(dve.tensor_tensor_scan(upto_e, ntile, ntile, 0.0, ALU.add, ALU.max))
            ch.link(dve.tensor_tensor(start_e, upto_e, ntile, ALU.subtract))
            ch.link(dve.tensor_copy(starts[:, 0:NEX], start_e[0:1, :]))
            ch.link(dve.tensor_copy(starts[:, NEX:NEX + 1], upto_e[0:1, NEX - 1:NEX]))
            ch.link(dve.tensor_scalar(start_e, start_e, float(MT), None, ALU.mult))
            ch.link(dve.tensor_tensor(index, index, tmp8, ALU.subtract))
            ch.link(dve.tensor_tensor(index, index, rank, ALU.add))
            ch.link(dve.tensor_tensor(index, index, start_e.unsqueeze(1).to_broadcast([P, NB, NEX]), ALU.add))
            for k, pick in enumerate((pick1, pick2)):
                ch.link(dve.tensor_tensor(tmp8, index, pick, ALU.mult))
                ch.link(dve.tensor_reduce(slot_f[:, :, k], tmp8, AX.X, ALU.add))
            ch.link(dve.tensor_copy(slots, slot_f))
            ch.link(dve.tensor_scalar(high_i, slots, P.bit_length() - 1, None, ALU.arith_shift_right))
            ch.link(dve.tensor_copy(high_f, high_i))
            ch.link(dve.scalar_tensor_tensor(slot_low_f, high_f, -float(P), slot_f, ALU.mult, ALU.add))
            dve.wait_ge(token_numbers, 1)
            ch.link(dve.tensor_tensor(token_f, token_f, valid[:, :], ALU.mult))
            dve.sem_inc(slots_ready, 1)
            dve.sem_inc(res_part, 1)
            dve.sem_inc(hidden_ready, 4)
            dve.sem_inc(answer_ready, 1)

            def slot_parts(b, u, i):
                after(dve, slots_summed, b - 1)
                dve.tensor_tensor(low_hot[:, 2 * u:2 * u + 2, :],
                                  slot_low_f[:, ds(b, 1), :].rearrange("p o k -> p (o k)").unsqueeze(2).to_broadcast([P, 2, P]),
                                  iota_f[:, :].unsqueeze(1).to_broadcast([P, 2, P]), ALU.is_equal).then_inc(low_ready, 1)
                for k in range(2):
                    m = dve.tensor_scalar(high_token[:, 2 * u + k, :], iota_f[:, 0:NH], high_f[:, ds(b, 1), k],
                                          token_f[:, ds(b, 1)], ALU.is_equal, ALU.mult)
                m.then_inc(high_ready, 1)
            pairs(dve, slot_parts)
            dve.wait_ge(slots_summed, NB + 1)
            ch.link(dve.tensor_copy(slot_token, bank[LOGIT_BANK][:, 0:NH]))
            dve.sem_inc(slot_tokens_ready, 1)

            def expert(e, u, i):
                dve.wait_ge(experts_in[u], 96 * (i + 1))
                dve.sem_inc(waits_passed, 1)
                lo = dve.value_load(starts[:, ds(e, 1)], min_val=0, max_val=NT - 1)
                hi = dve.value_load(starts[:, ds(e + 1, 1)], min_val=1, max_val=NT)
                with dve.Fori(lo, hi) as j:
                    dve.wait_ge(answer_up, j + 1)
                    dve.wait_ge(answer_stored, 16 * (j + 1))
                    for h in range(MH):
                        m = dve.tensor_tensor(yb[:, h, :], bank[A_BANKS[h]][:, 0:D], eb2[u], ALU.add)
                    m.then_inc(answer_ready, 1)
                dve.wait_ge(answer_ready, hi + 1)
                dve.sem_inc(expert_used, 1)
            with dve.Fori(0, NEX // 2) as i:
                expert(2 * i, 0, i)
                expert(2 * i + 1, 1, i)

            def combine(b, u, i):
                dve.wait_ge(got_in[u], 32 * (i + 1))
                after(dve, res_stored[u], 16 * i)
                dve.scalar_tensor_tensor(res[:, u, :], got[:, u, 0, :], gates[:, ds(b, 1), 0], row_of(agg, b),
                                         ALU.mult, ALU.add).then_inc(res_part, 1)
                dve.wait_ge(res_part, b + 2)
                dve.scalar_tensor_tensor(res[:, u, :], got[:, u, 1, :], gates[:, ds(b, 1), 1], res[:, u, :],
                                         ALU.mult, ALU.add).then_inc(res_ready, 1)
            fours(dve, combine)


        @block.sync
        def _(sp):
            sp_program(sp)

        @block.gpsimd
        def _(pool):
            pool_program(pool)

        @block.tensor
        def _(pe):
            pe_program(pe)

        @block.scalar
        def _(act):
            act_program(act)

        @block.vector
        def _(dve):
            dve_program(dve)


NAMES = ["x", "src", "dst", "edge_type_8", "L0_gnn_basis", "L0_gnn_comp", "L0_gnn_loop_w", "L0_gnn_h_bias",
         "L0_gnn_ln_gamma", "L0_gnn_ln_beta", "L0_mix_Wq", "L0_mix_Wk", "L0_mix_Wv", "L0_mix_Wm", "L0_mix_W1",
         "L0_mix_W2", "L0_mix_g1", "L0_mix_b1", "L0_mix_g2", "L0_mix_b2", "L0_ffn_Wr", "L0_ffn_br", "L0_ffn_ln_g",
         "L0_ffn_ln_b", "L0_ffn_W1", "L0_ffn_b1", "L0_ffn_W2", "L0_ffn_b2"]


def kernel(**inputs):
    import numpy as np
    import concourse.bacc as bacc
    from concourse.bass_utils import run_bass_kernel_spmd

    nc = bacc.Bacc("TRN2", target_bir_lowering=False, num_devices=1)
    arrays, args = {}, []
    for name in NAMES:
        a = np.ascontiguousarray(inputs[name])
        arrays[f"in_{name}"] = a
        args.append(nc.dram_tensor(f"in_{name}", a.shape, mybir.dt.from_np(a.dtype), kind="ExternalInput").ap())
    out = nc.dram_tensor("out_x", inputs["x"].shape, F32, kind="ExternalOutput").ap()
    bass_gps_layer(nc, *args, out)
    r = run_bass_kernel_spmd(nc, [arrays], core_ids=[0])
    return r.results[0]["out_x"]
```
